# Optimizing a Trainium2 kernel written in Bass

```python
import numpy as np
import jax
import jax.numpy as jnp

def _softmax(x, axis=-1):
    return jax.nn.softmax(x, axis=axis)
def _gelu(x):
    return jax.nn.gelu(x, approximate=True)
def _silu(x):
    return jax.nn.silu(x)
def _sigmoid(x):
    return jax.nn.sigmoid(x)
def _layernorm(x, axis=-1, eps=1e-5):
    m = jnp.mean(x, axis=axis, keepdims=True)
    v = jnp.var(x, axis=axis, keepdims=True)
    return (x - m) / jnp.sqrt(v + eps)
def _scatter_add(tgt, idx, src, axis=0):
    return tgt.at[idx].add(src)
def _segment_sum(src, seg, n):
    return jax.ops.segment_sum(src, seg, n)

kernel_name = 'mk_adj_preln_d2_adj_128_09f548'

def setup_inputs(seed: int = 0):
    np.random.seed(seed)
    _w = jnp.asarray
    def _rec_inputs():
        import jax
        import jax.numpy as jnp
        _gk = jax.random.key(seed)
        x = -0.0005207 + 1.001 * jax.random.normal(jax.random.fold_in(_gk, 1), (8, 2048, 128), jnp.float32)
        _w = (1.0 + jnp.arange(2048, dtype=jnp.float32)) ** -0.5
        _w = _w / _w.mean()
        _pij = jnp.clip(0.015625 * _w[:, None] * _w[None, :], 0.0, 1.0)
        _a = jax.random.uniform(jax.random.fold_in(_gk, 2), (8, 2048, 2048)) < _pij
        _a = jnp.logical_or(_a, jnp.swapaxes(_a, -1, -2))
        _a = jnp.logical_or(_a, jnp.eye(2048, dtype=bool))
        _af = _a.astype(jnp.float32)
        _af = _af * jax.random.uniform(jax.random.fold_in(_gk, 3), (8, 2048, 2048), jnp.float32, 0.05, 1)
        adj = _af
        _nm = jnp.ones((8, 2048), dtype=bool)
        nodemask = jnp.where(_nm, 1.0, 0.0).astype(jnp.int32)
        return x, adj, nodemask
    x, adj, nodemask = _rec_inputs()
    def _L0_gnn_setup():
        import jax, jax.numpy as jnp
        import numpy as np
        B, N, D = (8, 2048, 128)
        key = jax.random.key(seed)
        k1, k2, k3 = jax.random.split(key, 3)
        embeddings = jax.random.normal(k1, (B, N, D), dtype=jnp.float32)
        cost_matrix = jax.random.uniform(k2, (B, N, N), dtype=jnp.float32)
        W = jax.random.normal(k3, (D, 2 * D), dtype=jnp.float32) * (1.0 / np.sqrt(2 * D))
        b = jnp.zeros((D,), dtype=jnp.float32)
        return {'embeddings': embeddings, 'cost_matrix': cost_matrix, 'W': W, 'b': b}
    _L0_gnn_all = _L0_gnn_setup()
    _L0_gnn_in = {k: v for k, v in _L0_gnn_all.items() if k in ('W', 'b', )}
    del _L0_gnn_all

    def _L1_gnn_setup():
        import jax, jax.numpy as jnp
        import numpy as np
        T_DIL = 10
        K_DIL = 2
        BN_EPS = 1e-05
        NORM_EPS = 1e-12

        def _dilate_pattern(adj_bool, mask_b):
            N = adj_bool.shape[0]

            def step(carry, n):
                row = jnp.take(carry, n, axis=0)
                nbi = row.astype(jnp.int32)
                num = jnp.sum(nbi)
                sf = jnp.where(num > T_DIL, (num + K_DIL - 1) // K_DIL, 1)
                rank = jnp.cumsum(nbi)
                rm = row & (rank % sf == 0)
                valid = (mask_b[n] != 0) & (num > 1)
                rm = jnp.where(valid, rm, False)
                keep = ~rm
                carry = carry.at[n].set(row & keep)
                carry = carry.at[:, n].set(carry[:, n] & keep)
                return (carry, None)
            out, _ = jax.lax.scan(step, adj_bool, jnp.arange(N))
            return out

        def _dilate(adj, mask):
            keep = jax.vmap(_dilate_pattern)(adj > 0, mask)
            return adj * keep.astype(adj.dtype)

        def _sage(x, adj, Wr, Wx, b, mf):
            deg = jnp.clip(jnp.sum(adj, axis=-1, keepdims=True), 1.0, None)
            agg = jnp.einsum('bij,bjd->bid', adj, x) / deg
            out = agg @ Wr + x @ Wx + b
            nrm = jnp.maximum(jnp.linalg.norm(out, axis=-1, keepdims=True), NORM_EPS)
            return out / nrm * mf[..., None]

        def _bn(x, g, b):
            m = jnp.mean(x, axis=(0, 1))
            v = jnp.var(x, axis=(0, 1))
            return (x - m) * jax.lax.rsqrt(v + BN_EPS) * g + b

        def _forward(x, adj, mask, Wr1, Wx1, b1, g1, be1, Wr2, Wx2, b2, g2, be2, Wr3, Wx3, b3, g3, be3, Wl, bl):
            mf = mask.astype(x.dtype)
            adj_d = _dilate(adj, mask)
            h1 = _bn(jax.nn.relu(_sage(x, adj_d, Wr1, Wx1, b1, mf)), g1, be1)
            h2 = _bn(jax.nn.relu(_sage(h1, adj_d, Wr2, Wx2, b2, mf)), g2, be2)
            h3 = _bn(jax.nn.relu(_sage(h2, adj_d, Wr3, Wx3, b3, mf)), g3, be3)
            xc = jnp.concatenate([h1, h2, h3], axis=-1) * mf[..., None]
            return (xc @ Wl + bl) * mf[..., None]
        B, N, D, H, E = (8, 2048, 128, 128, 128)
        key = jax.random.key(seed)
        ks = jax.random.split(key, 24)
        x = jax.random.normal(ks[0], (B, N, D), dtype=jnp.float32)
        a = jax.random.bernoulli(ks[1], 0.01, (B, N, N))
        a = a | jnp.swapaxes(a, 1, 2)
        a = a & ~jnp.eye(N, dtype=bool)[None]
        adj = a.astype(jnp.float32)
        mask = jnp.ones((B, N), dtype=jnp.int32)
        s = 0.05
        p = {}
        dims = [(D, H), (H, H), (H, E)]
        for i, (di, do) in enumerate(dims, 1):
            p[f'Wr{i}'] = s * jax.random.normal(ks[2 * i], (di, do), dtype=jnp.float32)
            p[f'Wx{i}'] = s * jax.random.normal(ks[2 * i + 1], (di, do), dtype=jnp.float32)
            p[f'b{i}'] = jnp.zeros((do,), dtype=jnp.float32)
            p[f'g{i}'] = jnp.ones((do,), dtype=jnp.float32)
            p[f'be{i}'] = jnp.zeros((do,), dtype=jnp.float32)
        p['Wl'] = s * jax.random.normal(ks[10], (2 * H + E, E), dtype=jnp.float32)
        p['bl'] = jnp.zeros((E,), dtype=jnp.float32)
        return {'x': x, 'adj': adj, 'mask': mask, **p}
    _L1_gnn_all = _L1_gnn_setup()
    _L1_gnn_in = {k: v for k, v in _L1_gnn_all.items() if k in ('Wr1', 'Wx1', 'b1', 'g1', 'be1', 'Wr2', 'Wx2', 'b2', 'g2', 'be2', 'Wr3', 'Wx3', 'b3', 'g3', 'be3', 'Wl', 'bl', )}
    del _L1_gnn_all

    return {
        "x": x,
        "adj": adj,
        "nodemask": nodemask,
        "L0_gnn_W": _L0_gnn_in["W"],
        "L0_gnn_b": _L0_gnn_in["b"],
        "L1_gnn_Wr1": _L1_gnn_in["Wr1"],
        "L1_gnn_Wx1": _L1_gnn_in["Wx1"],
        "L1_gnn_b1": _L1_gnn_in["b1"],
        "L1_gnn_g1": _L1_gnn_in["g1"],
        "L1_gnn_be1": _L1_gnn_in["be1"],
        "L1_gnn_Wr2": _L1_gnn_in["Wr2"],
        "L1_gnn_Wx2": _L1_gnn_in["Wx2"],
        "L1_gnn_b2": _L1_gnn_in["b2"],
        "L1_gnn_g2": _L1_gnn_in["g2"],
        "L1_gnn_be2": _L1_gnn_in["be2"],
        "L1_gnn_Wr3": _L1_gnn_in["Wr3"],
        "L1_gnn_Wx3": _L1_gnn_in["Wx3"],
        "L1_gnn_b3": _L1_gnn_in["b3"],
        "L1_gnn_g3": _L1_gnn_in["g3"],
        "L1_gnn_be3": _L1_gnn_in["be3"],
        "L1_gnn_Wl": _L1_gnn_in["Wl"],
        "L1_gnn_bl": _L1_gnn_in["bl"],
    }

def reference(x, adj, nodemask, L0_gnn_W, L0_gnn_b, L1_gnn_Wr1, L1_gnn_Wx1, L1_gnn_b1, L1_gnn_g1, L1_gnn_be1, L1_gnn_Wr2, L1_gnn_Wx2, L1_gnn_b2, L1_gnn_g2, L1_gnn_be2, L1_gnn_Wr3, L1_gnn_Wx3, L1_gnn_b3, L1_gnn_g3, L1_gnn_be3, L1_gnn_Wl, L1_gnn_bl):
    import jax
    import jax.numpy as jnp
    def _L0_gnn_ref(embeddings, cost_matrix, W, b):
        import jax, jax.numpy as jnp
        import numpy as np
        B, N, D = (8, 2048, 128)
        degree = (cost_matrix != 0).astype(embeddings.dtype).sum(axis=-1)
        sum_neighbors = jnp.einsum('bij,bid->bjd', cost_matrix, embeddings)
        sum_neighbors = sum_neighbors / degree[..., None]
        concatenated = jnp.concatenate([embeddings, sum_neighbors], axis=-1)
        return jax.nn.relu(jnp.einsum('bnf,df->bnd', concatenated, W) + b)

    def _L1_gnn_ref(x, adj, mask, Wr1, Wx1, b1, g1, be1, Wr2, Wx2, b2, g2, be2, Wr3, Wx3, b3, g3, be3, Wl, bl):
        import jax, jax.numpy as jnp
        import numpy as np
        T_DIL = 10
        K_DIL = 2
        BN_EPS = 1e-05
        NORM_EPS = 1e-12

        def _dilate_pattern(adj_bool, mask_b):
            N = adj_bool.shape[0]

            def step(carry, n):
                row = jnp.take(carry, n, axis=0)
                nbi = row.astype(jnp.int32)
                num = jnp.sum(nbi)
                sf = jnp.where(num > T_DIL, (num + K_DIL - 1) // K_DIL, 1)
                rank = jnp.cumsum(nbi)
                rm = row & (rank % sf == 0)
                valid = (mask_b[n] != 0) & (num > 1)
                rm = jnp.where(valid, rm, False)
                keep = ~rm
                carry = carry.at[n].set(row & keep)
                carry = carry.at[:, n].set(carry[:, n] & keep)
                return (carry, None)
            out, _ = jax.lax.scan(step, adj_bool, jnp.arange(N))
            return out

        def _dilate(adj, mask):
            keep = jax.vmap(_dilate_pattern)(adj > 0, mask)
            return adj * keep.astype(adj.dtype)

        def _sage(x, adj, Wr, Wx, b, mf):
            deg = jnp.clip(jnp.sum(adj, axis=-1, keepdims=True), 1.0, None)
            agg = jnp.einsum('bij,bjd->bid', adj, x) / deg
            out = agg @ Wr + x @ Wx + b
            nrm = jnp.maximum(jnp.linalg.norm(out, axis=-1, keepdims=True), NORM_EPS)
            return out / nrm * mf[..., None]

        def _bn(x, g, b):
            m = jnp.mean(x, axis=(0, 1))
            v = jnp.var(x, axis=(0, 1))
            return (x - m) * jax.lax.rsqrt(v + BN_EPS) * g + b

        def _forward(x, adj, mask, Wr1, Wx1, b1, g1, be1, Wr2, Wx2, b2, g2, be2, Wr3, Wx3, b3, g3, be3, Wl, bl):
            mf = mask.astype(x.dtype)
            adj_d = _dilate(adj, mask)
            h1 = _bn(jax.nn.relu(_sage(x, adj_d, Wr1, Wx1, b1, mf)), g1, be1)
            h2 = _bn(jax.nn.relu(_sage(h1, adj_d, Wr2, Wx2, b2, mf)), g2, be2)
            h3 = _bn(jax.nn.relu(_sage(h2, adj_d, Wr3, Wx3, b3, mf)), g3, be3)
            xc = jnp.concatenate([h1, h2, h3], axis=-1) * mf[..., None]
            return (xc @ Wl + bl) * mf[..., None]
        return _forward(x, adj, mask, Wr1, Wx1, b1, g1, be1, Wr2, Wx2, b2, g2, be2, Wr3, Wx3, b3, g3, be3, Wl, bl)

    h = jnp.maximum(_layernorm(x, axis=-1), 0.0)
    x = x + _L0_gnn_ref(h, adj, L0_gnn_W, L0_gnn_b)
    h = jnp.maximum(_layernorm(x, axis=-1), 0.0)
    x = x + _L1_gnn_ref(h, adj, nodemask, L1_gnn_Wr1, L1_gnn_Wx1, L1_gnn_b1, L1_gnn_g1, L1_gnn_be1, L1_gnn_Wr2, L1_gnn_Wx2, L1_gnn_b2, L1_gnn_g2, L1_gnn_be2, L1_gnn_Wr3, L1_gnn_Wx3, L1_gnn_b3, L1_gnn_g3, L1_gnn_be3, L1_gnn_Wl, L1_gnn_bl)
    return x


_drawn_inputs = setup_inputs


def setup_inputs(seed=0):
    import zlib

    import numpy as np

    out = dict(_drawn_inputs(seed))
    spreads = {'L0_gnn_b': (0.0, 0.1),
     'L1_gnn_b1': (0.0, 0.1),
     'L1_gnn_g1': (1.0, 0.2),
     'L1_gnn_be1': (0.0, 0.1),
     'L1_gnn_b2': (0.0, 0.1),
     'L1_gnn_g2': (1.0, 0.2),
     'L1_gnn_be2': (0.0, 0.1),
     'L1_gnn_b3': (0.0, 0.1),
     'L1_gnn_g3': (1.0, 0.2),
     'L1_gnn_be3': (0.0, 0.1),
     'L1_gnn_bl': (0.0, 0.1)}
    factors = {}
    for name, (base, spread) in spreads.items():
        noise = np.random.default_rng([zlib.crc32(name.encode()), seed]).standard_normal(out[name].shape)
        drawn = base * np.exp(spread * noise) if base else spread * noise
        out[name] = jnp.asarray(drawn.astype(out[name].dtype))
    for name, factor in factors.items():
        out[name] = (out[name] * factor).astype(out[name].dtype)
    return out
```

```python
from contextlib import ExitStack

import concourse.bass as bass
from concourse import mybir

ALU = mybir.AluOpType
ACT = mybir.ActivationFunctionType
AX = mybir.AxisListType.X
F32 = mybir.dt.float32
BF16 = mybir.dt.bfloat16
F16 = mybir.dt.float16
I32 = mybir.dt.int32
U16 = mybir.dt.uint16

P = 128
B = 8
N = 2048
NB = N // P
COLS = B * NB
WORD = 16
WB = P // WORD
WORDS = N // WORD
Q = 4
G = NB // Q
ROUNDS = 5
T_DIL = 10.0
BN_EPS = 1e-5
LN_EPS = 1e-5
NORM_EPS = 1e-12
NONE = 4096.0


class Chain:

    def __init__(self, engine, sem, base=0):
        self.engine, self.sem, self.base, self.n = engine, sem, base, 0

    def __call__(self, instruction):
        instruction.then_inc(self.sem, 1)
        self.n += 1
        self.engine.wait_ge(self.sem, self.base + self.n)


HEAD = 8


def fresh(nc, ctx, tag):
    made = []

    def clear():
        with nc.Block() as block:
            @block.gpsimd
            def _(pool):
                for s in made:
                    pool.sem_clear(s)

    def sem(name):
        made.append(ctx.enter_context(nc.semaphore(name + tag)))
        return made[-1]

    ctx.callback(lambda: clear())
    return sem


def spread(ap, n):
    return ap.unsqueeze(2).broadcast_to([ap.shape[0], ap.shape[1], n])


def repeat(ap, n):
    return ap.unsqueeze(1).broadcast_to([ap.shape[0], n, ap.shape[1]])


def constants(nc, ctx, nodemask):
    def sb(name, shape, dt):
        return ctx.enter_context(nc.sbuf_tensor(name, shape, dt))

    c = {
        "ident": sb("ident", [P, P], F32),
        "ident_b": sb("ident_b", [P, P], BF16),
        "ones": sb("ones", [P, P], F32),
        "mask": sb("mask", [P, B, NB], F32),
        "word_index": sb("word_index", [P, WORDS], F32),
        "bits": sb("bits", [P, WORD, WB], U16),
        "ln_eps": sb("ln_eps", [P, 1], F32),
        "bn_eps": sb("bn_eps", [P, 1], F32),
    }
    with ExitStack() as inner:
        sem = fresh(nc, inner, "_c")
        mask_int = inner.enter_context(nc.sbuf_tensor("mask_int", [COLS, P], I32))
        mask_rows = inner.enter_context(nc.sbuf_tensor("mask_rows", [COLS, P], F32))
        mask_ps = inner.enter_context(nc.psum_tensor("mask_ps", [P, 512], F32))
        mask_loaded = sem("mask_loaded")
        rows_ready = sem("rows_ready")
        mask_turned = sem("mask_turned")
        filled = sem("filled")
        mask_copied = sem("mask_copied")
        block = inner.enter_context(nc.Block())

        @block.sync
        def _(sp):
            sp.dma_start(mask_int[:], nodemask.rearrange("b (j p) -> (b j) p", p=P)).then_inc(mask_loaded, 16)

        @block.gpsimd
        def _(pool):
            link = Chain(pool, filled)
            for t in ("ident", "ident_b"):
                link(nc.gpsimd.memset(c[t][:], 0.0))
                link(nc.gpsimd.affine_select(out=c[t][:], in_=c[t][:], compare_op=ALU.not_equal, fill=1.0,
                                             base=0, pattern=[[-1, P]], channel_multiplier=1))
            link(nc.gpsimd.memset(c["ones"][:], 1.0))
            link(nc.gpsimd.memset(c["ln_eps"][:], LN_EPS))
            link(nc.gpsimd.memset(c["bn_eps"][:], BN_EPS))
            for bit in range(WORD):
                link(nc.gpsimd.memset(c["bits"][:, bit, :], 1 << bit))
            link(nc.gpsimd.iota(c["word_index"][:], pattern=[[1, WORDS]], base=0, channel_multiplier=0,
                                allow_small_or_imprecise_dtypes=True))

        @block.vector
        def _(dve):
            dve.wait_ge(mask_loaded, 16)
            nc.vector.tensor_copy(mask_rows[:], mask_int[:]).then_inc(rows_ready, 1)
            dve.wait_ge(mask_turned, 1)
            nc.vector.tensor_copy(c["mask"][:].rearrange("p b j -> p (b j)"),
                                  mask_ps[:, 0:COLS]).then_inc(mask_copied, 1)
            dve.wait_ge(mask_copied, 1)

        @block.tensor
        def _(pe):
            pe.wait_ge(rows_ready, 1)
            pe.wait_ge(filled, 4)
            nc.tensor.transpose(mask_ps[:, 0:COLS], mask_rows[:], c["ident"][:]).then_inc(mask_turned, 1)
    return c


def norm(nc, c, x, h_out):
    with ExitStack() as ctx:
        def sb(name, shape, dt):
            return ctx.enter_context(nc.sbuf_tensor(name + "_norm", shape, dt))

        sem = fresh(nc, ctx, "_norm")

        xt = [sb(f"xt{i}", [P, NB, P], F32) for i in range(2)]
        h = [sb(f"h{i}", [P, NB, P], F32) for i in range(2)]
        square = sb("square", [P, NB, P], F32)
        mean = sb("mean", [P, NB], F32)
        var = sb("var", [P, NB], F32)
        dev = sb("dev", [P, NB], F32)
        rstd = sb("rstd", [P, NB], F32)
        x_loaded = [sem(f"x_loaded{i}") for i in range(2)]
        h_stored = [sem(f"h_stored{i}") for i in range(2)]
        dve_step = sem("dve_step")
        centred = sem("centred")
        squared = sem("squared")
        summed = sem("summed")
        rooted = sem("rooted")
        scaled = sem("scaled")
        h_ready = sem("h_ready")
        block = ctx.enter_context(nc.Block())

        @block.sync
        def _(sp):
            with sp.Fori(0, B // 2) as pair:
                b = pair * 2
                for i in range(2):
                    sp.wait_ge(h_ready, HEAD + b + i - 1)
                    for g in range(G):
                        sp.dma_start(xt[i][:, g * Q:(g + 1) * Q, :],
                                     x.rearrange("b (g q p) d -> b g p q d", p=P, q=Q)[b + i, g]).then_inc(x_loaded[i], 16)

        @block.vector
        def _(dve):
            with dve.Fori(0, B // 2) as pair:
                b = pair * 2
                for i in range(2):
                    link = Chain(dve, dve_step, (b + i) * 3)
                    dve.wait_ge(x_loaded[i], (b * 8 + 16) * G)
                    link(nc.vector.tensor_reduce(mean[:], xt[i][:], AX, ALU.add))
                    link(nc.vector.tensor_scalar(mean[:], mean[:], 1.0 / P, None, ALU.mult))
                    nc.vector.tensor_tensor(xt[i][:], xt[i][:], spread(mean[:], P), ALU.subtract).then_inc(centred, 1)
                    dve.wait_ge(squared, b + i + 1)
                    nc.vector.tensor_reduce(var[:], square[:], AX, ALU.add).then_inc(summed, 1)
                    dve.wait_ge(rooted, b + i + 1)
                    link(nc.vector.reciprocal(rstd[:], dev[:]))
                    nc.vector.tensor_tensor(xt[i][:], xt[i][:], spread(rstd[:], P), ALU.mult).then_inc(scaled, 1)

        @block.scalar
        def _(act):
            act.sem_inc(h_ready, HEAD)
            for i in range(2):
                act.sem_inc(h_stored[i], 1)
            with act.Fori(0, B // 2) as pair:
                b = pair * 2
                for i in range(2):
                    act.wait_ge(centred, b + i + 1)
                    nc.scalar.activation(square[:], xt[i][:], ACT.Square).then_inc(squared, 1)
                    act.wait_ge(summed, b + i + 1)
                    nc.scalar.activation(dev[:], var[:], ACT.Sqrt, scale=1.0 / P, bias=c["ln_eps"][:]).then_inc(rooted, 1)
                    act.wait_ge(scaled, b + i + 1)
                    act.wait_ge(h_stored[i], b * 8 + 1)
                    nc.scalar.activation(h[i][:], xt[i][:], ACT.Relu).then_inc(h_ready, 1)
                    act.wait_ge(h_ready, HEAD + b + i + 1)
                    act.dma_start(h_out[b + i], h[i][:]).then_inc(h_stored[i], 16)
            for i in range(2):
                act.wait_ge(h_stored[i], B // 2 * 16 + 1)


def dilate(nc, c, adj, col_bits, deg, own):
    with ExitStack() as ctx:
        def sb(name, shape, dt):
            return ctx.enter_context(nc.sbuf_tensor(name + "_dil", shape, dt))

        def ps(name, shape, dt):
            return ctx.enter_context(nc.psum_tensor(name + "_dil", shape, dt))

        sem = fresh(nc, ctx, "_dil")

        nat = [sb(f"nat{i}", [P, N], F32) for i in range(2)]
        sign = sb("sign", [P, B, N], BF16)
        waste = [sb(f"waste{i}", [P, N], BF16) for i in range(3)]
        gone = sb("gone", [P, N], U16)
        v = sb("v", [P, B, N], BF16)
        rank = [sb(f"rank{i}", [P, N], F16) for i in range(2)]
        hot = [sb(f"hot{i}", [P, 3, N], BF16) for i in range(2)]
        index = sb("index", [P, N], F16)
        weight = sb("weight", [P, WB], BF16)
        weight3 = sb("weight3", [P, WORD, WB], F32)
        below = sb("below", [P, NB, NB], F32)
        upper2 = sb("upper2", [P, P], BF16)
        upper = sb("upper", [P, P], BF16)
        restart = sb("restart", [P, B, P], BF16)
        chunk = sb("chunk", [P, B, NB], F32)
        chunk_left = sb("chunk_left", [P, B, NB], F32)
        left = sb("left", [P, B], F32)
        outside = sb("outside", [P, B], F32)
        masked = sb("masked", [P, B], F32)
        num = sb("num", [P, B], I32)
        odd = sb("odd", [P, B], I32)
        t0 = sb("t0", [P, B], F32)
        t1 = sb("t1", [P, B], F32)
        half = sb("half", [P, B], F32)
        last = sb("last", [P, B], F32)
        thr = sb("thr", [P, B], F32)
        every = sb("every", [P, B], F32)
        a2 = sb("a2", [P, B, P], BF16)
        vb = sb("vb", [P, B, P], BF16)
        rk = sb("rk", [P, B, P], BF16)
        q1 = sb("q1", [P, B, P], BF16)
        q2 = sb("q2", [P, B, P], BF16)
        rm = [sb(f"rm{i}", [P, B, P], BF16) for i in range(2)]
        swapped = sb("swapped", [P, B, P], BF16)
        turned = sb("turned", [P, B, P], BF16)
        differ = sb("differ", [P, 1], F32)
        flag = sb("flag", [1, 1], I32)
        bias = sb("bias", [P, 2, B], F32)
        signs = sb("signs", [P, 2, B], F32)
        pos = sb("pos", [P, 2, B], F32)
        pos_i = sb("pos_i", [P, 2, B], I32)
        high = sb("high", [P, 2, B], I32)
        low = sb("low", [P, 2, B], I32)
        bit = sb("bit", [P, 2, B], I32)
        one = sb("one", [P, 2, B], I32)

        turn_ps = ps("turn_ps", [P, B, P], BF16)
        pack_ps = [ps(f"pack_ps{i}", [P, 512], F32) for i in range(2)]
        flag_ps = ps("flag_ps", [P, 512], F32)

        nat_full = [sem(f"nat_full{i}") for i in range(2)]
        sign_ready = sem("sign_ready")
        act_step = sem("act_step")
        set_up = sem("set_up")
        weight_ready = sem("weight_ready")
        row_step = sem("row_step")
        joint_step = sem("joint_step")
        rm_ready = sem("rm_ready")
        turned_ready = sem("turned_ready")
        differ_ready = sem("differ_ready")
        flag_ready = sem("flag_ready")
        rank_ready = sem("rank_ready")
        signs_ready = sem("signs_ready")
        find_step = sem("find_step")
        hot_ready = sem("hot_ready")
        pack_ready = sem("pack_ready")
        bits_ready = sem("bits_ready")

        SET_UP = 12
        ROW_STEPS = 3
        JOINT_STEPS = 11 + 11 * ROUNDS
        FIND_STEPS = 3
        block = ctx.enter_context(nc.Block())
        rows = adj.rearrange("b (j p) n -> b j p n", p=P)

        @block.gpsimd
        def _(pool):
            link = Chain(pool, set_up)
            link(nc.gpsimd.iota(index[:], pattern=[[1, N]], base=0, channel_multiplier=0,
                                allow_small_or_imprecise_dtypes=True))
            link(nc.gpsimd.memset(one[:], 1))
            link(nc.gpsimd.memset(turned[:], 0.0))
            link(nc.gpsimd.memset(col_bits[:].rearrange("p b k w -> p (b k w)").bitcast(I32), 0))
            link(nc.gpsimd.memset(below[:], 1.0))
            link(nc.gpsimd.memset(upper[:], 1.0))
            link(nc.gpsimd.memset(restart[:], 1.0))
            link(nc.gpsimd.memset(restart[:, :, 0:1], 0.0))
            link(nc.gpsimd.affine_select(out=below[:], in_=below[:], compare_op=ALU.is_gt, fill=0.0,
                                         base=0, pattern=[[1, NB], [-1, NB]], channel_multiplier=0))
            link(nc.gpsimd.memset(upper2[:], 2.0))
            link(nc.gpsimd.affine_select(out=upper2[:], in_=upper2[:], compare_op=ALU.is_ge, fill=1.0,
                                         base=0, pattern=[[1, P]], channel_multiplier=-1))
            link(nc.gpsimd.affine_select(out=upper[:], in_=upper[:], compare_op=ALU.is_gt, fill=0.0,
                                         base=0, pattern=[[1, P]], channel_multiplier=-1))
            assert link.n == SET_UP

        @block.sync
        def _(sp):
            with sp.Fori(0, NB) as j:
                with sp.Fori(0, B // 2) as pair:
                    b = pair * 2
                    for i in range(2):
                        sp.wait_ge(sign_ready, HEAD + j * B + b + i - 1)
                        sp.dma_start(nat[i][:], rows[b + i, j, :, :]).then_inc(nat_full[i], 16)

        @block.scalar
        def _(act):
            act.sem_inc(sign_ready, HEAD)
            act.sem_inc(bits_ready, HEAD)
            act.sem_inc(act_step, HEAD)
            act.sem_inc(signs_ready, HEAD)

            def signs_of(j, first):
                with act.Fori(0, B // 2) as pair:
                    b = pair * 2
                    for i in range(2):
                        u = j * B + b + i
                        act.wait_ge(nat_full[i], j * (B * 8) + b * 8 + 16)
                        if not first:
                            act.wait_ge(row_step, (u - B) * ROW_STEPS + 2)
                        nc.scalar.activation(sign[:, b + i, :], nat[i][:], ACT.Sign).then_inc(sign_ready, 1)
                        act.wait_ge(sign_ready, HEAD + u + 1)
                        act.wait_ge(act_step, HEAD + u)
                        nc.scalar.activation(waste[2][:], sign[:, b + i, :], ACT.Square,
                                             accum_out=deg[:, b + i, bass.ds(j, 1)]).then_inc(act_step, 1)

            def find_and_store(j):
                with act.Fori(0, B // 2) as pair:
                    b = pair * 2
                    for i in range(2):
                        act.wait_ge(rank_ready, j * B + b + i + 1)
                        for t in range(2):
                            act.wait_ge(signs_ready, HEAD + (j * B + b + i) * 2 + t - 1)
                            nc.scalar.activation(waste[t][:], rank[i][:], ACT.Sign,
                                                 bias=bias[:, t, bass.ds(b + i, 1)],
                                                 accum_out=signs[:, t, bass.ds(b + i, 1)]).then_inc(signs_ready, 1)
                with act.Fori(0, B // 2) as pair:
                    b = pair * 2
                    for i in range(2):
                        act.wait_ge(pack_ready, HEAD + j * B + b + i + 1)
                        nc.scalar.copy(col_bits[:, b + i, :, bass.ds(j * WB, WB)],
                                       pack_ps[i][:, 0:WORDS].rearrange("p (k w) -> p k w", w=WB)).then_inc(bits_ready, 1)

            signs_of(0, True)
            with act.Fori(0, NB - 1) as j:
                signs_of(j + 1, False)
                find_and_store(j)
            find_and_store(NB - 1)
            act.wait_ge(bits_ready, HEAD + COLS)

        @block.tensor
        def _(pe):
            pe.sem_inc(pack_ready, HEAD)
            pe.wait_ge(weight_ready, 2)
            with pe.Fori(0, NB) as j:
                for r in range(ROUNDS - 1):
                    pe.wait_ge(rm_ready, j * (ROUNDS - 1) + r + 1)
                    for b in range(B):
                        ins = nc.tensor.transpose(turn_ps[:, b, :], rm[r % 2][:, b, :], c["ident_b"][:])
                    ins.then_inc(turned_ready, 1)
                pe.wait_ge(differ_ready, j + 1)
                nc.tensor.matmul(flag_ps[0:1, 0:1], differ[:], c["ones"][:, 0:1],
                                 start=True, stop=True).then_inc(flag_ready, 1)
                with pe.Fori(0, B // 2) as pair:
                    b = pair * 2
                    for i in range(2):
                        u = j * B + b + i
                        pe.wait_ge(hot_ready, u + 1)
                        pe.wait_ge(bits_ready, HEAD + u - 1)
                        for k in range(NB):
                            for t in range(3):
                                ins = nc.tensor.matmul(pack_ps[i][:, k * WB:(k + 1) * WB],
                                                       hot[i][:, t, k * P:(k + 1) * P],
                                                       weight[:], start=(t == 0), stop=(t == 2))
                        ins.then_inc(pack_ready, 1)

        @block.vector
        def _(dve):
            flat = "p b m -> p (b m)"
            link = Chain(dve, weight_ready)
            dve.wait_ge(set_up, SET_UP)
            link(nc.vector.tensor_tensor(weight3[:], c["ident"][:].rearrange("p (k w) -> p k w", w=WB),
                                         c["bits"][:], ALU.mult))
            with nc.allow_low_precision("powers of two"):
                link(nc.vector.tensor_reduce(weight[:], weight3[:].rearrange("p k w -> p w k"), AX, ALU.add))

            def counts(link):
                link(nc.vector.tensor_tensor(num[:], rk[:, :, P - 1], outside[:], ALU.add))
                link(nc.vector.tensor_scalar(odd[:], num[:], 1, None, ALU.bitwise_and))
                nc.vector.tensor_tensor(t0[:], num[:], left[:], ALU.subtract)
                link(nc.vector.tensor_tensor(t1[:], num[:], odd[:], ALU.add))
                nc.vector.scalar_tensor_tensor(half[:], t1[:], 0.5, left[:], ALU.mult, ALU.subtract)
                nc.vector.scalar_tensor_tensor(last[:], odd[:], NONE, t0[:], ALU.mult, ALU.add)
                link(nc.vector.scalar_tensor_tensor(thr[:], num[:], 1.0, masked[:], ALU.is_gt, ALU.mult))
                nc.vector.tensor_scalar(t1[:], num[:], T_DIL, -1.0, ALU.is_le, ALU.mult)
                link(nc.vector.tensor_scalar(thr[:], thr[:], -9.0, 9.0, ALU.mult, ALU.add))
                link(nc.vector.tensor_tensor(thr[:], thr[:], t1[:], ALU.add))

            def removals(link, out):
                nc.vector.tensor_tensor(q1[:], rk[:], spread(half[:], P), ALU.is_equal)
                link(nc.vector.tensor_tensor(q2[:], rk[:], spread(last[:], P), ALU.is_equal))
                link(nc.vector.tensor_tensor(q1[:], q1[:], q2[:], ALU.add))
                link(nc.vector.tensor_tensor(q1[:], q1[:], spread(thr[:], P), ALU.is_gt))
                return nc.vector.tensor_tensor(out[:], q1[:], vb[:], ALU.mult)

            with dve.Fori(0, NB) as j:
                with dve.Fori(0, B) as b:
                    link = Chain(dve, row_step, (j * B + b) * ROW_STEPS)
                    dve.wait_ge(bits_ready, j * B + b + 1)
                    words = col_bits[:, b, j, :].rearrange("p (k w) -> p k w", w=WB).unsqueeze(2)
                    link(nc.vector.tensor_tensor(gone[:].rearrange("p (k o w) -> p k o w", o=WORD, w=WB),
                                                 words.broadcast_to([P, NB, WORD, WB]),
                                                 c["bits"][:].unsqueeze(1).broadcast_to([P, NB, WORD, WB]),
                                                 ALU.bitwise_and))
                    dve.wait_ge(sign_ready, HEAD + j * B + b + 1)
                    link(nc.vector.tensor_tensor(v[:, b, :], sign[:, b, :], gone[:], ALU.is_gt))
                    link(nc.vector.tensor_reduce(chunk[:, b, :], v[:, b, :].rearrange("p (k m) -> p k m", m=P),
                                                 AX, ALU.add))

                link = Chain(dve, joint_step, j * JOINT_STEPS)
                link(nc.vector.tensor_tensor(chunk_left[:], chunk[:], repeat(below[:, j, :], B), ALU.mult))
                nc.vector.tensor_reduce(t0[:], chunk[:], AX, ALU.add)
                link(nc.vector.tensor_reduce(left[:], chunk_left[:], AX, ALU.add))
                link(nc.vector.tensor_tensor(outside[:], t0[:], chunk[:, :, j], ALU.subtract))
                link(nc.vector.tensor_scalar(masked[:], c["mask"][:, :, j], 0.0, None, ALU.not_equal))
                link(nc.vector.tensor_tensor(a2[:], v[:, :, bass.ds(j * P, P)], repeat(upper2[:], B), ALU.mult))
                link(nc.vector.tensor_scalar(vb[:], v[:, :, bass.ds(j * P, P)], 1.0, None, ALU.mult))
                for r in range(ROUNDS):
                    if r > 0:
                        dve.wait_ge(turned_ready, j * (ROUNDS - 1) + r)
                        link(nc.vector.tensor_tensor(vb[:], a2[:], turn_ps[:], ALU.is_gt))
                    link(nc.vector.tensor_tensor_scan(rk[:].rearrange(flat), restart[:].rearrange(flat),
                                                      vb[:].rearrange(flat), 0.0, ALU.mult, ALU.add))
                    counts(link)
                    last_rm = removals(link, rm[r % 2])
                    if r < ROUNDS - 1:
                        last_rm.then_inc(rm_ready, 1)
                    else:
                        link(last_rm)
                now = rm[(ROUNDS - 1) % 2]
                link(nc.vector.tensor_tensor(q1[:], rm[0][:], rm[1][:], ALU.not_equal))
                link(nc.vector.tensor_tensor(q1[:], q1[:], repeat(upper[:], B), ALU.mult))
                nc.vector.tensor_reduce(differ[:], q1[:].rearrange(flat), AX, ALU.add).then_inc(differ_ready, 1)
                dve.wait_ge(flag_ready, j + 1)
                nc.vector.tensor_copy(flag[:], flag_ps[0:1, 0:1])
                dve.drain()
                changed = dve.value_load(flag[0:1, 0:1], min_val=0, max_val=P * P * B)
                with dve.If(changed > 0):
                    with dve.Fori(0, P):
                        nc.vector.transpose(swapped[:].rearrange(flat), now[:].rearrange(flat))
                        dve.drain()
                        for top in range(0, P, 32):
                            for under in range(top, P, 32):
                                nc.vector.tensor_copy(turned[under:under + 32, :, top:top + 32],
                                                      swapped[top:top + 32, :, under:under + 32])
                        dve.drain()
                        nc.vector.tensor_tensor(vb[:], a2[:], turned[:], ALU.is_gt)
                        dve.drain()
                        nc.vector.tensor_tensor_scan(rk[:].rearrange(flat), restart[:].rearrange(flat),
                                                     vb[:].rearrange(flat), 0.0, ALU.mult, ALU.add)
                        dve.drain()
                        counts(lambda ins: dve.drain())
                        removals(lambda ins: dve.drain(), now)
                        dve.drain()

                nc.vector.tensor_scalar(v[:, :, bass.ds(j * P, P)], vb[:], 1.0, None, ALU.mult)
                nc.vector.tensor_scalar(every[:], thr[:], 0.0, None, ALU.is_lt)
                nc.vector.tensor_tensor(bias[:, 0, :], half[:], left[:], ALU.add)
                link(nc.vector.tensor_scalar(t0[:], thr[:], 0.0, None, ALU.is_equal))
                nc.vector.tensor_tensor(bias[:, 1, :], last[:], left[:], ALU.add)
                link(nc.vector.tensor_scalar(t1[:], t0[:], 2 * NONE, 0.5 - 2 * NONE, ALU.mult, ALU.add))
                link(nc.vector.tensor_tensor(bias[:], repeat(t1[:], 2), bias[:], ALU.subtract))
                assert link.n == JOINT_STEPS
                nc.vector.tensor_scalar(own[:, 4, :, j], every[:], float(2 ** WORD - 1), None, ALU.mult)
                with dve.Fori(0, B // 2) as pair:
                    b = pair * 2
                    for i in range(2):
                        dve.wait_ge(signs_ready, HEAD + (j * B + b) * 2)
                        nc.vector.tensor_tensor_scan(rank[i][:], v[:, b + i, :], v[:, b + i, :], 0.0,
                                                     ALU.add, ALU.max).then_inc(rank_ready, 1)

                link = Chain(dve, find_step, j * FIND_STEPS)
                dve.wait_ge(signs_ready, HEAD + (j + 1) * (2 * B))
                nc.vector.tensor_scalar(pos[:], signs[:], -0.5, N / 2, ALU.mult, ALU.add)
                link(nc.vector.tensor_scalar(pos_i[:], signs[:], -0.5, N / 2, ALU.mult, ALU.add))
                nc.vector.tensor_scalar(high[:], pos_i[:], 7, 3, ALU.logical_shift_right, ALU.logical_shift_left)
                nc.vector.tensor_scalar(low[:], pos_i[:], WB - 1, None, ALU.bitwise_and)
                link(nc.vector.tensor_scalar(bit[:], pos_i[:], 3, WORD - 1, ALU.logical_shift_right, ALU.bitwise_and))
                link(nc.vector.tensor_tensor(bit[:], one[:], bit[:], ALU.logical_shift_left))
                nc.vector.tensor_tensor(own[:, 0, :, j], high[:, 0, :], low[:, 0, :], ALU.add)
                nc.vector.tensor_tensor(own[:, 2, :, j], high[:, 1, :], low[:, 1, :], ALU.add)
                nc.vector.tensor_copy(own[:, 1, :, j], bit[:, 0, :])
                nc.vector.tensor_copy(own[:, 3, :, j], bit[:, 1, :])
                assert link.n == FIND_STEPS

                with dve.Fori(0, B // 2) as pair:
                    b = pair * 2
                    for i in range(2):
                        dve.wait_ge(pack_ready, HEAD + j * B + b + i - 1)
                        for t in range(2):
                            nc.vector.tensor_scalar(hot[i][:, t, :], index[:], pos[:, t, bass.ds(b + i, 1)],
                                                    None, ALU.is_equal)
                        nc.vector.tensor_scalar(hot[i][:, 2, :], v[:, b + i, :], every[:, bass.ds(b + i, 1)],
                                                None, ALU.mult).then_inc(hot_ready, 1)


def weights(nc, c, tag, w, prev):
    with ExitStack() as ctx:
        def sb(name, shape, dt=F32):
            return ctx.enter_context(nc.sbuf_tensor(name + tag, shape, dt))

        sem = fresh(nc, ctx, tag)

        raw = sb("raw", [P, 3, P])
        bias_row = sb("bias_row", [1, P])
        final_row = sb("final_row", [1, P])
        gamma = sb("gamma", [P, 1])
        beta_in = sb("beta_in", [P, 1])
        moments = sb("moments", [P, 2])
        square = sb("square", [P, 1])
        var = sb("var", [P, 1])
        dev = sb("dev", [P, 1])
        alpha = sb("alpha", [P, 1])
        beta = sb("beta", [P, 1])
        beta_wide = sb("beta_wide", [P, P])
        sums_ps = ctx.enter_context(nc.psum_tensor("sums_ps" + tag, [P, 512], F32))
        moved_ps = [ctx.enter_context(nc.psum_tensor(f"moved_ps{i}" + tag, [P, 512], F32)) for i in range(4)]
        loaded = sem("loaded")
        turned = sem("turned")
        summed = sem("summed")
        step = sem("step")
        var_ready = sem("var_ready")
        dev_ready = sem("dev_ready")
        wide_ready = sem("wide_ready")
        moved = sem("moved")
        block = ctx.enter_context(nc.Block())
        parts = [t for t in ("Wr", "Wx", "Wl") if t in w]
        place = {"Wr": 0, "Wx": 1, "Wl": 2}
        loads = len(parts) + ("b" in w) + ("bl" in w) + 2 * (prev is not None)

        @block.sync
        def _(sp):
            for t in parts:
                sp.dma_start(raw[:, place[t], :], w[t]).then_inc(loaded, 16)
            if "b" in w:
                sp.dma_start(bias_row[:], w["b"].unsqueeze(0)).then_inc(loaded, 16)
            if "bl" in w:
                sp.dma_start(final_row[:], w["bl"].unsqueeze(0)).then_inc(loaded, 16)
            if prev is not None:
                sp.dma_start(gamma[:], w["g"].unsqueeze(1)).then_inc(loaded, 16)
                sp.dma_start(beta_in[:], w["be"].unsqueeze(1)).then_inc(loaded, 16)

        @block.tensor
        def _(pe):
            pe.wait_ge(loaded, 16 * loads)
            if w.get("turn"):
                for i, t in enumerate(parts):
                    nc.tensor.transpose(moved_ps[i][:, 0:P], raw[:, place[t], :], c["ident"][:]).then_inc(turned, 1)
            if "b" in w:
                nc.tensor.matmul(moved_ps[3][:, 0:P], c["ones"][0:1, :], bias_row[:],
                                 start=True, stop=prev is None).then_inc(moved, 1)
            if "bl" in w:
                nc.tensor.matmul(sums_ps[:, 256:256 + P], c["ones"][0:1, :], final_row[:],
                                 start=True, stop=True).then_inc(moved, 1)
            if prev is not None:
                for s in range(2):
                    for q in range(Q):
                        ins = nc.tensor.matmul(sums_ps[:, s:s + 1], prev[s][:, q, :], c["ones"][:, 0:1],
                                               start=(q == 0), stop=(q == Q - 1))
                ins.then_inc(summed, 1)
                pe.wait_ge(wide_ready, 1)
                for t in parts:
                    if t == "Wx":
                        ins = nc.tensor.matmul(moved_ps[3][:, 0:P], beta_wide[:], raw[:, 1, :], start=False, stop=True)
                    else:
                        ins = nc.tensor.matmul(moved_ps[place[t]][:, 0:P], beta_wide[:], raw[:, place[t], :],
                                               start=True, stop=True)
                    ins.then_inc(moved, 1)

        @block.scalar
        def _(act):
            if prev is not None:
                act.wait_ge(var_ready, 1)
                nc.scalar.activation(dev[:], var[:], ACT.Sqrt, bias=c["bn_eps"][:]).then_inc(dev_ready, 1)

        @block.vector
        def _(dve):
            link = Chain(dve, step)
            if w.get("turn"):
                nc.vector.memset(w["row_Wl"], 0.0)
            dve.wait_ge(loaded, 16 * loads)
            if w.get("turn"):
                dve.wait_ge(turned, len(parts))
                for i, t in enumerate(parts):
                    nc.vector.tensor_copy(w["to_" + t], moved_ps[i][:, 0:P])
            elif prev is None:
                for t in parts:
                    nc.vector.tensor_copy(w["to_" + t], raw[:, place[t], :])
            else:
                dve.wait_ge(summed, 1)
                link(nc.vector.tensor_scalar(moments[:], sums_ps[:, 0:2], 1.0 / (B * N), None, ALU.mult))
                link(nc.vector.tensor_tensor(square[:], moments[:, 0:1], moments[:, 0:1], ALU.mult))
                link(nc.vector.tensor_tensor(var[:], moments[:, 1:2], square[:], ALU.subtract))
                nc.vector.tensor_scalar(var[:], var[:], 0.0, None, ALU.max).then_inc(var_ready, 1)
                dve.wait_ge(dev_ready, 1)
                link(nc.vector.reciprocal(alpha[:], dev[:]))
                link(nc.vector.tensor_tensor(alpha[:], alpha[:], gamma[:], ALU.mult))
                link(nc.vector.tensor_tensor(beta[:], moments[:, 0:1], alpha[:], ALU.mult))
                link(nc.vector.tensor_tensor(beta[:], beta_in[:], beta[:], ALU.subtract))
                nc.vector.tensor_scalar(beta_wide[:], c["ones"][:], beta[:], None, ALU.mult).then_inc(wide_ready, 1)
                for t in parts:
                    nc.vector.tensor_scalar(w["to_" + t], raw[:, place[t], :], alpha[:], None, ALU.mult)
                dve.wait_ge(moved, len(parts) + ("b" in w) + ("bl" in w))
                if "Wr" in w:
                    nc.vector.tensor_copy(w["row_Wr"], moved_ps[0][:, 0:P])
                nc.vector.tensor_tensor(w["row_Wl"], w["row_Wl"], moved_ps[2][:, 0:P], ALU.add)
            if "b" in w:
                dve.wait_ge(moved, 1)
                nc.vector.tensor_copy(w["row_b"], moved_ps[3][:, 0:P])
            if "bl" in w:
                nc.vector.tensor_copy(w["row_bl"], sums_ps[:, 256:256 + P])


def layer(nc, c, L, adj, turned_adj, r_in, r_out, k):
    GNN, MASK, DEEP = L == 0, L == 1, L >= 2
    ZW = 2 * P if DEEP else P
    W = Q * P
    with ExitStack() as ctx:
        def sb(name, shape, dt=F32):
            return ctx.enter_context(nc.sbuf_tensor(name + f"_L{L}", shape, dt))

        def ps(name, shape, dt=F32):
            return ctx.enter_context(nc.psum_tensor(name + f"_L{L}", shape, dt))

        sem = fresh(nc, ctx, f"_L{L}")

        HALF = NB // 2
        STAGES = 1 if MASK else 2
        stage = [sb(f"stage{i}", [P, NB, P]) for i in range(STAGES)]
        piece = [sb(f"piece{i}", [P, HALF, W]) for i in range(4)]
        r_t = [sb(f"r_t{i}", [P, W]) for i in range(2)]
        agg = [sb(f"agg{i}", [P, W]) for i in range(2)]
        z = [sb(f"z{i}", [P, Q, P]) for i in range(2)]
        r = [sb(f"r{i}", [P, Q, P]) for i in range(2)]
        waste = [sb(f"waste{i}", [P, P], BF16) for i in range(Q)]
        ss = sb("ss", [P, Q])
        root = sb("root", [P, Q])
        inv = sb("inv", [P, Q])
        if GNN:
            x_in = [sb(f"x_in{i}", [P, Q, P]) for i in range(2)]
            x2 = [sb(f"x2{i}", [P, Q, P]) for i in range(2)]
            mean = sb("mean", [P, Q])
        else:
            r_sq = sb("r_sq", [P, Q, P])
        if MASK:
            nat = [sb(f"nat{i}", [P, N]) for i in range(2 * Q)]
            word1 = sb("word1", [P, WORDS])
            word2 = sb("word2", [P, WORDS])
            words = sb("words", [P, WORDS], U16)
            words2 = sb("words2", [P, WORDS], U16)
            gone = sb("gone", [P, N], U16)
            row_sum = sb("row_sum", [P, Q])
            row_max = sb("row_max", [P, Q])
        if DEEP:
            extra = [sb(f"extra{i}", [P, Q, P]) for i in range(2)]

        turn_ps = ps("turn_ps", [P, W])
        agg_ps = [ps(f"agg_ps{i}", [P, W]) for i in range(1 if MASK else 2)]
        a_ps = ps("a_ps", [P, Q, P])
        z_ps = ps("z_ps", [P, Q, ZW])
        if MASK:
            piece_ps = [ps(f"piece_ps{i}", [P, W]) for i in range(4)]

        stage_full = [sem(f"stage_full{i}") for i in range(2)]
        piece_full = [sem(f"piece_full{i}") for i in range(4)]
        piece_stored = [sem(f"piece_stored{i}") for i in range(4)]
        nat_full = [sem(f"nat_full{i}") for i in range(2 * Q)]
        x_full = [sem(f"x_full{i}") for i in range(2)]
        r_stored = [sem(f"r_stored{i}") for i in range(2)]
        x2_stored = [sem(f"x2_stored{i}") for i in range(2)]
        half_used = sem("half_used")
        turn_ready = sem("turn_ready")
        rt_ready = sem("rt_ready")
        aggs_ready = sem("aggs_ready")
        a_ready = sem("a_ready")
        z_ready = sem("z_ready")
        mask_ready = sem("mask_ready")
        mask_step = sem("mask_step")
        piece_turned = sem("piece_turned")
        piece_moved = sem("piece_moved")
        dve_step = sem("dve_step")
        end_step = sem("end_step")
        ss_ready = sem("ss_ready")
        root_ready = sem("root_ready")
        inv_ready = sem("inv_ready")
        r_ready = sem("r_ready")
        extra_ready = sem("extra_ready")
        pool_step = sem("pool_step")
        added = sem("added")
        once = sem("once")
        block = ctx.enter_context(nc.Block())
        UNITS = 2 * G
        BODIES = B // 2
        adj_cols = adj.rearrange("b (k p) (g c) -> b g p k c", p=P, c=W)
        adj_rows = adj.rearrange("b (k p) n -> b k p n", p=P)

        @block.sync
        def _(sp):
            with sp.Fori(0, BODIES) as body:
                for n in range(UNITS):
                    u = body * UNITS + n
                    b, g = body * 2 + n // G, n % G
                    if MASK:
                        for q in range(Q):
                            if q == 0:
                                sp.wait_ge(piece_turned, NB * HEAD + (u - 1) * NB)
                            i = (n % 2) * Q + q
                            sp.dma_start(nat[i][:], adj_rows[b, g * Q + q]).then_inc(nat_full[i], 16)
                    if g == 0:
                        sp.wait_ge(half_used, 2 * (HEAD + u - (STAGES - 1) * G))
                        sp.dma_start(stage[n // G % STAGES][:], r_in[b]).then_inc(stage_full[n // G % STAGES], 16)
                    if GNN:
                        sp.wait_ge(z_ready, HEAD + u - 1)
                        sp.dma_start(x_in[n % 2][:], k["x"].rearrange("b (g q p) d -> b g p q d", p=P, q=Q)[b, g]
                                     ).then_inc(x_full[n % 2], 16)
                    if not MASK:
                        for h in range(2):
                            i = 2 * (n % 2) + h
                            sp.wait_ge(half_used, 2 * HEAD + 2 * (u - 2) + h + 1)
                            src = (adj_cols[b, g, :, h * HALF:(h + 1) * HALF, :] if GNN
                                   else turned_adj[b, g, :, h * HALF:(h + 1) * HALF, :])
                            sp.dma_start(piece[i][:], src).then_inc(piece_full[i], 16)

        @block.tensor
        def _(pe):
            pe.sem_inc(half_used, 2 * HEAD)
            if MASK:
                pe.sem_inc(piece_turned, NB * HEAD)

            def post_a(u, n):
                pe.wait_ge(aggs_ready, u + 1)
                pe.wait_ge(z_ready, HEAD + u)
                for q in range(Q):
                    ins = nc.tensor.matmul(a_ps[:, q, :], agg[n % 2][:, q * P:(q + 1) * P], k["wA"][:],
                                           start=True, stop=True)
                ins.then_inc(a_ready, 1)

            with pe.Fori(0, BODIES) as body:
                for n in range(UNITS):
                    u = body * UNITS + n
                    g, s = n % G, n // G % STAGES

                    def sum_block(m):
                        i = 2 * (n % 2) + m // HALF
                        if m % HALF == 0 and not MASK:
                            pe.wait_ge(piece_full[i], (body * (UNITS // 2) + n // 2 + 1) * 16)
                        if MASK:
                            pe.wait_ge(piece_moved, HEAD + u * NB + m + 1)
                        ins = nc.tensor.matmul(agg_ps[n % len(agg_ps)][:], stage[s][:, m, :],
                                               piece[i][:, m % HALF, :], start=(m == 0), stop=(m == NB - 1))
                        if m % HALF == HALF - 1:
                            ins.then_inc(half_used, 1)

                    if MASK and n > 0:
                        post_a(u - 1, n - 1)
                    if g == 0:
                        pe.wait_ge(stage_full[s], (body * (2 // STAGES) + (n // G) // STAGES + 1) * 16)
                    for q in range(Q):
                        ins = nc.tensor.transpose(turn_ps[:, q * P:(q + 1) * P], stage[s][:, g * Q + q, :], c["ident"][:])
                    ins.then_inc(turn_ready, 1)
                    if MASK:
                        pe.wait_ge(mask_ready, (u + 1) * Q)
                    for m in range(NB + 2):
                        if MASK and m < NB:
                            pe.wait_ge(piece_moved, HEAD + u * NB + m - 3)
                            for q in range(Q):
                                ins = nc.tensor.transpose(piece_ps[m % 4][:, q * P:(q + 1) * P],
                                                          nat[(n % 2) * Q + q][:, m * P:(m + 1) * P], c["ident"][:])
                            ins.then_inc(piece_turned, 1)
                        if m >= 2:
                            sum_block(m - 2)
                        if m == 6 and not MASK and n > 0:
                            post_a(u - 1, n - 1)
                        if m == 13:
                            pe.wait_ge(rt_ready, u + 1)
                            pe.wait_ge(z_ready, HEAD + u)
                            for q in range(Q):
                                nc.tensor.matmul(z_ps[:, q, :], r_t[n % 2][:, q * P:(q + 1) * P], k["wZ"][:, 0:ZW],
                                                 start=True, stop=True)
                post_a(body * UNITS + UNITS - 1, UNITS - 1)

        @block.scalar
        def _(act):
            act.sem_inc(r_ready, HEAD)
            for i in range(2):
                act.sem_inc(r_stored[i], 1)
                act.sem_inc(x2_stored[i], 1)
            if MASK:
                act.sem_inc(piece_moved, HEAD)
                for i in range(4):
                    act.sem_inc(piece_stored[i], 1)

            def post(u, n, body):
                i = n % 2
                b, g = body * 2 + n // G, n % G
                if GNN:
                    act.wait_ge(z_ready, HEAD + u + 1)
                    act.dma_start(k["x2"][b, :, g * Q:(g + 1) * Q, :], x2[i][:]).then_inc(x2_stored[i], 16)
                act.wait_ge(z_ready, HEAD + u + 1)
                act.wait_ge(r_ready, HEAD + u)
                for q in range(Q):
                    ins = nc.scalar.activation(waste[q][:], z[i][:, q, :], ACT.Square, accum_out=ss[:, q:q + 1])
                ins.then_inc(ss_ready, 1)
                act.wait_ge(ss_ready, u + 1)
                if GNN:
                    ins = nc.scalar.activation(root[:], ss[:], ACT.Sqrt, scale=1.0 / P, bias=c["ln_eps"][:])
                else:
                    ins = nc.scalar.activation(root[:], ss[:], ACT.Sqrt)
                ins.then_inc(root_ready, 1)
                act.wait_ge(inv_ready, u + 1)
                act.wait_ge(r_stored[i], (body * (UNITS // 2) + n // 2) * 16 + 1)
                if not GNN:
                    act.wait_ge(added, HEAD + u - 1)
                for q in range(Q):
                    ins = nc.scalar.activation(r[i][:, q, :], z[i][:, q, :], ACT.Relu, scale=inv[:, q:q + 1])
                ins.then_inc(r_ready, 1)
                act.wait_ge(r_ready, HEAD + u + 1)
                act.dma_start(r_out[b, :, g * Q:(g + 1) * Q, :], r[i][:]).then_inc(r_stored[i], 16)

            with act.Fori(0, BODIES) as body:
                for n in range(UNITS):
                    u = body * UNITS + n
                    b, g = body * 2 + n // G, n % G
                    act.wait_ge(turn_ready, u + 1)
                    nc.scalar.copy(r_t[n % 2][:], turn_ps[:]).then_inc(rt_ready, 1)
                    if MASK:
                        for m in range(NB):
                            i = 2 * (n % 2) + m // HALF
                            if m % HALF == 0:
                                act.wait_ge(piece_stored[i], (body * (UNITS // 2) + n // 2) * 16 + 1)
                            act.wait_ge(piece_turned, NB * HEAD + u * NB + m + 1)
                            nc.scalar.copy(piece[i][:, m % HALF, :], piece_ps[m % 4][:]).then_inc(piece_moved, 1)
                            if m % HALF == HALF - 1:
                                act.wait_ge(piece_moved, HEAD + u * NB + m + 1)
                                h = m // HALF
                                act.dma_start(turned_adj[b, g, :, h * HALF:(h + 1) * HALF, :],
                                              piece[i][:]).then_inc(piece_stored[i], 16)
                            if m == HALF - 1 and n > 0:
                                post(u - 1, n - 1, body)
                    elif n > 0:
                        post(u - 1, n - 1, body)
                    act.wait_ge(half_used, 2 * (HEAD + u + 1))
                    nc.scalar.copy(agg[n % 2][:], agg_ps[n % len(agg_ps)][:]).then_inc(aggs_ready, 1)
                post(body * UNITS + UNITS - 1, UNITS - 1, body)
            for i in range(2):
                act.wait_ge(r_stored[i], BODIES * (UNITS // 2) * 16 + 1)
                if GNN:
                    act.wait_ge(x2_stored[i], BODIES * (UNITS // 2) * 16 + 1)
            if MASK:
                for i in range(4):
                    act.wait_ge(piece_stored[i], BODIES * (UNITS // 2) * 16 + 1)

        @block.vector
        def _(dve):
            dve.sem_inc(z_ready, HEAD)
            if GNN:
                nc.vector.reciprocal(k["rdeg"][:], k["deg"][:]).then_inc(once, 1)
                dve.wait_ge(once, 1)

            STEPS = 5 if GNN else 2

            def post(u, n, body):
                i = n % 2
                b, g = body * 2 + n // G, n % G
                link = Chain(dve, dve_step, u * STEPS)
                dve.wait_ge(a_ready, u + 1)
                dve.wait_ge(r_ready, HEAD + u - 1)
                if DEEP:
                    y = k["y"][:, b, g * Q:(g + 1) * Q, :]
                    if L == 2:
                        nc.vector.tensor_scalar(y, z_ps[:, :, P:2 * P], 1.0, None, ALU.mult)
                    else:
                        nc.vector.tensor_tensor(y, y, z_ps[:, :, P:2 * P], ALU.add)
                link(nc.vector.tensor_tensor(z[i][:], a_ps[:], spread(k["rdeg"][:, b, g * Q:(g + 1) * Q], P), ALU.mult))
                link(nc.vector.tensor_tensor(z[i][:], z[i][:], z_ps[:, :, 0:P], ALU.add))
                if GNN:
                    link(nc.vector.tensor_tensor(z[i][:], z[i][:], repeat(k["row_b"][:], Q), ALU.add))
                    dve.wait_ge(x_full[i], (body * (UNITS // 2) + n // 2 + 1) * 16)
                    dve.wait_ge(x2_stored[i], (body * (UNITS // 2) + n // 2) * 16 + 1)
                    link(nc.vector.scalar_tensor_tensor(x2[i][:], z[i][:], 0.0, x_in[i][:], ALU.max, ALU.add))
                    link(nc.vector.tensor_reduce(mean[:], x2[i][:], AX, ALU.add))
                    nc.vector.tensor_scalar(mean[:], mean[:], 1.0 / P, None, ALU.mult).then_inc(end_step, 1)
                    dve.wait_ge(end_step, u + 1)
                    nc.vector.tensor_tensor(z[i][:], x2[i][:], spread(mean[:], P), ALU.subtract).then_inc(z_ready, 1)
                else:
                    if DEEP:
                        dve.wait_ge(extra_ready, u + 1)
                        nc.vector.tensor_tensor(z[i][:], z[i][:], extra[i][:], ALU.add).then_inc(z_ready, 1)
                    else:
                        nc.vector.tensor_tensor(z[i][:], z[i][:], repeat(k["row_b"][:], Q), ALU.add).then_inc(z_ready, 1)
                dve.wait_ge(root_ready, u + 1)
                if not GNN:
                    nc.vector.tensor_scalar(root[:], root[:], NORM_EPS, None, ALU.max).then_inc(end_step, 1)
                    dve.wait_ge(end_step, 2 * u + 1)
                    nc.vector.reciprocal(inv[:], root[:]).then_inc(end_step, 1)
                    dve.wait_ge(end_step, 2 * u + 2)
                    nc.vector.tensor_tensor(inv[:], inv[:], c["mask"][:, b, g * Q:(g + 1) * Q], ALU.mult).then_inc(inv_ready, 1)
                else:
                    nc.vector.reciprocal(inv[:], root[:]).then_inc(inv_ready, 1)

            with dve.Fori(0, BODIES) as body:
                for n in range(UNITS):
                    u = body * UNITS + n
                    b, g = body * 2 + n // G, n % G
                    if MASK:
                        PER = 5 * Q + 2
                        link = Chain(dve, mask_step, u * PER)
                        for q in range(Q):
                            i, m = (n % 2) * Q + q, g * Q + q

                            def own(t):
                                return k["own"][:, t, b, m:m + 1]
                            nc.vector.tensor_scalar(word1[:], c["word_index"][:], own(0), own(1), ALU.is_equal, ALU.mult)
                            link(nc.vector.tensor_scalar(word2[:], c["word_index"][:], own(2), own(3), ALU.is_equal, ALU.mult))
                            link(nc.vector.scalar_tensor_tensor(words[:], word1[:], own(4), word2[:], ALU.add, ALU.add))
                            link(nc.vector.tensor_tensor(words2[:], words[:], k["col_bits"][:, b, m, :], ALU.bitwise_or))
                            link(nc.vector.tensor_tensor(
                                gone[:].rearrange("p (k o w) -> p k o w", o=WORD, w=WB),
                                words2[:].rearrange("p (k w) -> p k w", w=WB).unsqueeze(2).broadcast_to([P, NB, WORD, WB]),
                                c["bits"][:].unsqueeze(1).broadcast_to([P, NB, WORD, WB]), ALU.bitwise_and))
                            dve.wait_ge(nat_full[i], (body * (UNITS // 2) + n // 2 + 1) * 16)
                            link(nc.vector.scalar_tensor_tensor(nat[i][:], gone[:], 0.0, nat[i][:], ALU.is_equal, ALU.mult,
                                                                accum_out=row_sum[:, q:q + 1]))
                            nc.vector.sem_inc(mask_ready, 1)
                        link(nc.vector.tensor_scalar(row_max[:], row_sum[:], 1.0, None, ALU.max))
                        rdeg = k["rdeg"][:, b, g * Q:(g + 1) * Q]
                        link(nc.vector.reciprocal(rdeg, row_max[:]))
                        nc.vector.tensor_tensor(k["ratio"][:, b, g * Q:(g + 1) * Q], row_sum[:], rdeg, ALU.mult)
                        assert link.n == PER
                    if n > 0:
                        post(u - 1, n - 1, body)
                post(body * UNITS + UNITS - 1, UNITS - 1, body)

        if not GNN:
            @block.gpsimd
            def _(pool):
                pool.sem_inc(added, HEAD)
                link = Chain(pool, once)
                for s in k["sums"]:
                    link(nc.gpsimd.memset(s[:], 0.0))
                with pool.Fori(0, BODIES) as body:
                    for n in range(UNITS):
                        u = body * UNITS + n
                        i = n % 2
                        b, g = body * 2 + n // G, n % G
                        link = Chain(pool, pool_step, u * (3 if DEEP else 2))
                        if DEEP:
                            pool.wait_ge(z_ready, HEAD + u - 1)
                            link(nc.gpsimd.tensor_tensor(extra[i][:], spread(k["ratio"][:, b, g * Q:(g + 1) * Q], P),
                                                         repeat(k["row_Wr"][:], Q), ALU.mult))
                            nc.gpsimd.tensor_tensor(extra[i][:], extra[i][:], repeat(k["row_b"][:], Q),
                                                    ALU.add).then_inc(extra_ready, 1)
                        pool.wait_ge(r_ready, HEAD + u + 1)
                        link(nc.gpsimd.tensor_tensor(r_sq[:], r[i][:], r[i][:], ALU.mult))
                        nc.gpsimd.tensor_tensor(k["sums"][0][:], k["sums"][0][:], r[i][:], ALU.add)
                        link(nc.gpsimd.tensor_tensor(k["sums"][1][:], k["sums"][1][:], r_sq[:], ALU.add))
                        pool.sem_inc(added, 1)


def finish(nc, c, r_in, k, out):
    with ExitStack() as ctx:
        def sb(name, shape, dt=F32):
            return ctx.enter_context(nc.sbuf_tensor(name + "_fin", shape, dt))

        sem = fresh(nc, ctx, "_fin")

        r = [sb(f"r{i}", [P, Q, P]) for i in range(2)]
        x2 = [sb(f"x2{i}", [P, Q, P]) for i in range(2)]
        r_t = [sb(f"r_t{i}", [P, Q, P]) for i in range(2)]
        rest = [sb(f"rest{i}", [P, Q, P]) for i in range(2)]
        last = [sb(f"last{i}", [P, Q, P]) for i in range(2)]
        mask2 = sb("mask2", [P, B, NB])
        turn_ps = [ctx.enter_context(nc.psum_tensor(f"turn_ps{i}" + "_fin", [P, Q, P], F32)) for i in range(2)]
        y_ps = [ctx.enter_context(nc.psum_tensor(f"y_ps{i}" + "_fin", [P, Q, P], F32)) for i in range(2)]
        loaded = [sem(f"loaded{i}") for i in range(2)]
        stored = [sem(f"stored{i}") for i in range(2)]
        turn_ready = sem("turn_ready")
        rt_ready = sem("rt_ready")
        y_ready = sem("y_ready")
        rest_ready = sem("rest_ready")
        pool_step = sem("pool_step")
        dve_step = sem("dve_step")
        out_ready = sem("out_ready")
        mask_made = sem("mask_made")
        block = ctx.enter_context(nc.Block())
        nodes = out.rearrange("b (g q p) d -> b g p q d", p=P, q=Q)

        @block.sync
        def _(sp):
            with sp.Fori(0, B) as b:
                for g in range(G):
                    u, i = b * G + g, g % 2
                    sp.wait_ge(out_ready, HEAD + u - 1)
                    sp.dma_start(r[i][:], r_in[b, :, g * Q:(g + 1) * Q, :]).then_inc(loaded[i], 16)
                    sp.dma_start(x2[i][:], k["x2"][b, :, g * Q:(g + 1) * Q, :]).then_inc(loaded[i], 16)

        @block.tensor
        def _(pe):
            def turn(u, i, n):
                pe.wait_ge(loaded[i], n * 32)
                for q in range(Q):
                    ins = nc.tensor.transpose(turn_ps[i][:, q, :], r[i][:, q, :], c["ident"][:])
                ins.then_inc(turn_ready, 1)

            with pe.Fori(0, B) as b:
                for g in range(G):
                    u, i = b * G + g, g % 2
                    turn(u, i, b * 2 + g // 2 + 1)
                    pe.wait_ge(rt_ready, u + 1)
                    pe.wait_ge(out_ready, HEAD + u - 1)
                    for q in range(Q):
                        ins = nc.tensor.matmul(y_ps[i][:, q, :], r_t[i][:, q, :], k["wY"][:], start=True, stop=True)
                    ins.then_inc(y_ready, 1)

        @block.scalar
        def _(act):
            for i in range(2):
                act.sem_inc(stored[i], 1)
            with act.Fori(0, B) as b:
                for g in range(G):
                    u, i = b * G + g, g % 2
                    act.wait_ge(turn_ready, u + 1)
                    nc.scalar.copy(r_t[i][:], turn_ps[i][:]).then_inc(rt_ready, 1)
                    act.wait_ge(out_ready, HEAD + u + 1)
                    act.dma_start(nodes[b, g], last[i][:]).then_inc(stored[i], 16)
            for i in range(2):
                act.wait_ge(stored[i], B * 2 * 16 + 1)

        @block.gpsimd
        def _(pool):
            nc.gpsimd.tensor_tensor(mask2[:], c["mask"][:], c["mask"][:], ALU.mult).then_inc(mask_made, 1)
            with pool.Fori(0, B) as b:
                for g in range(G):
                    u, i = b * G + g, g % 2
                    link = Chain(pool, pool_step, u * 3)
                    pool.wait_ge(out_ready, HEAD + u - 1)
                    link(nc.gpsimd.tensor_tensor(rest[i][:], spread(c["mask"][:, b, g * Q:(g + 1) * Q], P),
                                                 repeat(k["row_bl"][:], Q), ALU.mult))
                    pool.wait_ge(loaded[i], (b * 2 + g // 2 + 1) * 32)
                    link(nc.gpsimd.tensor_tensor(rest[i][:], rest[i][:], x2[i][:], ALU.add))
                    y = k["y"][:, b, g * Q:(g + 1) * Q, :]
                    link(nc.gpsimd.tensor_tensor(y, y, repeat(k["row_Wl"][:], Q), ALU.add))
                    pool.sem_inc(rest_ready, 1)

        @block.vector
        def _(dve):
            dve.sem_inc(out_ready, HEAD)
            with dve.Fori(0, B) as b:
                for g in range(G):
                    u, i = b * G + g, g % 2
                    link = Chain(dve, dve_step, u * 2)
                    dve.wait_ge(rest_ready, u + 1)
                    dve.wait_ge(y_ready, u + 1)
                    dve.wait_ge(mask_made, 1)
                    dve.wait_ge(stored[i], (b * 2 + g // 2) * 16 + 1)
                    link(nc.vector.tensor_tensor(last[i][:], y_ps[i][:], k["y"][:, b, g * Q:(g + 1) * Q, :], ALU.add))
                    link(nc.vector.tensor_tensor(last[i][:], last[i][:], spread(mask2[:, b, g * Q:(g + 1) * Q], P),
                                                 ALU.mult))
                    nc.vector.tensor_tensor(last[i][:], last[i][:], rest[i][:], ALU.add).then_inc(out_ready, 1)


def build(nc, a, out):
    h = [nc.dram_tensor(f"r{i}", (B, P, NB, P), F32, kind="Internal").ap() for i in range(4)]
    x2 = nc.dram_tensor("x2_scratch", (B, P, NB, P), F32, kind="Internal").ap()
    turned = nc.dram_tensor("turned_adj", (B, G, P, NB, Q * P), F32, kind="Internal").ap()
    with ExitStack() as ctx:
        def sb(name, shape, dt=F32):
            return ctx.enter_context(nc.sbuf_tensor(name, shape, dt))

        c = constants(nc, ctx, a["nodemask"])
        k = {name: sb(name, [P, B, NB]) for name in ("deg", "rdeg", "ratio")}
        k["sums"] = [sb(f"sums{i}", [P, Q, P]) for i in range(2)]
        k["wA"], k["wZ"] = sb("wA", [P, P]), sb("wZ", [P, 2 * P])
        for name in ("row_Wr", "row_Wl", "row_b", "row_bl"):
            k[name] = sb(name, [P, P])
        k["x"], k["x2"] = a["x"], x2
        rows = {name: k[name][:] for name in ("row_Wr", "row_Wl", "row_b", "row_bl")}

        def sage(i, **more):
            return {"Wr": a[f"L1_gnn_Wr{i}"], "Wx": a[f"L1_gnn_Wx{i}"], "b": a[f"L1_gnn_b{i}"],
                    "to_Wr": k["wA"][:], "to_Wx": k["wZ"][:, 0:P], "to_Wl": k["wZ"][:, P:2 * P], **rows, **more}

        def normed(i):
            return {"g": a[f"L1_gnn_g{i}"], "be": a[f"L1_gnn_be{i}"], "Wl": a["L1_gnn_Wl"][(i - 1) * P:i * P, :]}

        with ExitStack() as early:
            k["col_bits"] = early.enter_context(nc.sbuf_tensor("col_bits", [P, B, NB, WORDS], U16))
            k["own"] = early.enter_context(nc.sbuf_tensor("own", [P, 5, B, NB], F32))
            norm(nc, c, a["x"], h[0])
            dilate(nc, c, a["adj"], k["col_bits"], k["deg"], k["own"])
            weights(nc, c, "_w0", {"Wx": a["L0_gnn_W"][:, 0:P], "Wr": a["L0_gnn_W"][:, P:2 * P], "b": a["L0_gnn_b"],
                            "turn": True, "to_Wr": k["wA"][:], "to_Wx": k["wZ"][:, 0:P], **rows}, None)
            layer(nc, c, 0, a["adj"], turned, h[0], h[1], k)
            weights(nc, c, "_w1", sage(1), None)
            layer(nc, c, 1, a["adj"], turned, h[1], h[2], k)
        k["y"] = sb("y", [P, B, NB, P])
        weights(nc, c, "_w2", sage(2, **normed(1)), k["sums"])
        layer(nc, c, 2, a["adj"], turned, h[2], h[3], k)
        weights(nc, c, "_w3", sage(3, **normed(2)), k["sums"])
        layer(nc, c, 3, a["adj"], turned, h[3], h[0], k)
        k["wY"] = k["wA"]
        weights(nc, c, "_w4", {**normed(3), "bl": a["L1_gnn_bl"], "to_Wl": k["wY"][:], **rows}, k["sums"])
        finish(nc, c, h[0], k, out)


NAMES = (["x", "adj", "nodemask", "L0_gnn_W", "L0_gnn_b"]
         + [f"L1_gnn_{t}{i}" for i in (1, 2, 3) for t in ("Wr", "Wx", "b", "g", "be")] + ["L1_gnn_Wl", "L1_gnn_bl"])


def kernel(**inputs):
    import numpy as _np
    import concourse.bacc as _bacc
    from concourse import mybir as _mybir
    from concourse.bass_utils import run_bass_kernel_spmd as _run

    nc = _bacc.Bacc("TRN2", target_bir_lowering=False, num_devices=1)
    arrays, args = {}, {}
    for name in NAMES:
        arr = _np.ascontiguousarray(inputs[name])
        arrays[f"in_{name}"] = arr
        args[name] = nc.dram_tensor(f"in_{name}", arr.shape, _mybir.dt.from_np(arr.dtype), kind="ExternalInput").ap()
    out = nc.dram_tensor("out", (B, N, P), F32, kind="ExternalOutput").ap()
    build(nc, args, out)
    r = _run(nc, [arrays], core_ids=[0])
    return r.results[0]["out"]
```

```python
from contextlib import ExitStack

import concourse.bass as bass
from concourse import mybir

ALU = mybir.AluOpType
ACT = mybir.ActivationFunctionType
AX = mybir.AxisListType.X
F32 = mybir.dt.float32
BF16 = mybir.dt.bfloat16
F16 = mybir.dt.float16
I32 = mybir.dt.int32
I8 = mybir.dt.int8
U16 = mybir.dt.uint16

P = 128
B = 8
N = 2048
NB = N // P
COLS = B * NB
WORD = 16
WB = P // WORD
WORDS = N // WORD
Q = 4
G = NB // Q
ROUNDS = 5
RANKS = 4
T_DIL = 10.0
BN_EPS = 1e-5
LN_EPS = 1e-5
NORM_EPS = 1e-12
NONE = 4096.0


class Chain:

    def __init__(self, engine, sem, base=0):
        self.engine, self.sem, self.base, self.n = engine, sem, base, 0

    def __call__(self, instruction):
        instruction.then_inc(self.sem, 1)
        self.n += 1
        self.engine.wait_ge(self.sem, self.base + self.n)


HEAD = 8


def fresh(nc, ctx, tag):
    made = []

    def clear(kind, *_):
        if kind is not None:
            return
        with nc.Block() as block:
            @block.gpsimd
            def _(pool):
                for s in made:
                    pool.sem_clear(s)

    def sem(name):
        made.append(ctx.enter_context(nc.semaphore(name + tag)))
        return made[-1]

    ctx.push(clear)
    return sem


def spread(ap, n):
    return ap.unsqueeze(2).broadcast_to([ap.shape[0], ap.shape[1], n])


def repeat(ap, n):
    return ap.unsqueeze(1).broadcast_to([ap.shape[0], n, ap.shape[1]])


def constants(nc, ctx, nodemask):
    def sb(name, shape, dt):
        return ctx.enter_context(nc.sbuf_tensor(name, shape, dt))

    c = {
        "ident": sb("ident", [P, P], F32),
        "ident_b": sb("ident_b", [P, P], BF16),
        "ones": sb("ones", [P, P], F32),
        "mask": sb("mask", [P, B, NB], F32),
        "word_index": sb("word_index", [P, WORDS], F32),
        "bits": sb("bits", [P, WORD, WB], U16),
        "ln_eps": sb("ln_eps", [P, 1], F32),
        "bn_eps": sb("bn_eps", [P, 1], F32),
    }
    with ExitStack() as inner:
        sem = fresh(nc, inner, "_c")
        mask_int = inner.enter_context(nc.sbuf_tensor("mask_int", [COLS, P], I32))
        mask_rows = inner.enter_context(nc.sbuf_tensor("mask_rows", [COLS, P], F32))
        mask_ps = inner.enter_context(nc.psum_tensor("mask_ps", [P, 512], F32))
        mask_loaded = sem("mask_loaded")
        rows_ready = sem("rows_ready")
        mask_turned = sem("mask_turned")
        filled = sem("filled")
        mask_copied = sem("mask_copied")
        block = inner.enter_context(nc.Block())

        @block.sync
        def _(sp):
            sp.dma_start(mask_int[:], nodemask.rearrange("b (j p) -> (b j) p", p=P)).then_inc(mask_loaded, 16)

        @block.gpsimd
        def _(pool):
            link = Chain(pool, filled)
            for t in ("ident", "ident_b"):
                link(nc.gpsimd.memset(c[t][:], 0.0))
                link(nc.gpsimd.affine_select(out=c[t][:], in_=c[t][:], compare_op=ALU.not_equal, fill=1.0,
                                             base=0, pattern=[[-1, P]], channel_multiplier=1))
            link(nc.gpsimd.memset(c["ones"][:], 1.0))
            link(nc.gpsimd.memset(c["ln_eps"][:], LN_EPS))
            link(nc.gpsimd.memset(c["bn_eps"][:], BN_EPS))
            for bit in range(WORD):
                link(nc.gpsimd.memset(c["bits"][:, bit, :], 1 << bit))
            link(nc.gpsimd.iota(c["word_index"][:], pattern=[[1, WORDS]], base=0, channel_multiplier=0,
                                allow_small_or_imprecise_dtypes=True))

        @block.vector
        def _(dve):
            dve.wait_ge(mask_loaded, 16)
            nc.vector.tensor_copy(mask_rows[:], mask_int[:]).then_inc(rows_ready, 1)
            dve.wait_ge(mask_turned, 1)
            nc.vector.tensor_copy(c["mask"][:].rearrange("p b j -> p (b j)"),
                                  mask_ps[:, 0:COLS]).then_inc(mask_copied, 1)
            dve.wait_ge(mask_copied, 1)

        @block.tensor
        def _(pe):
            pe.wait_ge(rows_ready, 1)
            pe.wait_ge(filled, 4)
            nc.tensor.transpose(mask_ps[:, 0:COLS], mask_rows[:], c["ident"][:]).then_inc(mask_turned, 1)
    return c


def norm(nc, c, x, h_out):
    with ExitStack() as ctx:
        def sb(name, shape, dt):
            return ctx.enter_context(nc.sbuf_tensor(name + "_norm", shape, dt))

        sem = fresh(nc, ctx, "_norm")

        xt = [sb(f"xt{i}", [P, NB, P], F32) for i in range(2)]
        h = [sb(f"h{i}", [P, NB, P], F32) for i in range(2)]
        square = sb("square", [P, NB, P], F32)
        mean = sb("mean", [P, NB], F32)
        var = sb("var", [P, NB], F32)
        dev = sb("dev", [P, NB], F32)
        rstd = sb("rstd", [P, NB], F32)
        x_loaded = [sem(f"x_loaded{i}") for i in range(2)]
        h_stored = [sem(f"h_stored{i}") for i in range(2)]
        dve_step = sem("dve_step")
        centred = sem("centred")
        squared = sem("squared")
        summed = sem("summed")
        rooted = sem("rooted")
        scaled = sem("scaled")
        h_ready = sem("h_ready")
        block = ctx.enter_context(nc.Block())

        @block.sync
        def _(sp):
            with sp.Fori(0, B // 2) as pair:
                b = pair * 2
                for i in range(2):
                    sp.wait_ge(h_ready, HEAD + b + i - 1)
                    for g in range(G):
                        sp.dma_start(xt[i][:, g * Q:(g + 1) * Q, :],
                                     x.rearrange("b (g q p) d -> b g p q d", p=P, q=Q)[b + i, g]).then_inc(x_loaded[i], 16)

        @block.vector
        def _(dve):
            with dve.Fori(0, B // 2) as pair:
                b = pair * 2
                for i in range(2):
                    link = Chain(dve, dve_step, (b + i) * 3)
                    dve.wait_ge(x_loaded[i], (b * 8 + 16) * G)
                    link(nc.vector.tensor_reduce(mean[:], xt[i][:], AX, ALU.add))
                    link(nc.vector.tensor_scalar(mean[:], mean[:], 1.0 / P, None, ALU.mult))
                    nc.vector.tensor_tensor(xt[i][:], xt[i][:], spread(mean[:], P), ALU.subtract).then_inc(centred, 1)
                    dve.wait_ge(squared, b + i + 1)
                    nc.vector.tensor_reduce(var[:], square[:], AX, ALU.add).then_inc(summed, 1)
                    dve.wait_ge(rooted, b + i + 1)
                    link(nc.vector.reciprocal(rstd[:], dev[:]))
                    nc.vector.tensor_tensor(xt[i][:], xt[i][:], spread(rstd[:], P), ALU.mult).then_inc(scaled, 1)

        @block.scalar
        def _(act):
            act.sem_inc(h_ready, HEAD)
            for i in range(2):
                act.sem_inc(h_stored[i], 1)
            with act.Fori(0, B // 2) as pair:
                b = pair * 2
                for i in range(2):
                    act.wait_ge(centred, b + i + 1)
                    nc.scalar.activation(square[:], xt[i][:], ACT.Square).then_inc(squared, 1)
                    act.wait_ge(summed, b + i + 1)
                    nc.scalar.activation(dev[:], var[:], ACT.Sqrt, scale=1.0 / P, bias=c["ln_eps"][:]).then_inc(rooted, 1)
                    act.wait_ge(scaled, b + i + 1)
                    act.wait_ge(h_stored[i], b * 8 + 1)
                    nc.scalar.activation(h[i][:], xt[i][:], ACT.Relu).then_inc(h_ready, 1)
                    act.wait_ge(h_ready, HEAD + b + i + 1)
                    act.dma_start(h_out[b + i], h[i][:]).then_inc(h_stored[i], 16)
            for i in range(2):
                act.wait_ge(h_stored[i], B // 2 * 16 + 1)


def dilate(nc, c, adj, col_bits, deg, own):
    with ExitStack() as ctx:
        def sb(name, shape, dt):
            return ctx.enter_context(nc.sbuf_tensor(name + "_dil", shape, dt))

        def ps(name, shape, dt):
            return ctx.enter_context(nc.psum_tensor(name + "_dil", shape, dt))

        sem = fresh(nc, ctx, "_dil")

        nat = [sb(f"nat{i}", [P, N], F32) for i in range(2)]
        sign = sb("sign", [P, B, N], BF16)
        waste = [sb(f"waste{i}", [P, N], I8) for i in range(3)]
        gone = [sb(f"gone{i}", [P, N], U16) for i in range(2)]
        v = sb("v", [P, B, N], BF16)
        rank = [sb(f"rank{i}", [P, N], F16)[:] for i in range(RANKS - 2)] + [t[:].bitcast(F16) for t in gone]
        hot = [sb(f"hot{i}", [P, 3, N], BF16) for i in range(2)]
        index = sb("index", [P, N], F16)
        weight = sb("weight", [P, WB], BF16)
        weight3 = sb("weight3", [P, WORD, WB], F32)
        halved = [sb(f"halved{i}", [P, NB, P // 2], BF16) for i in range(2)]
        below = sb("below", [P, NB, NB], F32)
        upper2 = sb("upper2", [P, P], BF16)
        restart = sb("restart", [P, B, P], BF16)
        chunk = sb("chunk", [P, B, NB], F32)
        chunk_left = sb("chunk_left", [P, B, NB], F32)
        left = sb("left", [P, B], F32)
        outside = sb("outside", [P, B], F32)
        masked = sb("masked", [P, B], F32)
        num = sb("num", [P, B], I32)
        odd = sb("odd", [P, B], I32)
        t0 = sb("t0", [P, B], F32)
        t1 = sb("t1", [P, B], F32)
        half = sb("half", [P, B], F32)
        last = sb("last", [P, B], F32)
        valid = sb("valid", [P, B], F32)
        none = sb("none", [P, B], F32)
        every = sb("every", [P, B], F32)
        spot = sb("spot", [P, 32], F32)
        spot_t = sb("spot_t", [P, 32], F32)
        spot_max = sb("spot_max", [P, 1], F32)
        spots = sb("spots", [1, 4], F32)
        a2 = sb("a2", [P, B, P], BF16)
        vbs = [sb(f"vb{i}", [P, B, P], BF16) for i in range(2)]
        rk = sb("rk", [P, B, P], BF16)
        q1 = sb("q1", [P, B, P], BF16)
        q2 = sb("q2", [P, B, P], BF16)
        rm = sb("rm", [P, B, P], BF16)
        swapped = sb("swapped", [P, B, P], BF16)
        turned = sb("turned", [P, B, P], BF16)
        flag = sb("flag", [1, 1], I32)
        bias = sb("bias", [P, 2, B], F32)
        signs = sb("signs", [P, 2, B], F32)
        pos = sb("pos", [P, 2, B], F32)
        pos_i = sb("pos_i", [P, 2, B], I32)
        high = sb("high", [P, 2, B], I32)
        low = sb("low", [P, 2, B], I32)
        bit = sb("bit", [P, 2, B], I32)
        one = sb("one", [P, 2, B], I32)

        pack_ps = [ps(f"pack_ps{i}", [P, 512], F32) for i in range(2)]

        nat_full = [sem(f"nat_full{i}") for i in range(2)]
        sign_ready = sem("sign_ready")
        act_step = sem("act_step")
        set_up = sem("set_up")
        weight_ready = sem("weight_ready")
        row_step = sem("row_step")
        joint_step = sem("joint_step")
        rank_ready = sem("rank_ready")
        signs_ready = sem("signs_ready")
        find_step = sem("find_step")
        hot_ready = sem("hot_ready")
        pack_ready = sem("pack_ready")
        bits_ready = sem("bits_ready")

        SET_UP = 11
        ROW_STEPS = 6
        JOINT_STEPS = 17
        FIND_STEPS = 3
        H = B // 2
        block = ctx.enter_context(nc.Block())
        rows = adj.rearrange("b (j p) n -> b j p n", p=P)

        @block.gpsimd
        def _(pool):
            link = Chain(pool, set_up)
            link(nc.gpsimd.iota(index[:], pattern=[[1, N]], base=0, channel_multiplier=0,
                                allow_small_or_imprecise_dtypes=True))
            link(nc.gpsimd.memset(one[:], 1))
            link(nc.gpsimd.memset(turned[:], 0.0))
            link(nc.gpsimd.memset(col_bits[:].rearrange("p b k w -> p (b k w)").bitcast(I32), 0))
            link(nc.gpsimd.memset(below[:], 1.0))
            link(nc.gpsimd.memset(spot[:], 0.0))
            link(nc.gpsimd.memset(restart[:], 1.0))
            link(nc.gpsimd.memset(restart[:, :, 0:1], 0.0))
            link(nc.gpsimd.affine_select(out=below[:], in_=below[:], compare_op=ALU.is_gt, fill=0.0,
                                         base=0, pattern=[[1, NB], [-1, NB]], channel_multiplier=0))
            link(nc.gpsimd.memset(upper2[:], 2.0))
            link(nc.gpsimd.affine_select(out=upper2[:], in_=upper2[:], compare_op=ALU.is_ge, fill=1.0,
                                         base=0, pattern=[[1, P]], channel_multiplier=-1))
            assert link.n == SET_UP

        @block.sync
        def _(sp):
            with sp.Fori(0, NB) as j:
                with sp.Fori(0, B // 2) as pair:
                    b = pair * 2
                    for i in range(2):
                        sp.wait_ge(sign_ready, HEAD + j * B + b + i - 1)
                        sp.dma_start(nat[i][:], rows[b + i, j, :, :]).then_inc(nat_full[i], 16)

        @block.scalar
        def _(act):
            act.sem_inc(sign_ready, HEAD)
            act.sem_inc(bits_ready, HEAD)
            act.sem_inc(act_step, HEAD)
            act.sem_inc(signs_ready, HEAD)

            def signs_of(j, first):
                with act.Fori(0, B // 2) as pair:
                    b = pair * 2
                    for i in range(2):
                        u = j * B + b + i
                        act.wait_ge(nat_full[i], j * (B * 8) + b * 8 + 16)
                        if not first:
                            act.wait_ge(row_step, HEAD + (j * B + b - B) * ROW_STEPS + 4)
                        nc.scalar.activation(sign[:, b + i, :], nat[i][:], ACT.Sign).then_inc(sign_ready, 1)
                        act.wait_ge(sign_ready, HEAD + u + 1)
                        act.wait_ge(act_step, HEAD + u)
                        nc.scalar.activation(waste[2][:], sign[:, b + i, :], ACT.Square,
                                             accum_out=deg[:, b + i, bass.ds(j, 1)]).then_inc(act_step, 1)

            def find_and_store(j):
                with act.Fori(0, B // RANKS) as part:
                    b = part * RANKS
                    for i in range(RANKS):
                        act.wait_ge(rank_ready, j * B + b + i + 1)
                        for t in range(2):
                            act.wait_ge(signs_ready, HEAD + (j * B + b + i) * 2 + t - 1)
                            nc.scalar.activation(waste[t][:], rank[i], ACT.Sign,
                                                 bias=bias[:, t, bass.ds(b + i, 1)],
                                                 accum_out=signs[:, t, bass.ds(b + i, 1)]).then_inc(signs_ready, 1)
                with act.Fori(0, B // 2) as pair:
                    b = pair * 2
                    for i in range(2):
                        act.wait_ge(pack_ready, HEAD + j * B + b + i + 1)
                        nc.scalar.copy(col_bits[:, b + i, :, bass.ds(j * WB, WB)],
                                       pack_ps[i][:, 0:WORDS].rearrange("p (k w) -> p k w", w=WB)).then_inc(bits_ready, 1)

            signs_of(0, True)
            with act.Fori(0, NB - 1) as j:
                signs_of(j + 1, False)
                find_and_store(j)
            find_and_store(NB - 1)
            act.wait_ge(bits_ready, HEAD + COLS)

        @block.tensor
        def _(pe):
            pe.sem_inc(pack_ready, HEAD)
            pe.wait_ge(weight_ready, 2)
            with pe.Fori(0, NB) as j:
                with pe.Fori(0, B // 2) as pair:
                    b = pair * 2
                    for i in range(2):
                        u = j * B + b + i
                        pe.wait_ge(hot_ready, u + 1)
                        pe.wait_ge(bits_ready, HEAD + u - 1)
                        for k in range(NB):
                            for t in range(3):
                                ins = nc.tensor.matmul(pack_ps[i][:, k * WB:(k + 1) * WB],
                                                       hot[i][:, t, k * P:(k + 1) * P],
                                                       weight[:], start=(t == 0), stop=(t == 2))
                        ins.then_inc(pack_ready, 1)

        @block.vector
        def _(dve):
            flat = "p b m -> p (b m)"
            dve.sem_inc(row_step, HEAD)
            link = Chain(dve, weight_ready)
            dve.wait_ge(set_up, SET_UP)
            link(nc.vector.tensor_tensor(weight3[:], c["ident"][:].rearrange("p (k w) -> p k w", w=WB),
                                         c["bits"][:], ALU.mult))
            with nc.allow_low_precision("powers of two"):
                link(nc.vector.tensor_reduce(weight[:], weight3[:].rearrange("p k w -> p w k"), AX, ALU.add))

            def full_round(link, vb):
                link(nc.vector.tensor_tensor_scan(rk[:].rearrange(flat), restart[:].rearrange(flat),
                                                  vb[:].rearrange(flat), 0.0, ALU.mult, ALU.add))
                link(nc.vector.tensor_tensor(num[:], rk[:, :, P - 1], outside[:], ALU.add))
                nc.vector.scalar_tensor_tensor(valid[:], num[:], 1.0, masked[:], ALU.is_gt, ALU.mult)
                link(nc.vector.tensor_scalar(odd[:], num[:], 1, None, ALU.bitwise_and))
                nc.vector.tensor_tensor(t0[:], num[:], left[:], ALU.subtract)
                nc.vector.scalar_tensor_tensor(every[:], num[:], T_DIL, valid[:], ALU.is_le, ALU.mult)
                nc.vector.tensor_tensor(t1[:], num[:], odd[:], ALU.add)
                link(nc.vector.tensor_scalar(none[:], valid[:], -NONE, NONE, ALU.mult, ALU.add))
                link(nc.vector.scalar_tensor_tensor(last[:], odd[:], NONE, t0[:], ALU.mult, ALU.add))
                nc.vector.scalar_tensor_tensor(half[:], t1[:], 0.5, left[:], ALU.mult, ALU.subtract)
                link(nc.vector.tensor_tensor(last[:], last[:], none[:], ALU.add))
                nc.vector.scalar_tensor_tensor(last[:], every[:], -3 * NONE, last[:], ALU.mult, ALU.add)
                link(nc.vector.tensor_tensor(half[:], half[:], none[:], ALU.add))
                nc.vector.tensor_tensor(q1[:], rk[:], spread(half[:], P), ALU.is_equal)
                link(nc.vector.tensor_tensor(q2[:], rk[:], spread(last[:], P), ALU.is_ge))
                link(nc.vector.tensor_tensor(q1[:], q1[:], q2[:], ALU.max))
                link(nc.vector.tensor_tensor(rm[:], q1[:], vb[:], ALU.mult))

            def turn_rows(link, new):
                link(nc.vector.transpose(swapped[:].rearrange(flat), rm[:].rearrange(flat)))
                for top in range(0, P, 32):
                    for under in range(top, P, 32):
                        ins = nc.vector.tensor_copy(turned[under:under + 32, :, top:top + 32],
                                                    swapped[top:top + 32, :, under:under + 32])
                link(ins)
                link(nc.vector.tensor_tensor(new[:], a2[:], turned[:], ALU.is_gt))

            def look(link, old, new):
                link(nc.vector.scalar_tensor_tensor(q1[:].rearrange(flat), old[:].rearrange(flat), 1.0,
                                                    new[:].rearrange(flat), ALU.mult, ALU.not_equal,
                                                    accum_out=spot[:, 0:1]))
                link(nc.vector.transpose(spot_t[:], spot[:]))
                link(nc.vector.tensor_reduce(spot_max[:], spot_t[:], AX, ALU.max))
                for quad in range(4):
                    ins = nc.vector.tensor_copy(spots[:, quad:quad + 1], spot_max[32 * quad:32 * quad + 1, :])
                link(ins)
                nc.vector.tensor_reduce(flag[:], spots[:], AX, ALU.max)
                dve.drain()
                return dve.value_load(flag[0:1, 0:1], min_val=0, max_val=P * B)

            def settle(depth):
                def link(ins):
                    dve.drain()
                old, new = vbs[depth % 2], vbs[(depth + 1) % 2]
                if depth < ROUNDS:
                    full_round(link, new)
                    turn_rows(link, old)
                    changed = look(link, new, old)
                    with dve.If(changed > 0):
                        settle(depth + 1)
                else:
                    with dve.Fori(0, P):
                        full_round(link, new)
                        turn_rows(link, new)

            with dve.Fori(0, NB) as j:
                with dve.Fori(0, B // 2) as pair:
                    b = pair * 2
                    count = (j * B + b) * ROW_STEPS + HEAD
                    done = 0

                    def step(ins):
                        nonlocal done
                        ins.then_inc(row_step, 1)
                        done += 1
                        dve.wait_ge(row_step, count + done - 1)

                    for i in range(2):
                        dve.wait_ge(bits_ready, j * B + b + i + 1)
                        words = col_bits[:, b + i, j, :].rearrange("p (k w) -> p k w", w=WB).unsqueeze(2)
                        step(nc.vector.tensor_tensor(gone[i][:].rearrange("p (k o w) -> p k o w", o=WORD, w=WB),
                                                     words.broadcast_to([P, NB, WORD, WB]),
                                                     c["bits"][:].unsqueeze(1).broadcast_to([P, NB, WORD, WB]),
                                                     ALU.bitwise_and))
                    for i in range(2):
                        dve.wait_ge(sign_ready, HEAD + j * B + b + i + 1)
                        step(nc.vector.tensor_tensor(v[:, b + i, :], sign[:, b + i, :], gone[i][:], ALU.is_gt))
                    size = P // 2
                    for i in range(2):
                        v_chunks = v[:, b + i, :].rearrange("p (k m) -> p k m", m=P)
                        step(nc.vector.tensor_tensor(halved[i][:], v_chunks[:, :, 0:size], v_chunks[:, :, size:P], ALU.add))
                    for size in (P // 4, P // 8):
                        for i in range(2):
                            step(nc.vector.tensor_tensor(halved[i][:, :, 0:size], halved[i][:, :, 0:size],
                                                         halved[i][:, :, size:2 * size], ALU.add))
                    for i in range(2):
                        step(nc.vector.tensor_reduce(chunk[:, b + i, :], halved[i][:, :, 0:size], AX, ALU.add))
                    assert done == 2 * ROW_STEPS
                dve.wait_ge(row_step, HEAD + (j + 1) * B * ROW_STEPS)

                link = Chain(dve, joint_step, j * JOINT_STEPS)
                link(nc.vector.tensor_tensor(chunk_left[:], chunk[:], repeat(below[:, j, :], B), ALU.mult))
                nc.vector.tensor_reduce(t0[:], chunk[:], AX, ALU.add)
                link(nc.vector.tensor_reduce(left[:], chunk_left[:], AX, ALU.add))
                nc.vector.tensor_tensor(outside[:], t0[:], chunk[:, :, j], ALU.subtract)
                nc.vector.tensor_scalar(masked[:], c["mask"][:, :, j], 0.0, None, ALU.not_equal)
                link(nc.vector.tensor_tensor(a2[:], v[:, :, bass.ds(j * P, P)], repeat(upper2[:], B), ALU.mult))
                link(nc.vector.tensor_scalar(vbs[0][:], v[:, :, bass.ds(j * P, P)], 1.0, None, ALU.mult))
                full_round(link, vbs[0])
                turn_rows(link, vbs[1])
                assert link.n == JOINT_STEPS
                def loose(ins):
                    dve.drain()
                changed = look(loose, vbs[0], vbs[1])
                with dve.If(changed > 0):
                    settle(0)
                nc.vector.tensor_tensor(vbs[0][:], a2[:], turned[:], ALU.is_gt)
                dve.drain()

                nc.vector.tensor_scalar(v[:, :, bass.ds(j * P, P)], vbs[0][:], 1.0, None, ALU.mult)
                nc.vector.scalar_tensor_tensor(half[:], every[:], NONE, half[:], ALU.mult, ALU.add)
                nc.vector.scalar_tensor_tensor(last[:], every[:], 4 * NONE, last[:], ALU.mult, ALU.add)
                nc.vector.tensor_scalar(t0[:], left[:], -1.0, 0.5, ALU.mult, ALU.add)
                dve.drain()
                nc.vector.tensor_tensor(bias[:, 0, :], t0[:], half[:], ALU.subtract)
                nc.vector.tensor_tensor(bias[:, 1, :], t0[:], last[:], ALU.subtract)
                nc.vector.tensor_scalar(own[:, 4, :, j], every[:], float(2 ** WORD - 1), None, ALU.mult)
                with dve.Fori(0, B // RANKS) as part:
                    b = part * RANKS
                    for i in range(RANKS):
                        dve.wait_ge(signs_ready, HEAD + (j * B + b + i - RANKS + 1) * 2)
                        nc.vector.tensor_tensor_scan(rank[i], v[:, b + i, :], v[:, b + i, :], 0.0,
                                                     ALU.add, ALU.max).then_inc(rank_ready, 1)

                for half_of in range(2):
                    b0 = half_of * H
                    these = slice(b0, b0 + H)
                    link = Chain(dve, find_step, (j * 2 + half_of) * FIND_STEPS)
                    dve.wait_ge(signs_ready, HEAD + (j * B + b0 + H) * 2)
                    nc.vector.tensor_scalar(pos[:, :, these], signs[:, :, these], -0.5, N / 2, ALU.mult, ALU.add)
                    link(nc.vector.tensor_scalar(pos_i[:, :, these], signs[:, :, these], -0.5, N / 2, ALU.mult, ALU.add))
                    nc.vector.tensor_scalar(high[:, :, these], pos_i[:, :, these], 7, 3,
                                            ALU.logical_shift_right, ALU.logical_shift_left)
                    nc.vector.tensor_scalar(low[:, :, these], pos_i[:, :, these], WB - 1, None, ALU.bitwise_and)
                    link(nc.vector.tensor_scalar(bit[:, :, these], pos_i[:, :, these], 3, WORD - 1,
                                                 ALU.logical_shift_right, ALU.bitwise_and))
                    link(nc.vector.tensor_tensor(bit[:, :, these], one[:, :, these], bit[:, :, these],
                                                 ALU.logical_shift_left))
                    for t in range(2):
                        nc.vector.tensor_tensor(own[:, 2 * t, these, j], high[:, t, these], low[:, t, these], ALU.add)
                        nc.vector.tensor_copy(own[:, 2 * t + 1, these, j], bit[:, t, these])
                    assert link.n == FIND_STEPS

                    with dve.Fori(0, H // 2) as pair:
                        b = pair * 2 + b0
                        for i in range(2):
                            dve.wait_ge(pack_ready, HEAD + j * B + b + i - 1)
                            for t in range(2):
                                nc.vector.tensor_scalar(hot[i][:, t, :], index[:], pos[:, t, bass.ds(b + i, 1)],
                                                        None, ALU.is_equal)
                            nc.vector.tensor_scalar(hot[i][:, 2, :], v[:, b + i, :], every[:, bass.ds(b + i, 1)],
                                                    None, ALU.mult).then_inc(hot_ready, 1)


def weights(nc, c, tag, w, prev):
    with ExitStack() as ctx:
        def sb(name, shape, dt=F32):
            return ctx.enter_context(nc.sbuf_tensor(name + tag, shape, dt))

        sem = fresh(nc, ctx, tag)

        raw = sb("raw", [P, 3, P])
        bias_row = sb("bias_row", [1, P])
        final_row = sb("final_row", [1, P])
        gamma = sb("gamma", [P, 1])
        beta_in = sb("beta_in", [P, 1])
        moments = sb("moments", [P, 2])
        square = sb("square", [P, 1])
        var = sb("var", [P, 1])
        dev = sb("dev", [P, 1])
        alpha = sb("alpha", [P, 1])
        beta = sb("beta", [P, 1])
        beta_wide = sb("beta_wide", [P, P])
        sums_ps = ctx.enter_context(nc.psum_tensor("sums_ps" + tag, [P, 512], F32))
        moved_ps = [ctx.enter_context(nc.psum_tensor(f"moved_ps{i}" + tag, [P, 512], F32)) for i in range(4)]
        loaded = sem("loaded")
        turned = sem("turned")
        summed = sem("summed")
        step = sem("step")
        var_ready = sem("var_ready")
        dev_ready = sem("dev_ready")
        wide_ready = sem("wide_ready")
        moved = sem("moved")
        block = ctx.enter_context(nc.Block())
        parts = [t for t in ("Wr", "Wx", "Wl") if t in w]
        place = {"Wr": 0, "Wx": 1, "Wl": 2}
        loads = len(parts) + ("b" in w) + ("bl" in w) + 2 * (prev is not None)

        @block.sync
        def _(sp):
            for t in parts:
                sp.dma_start(raw[:, place[t], :], w[t]).then_inc(loaded, 16)
            if "b" in w:
                sp.dma_start(bias_row[:], w["b"].unsqueeze(0)).then_inc(loaded, 16)
            if "bl" in w:
                sp.dma_start(final_row[:], w["bl"].unsqueeze(0)).then_inc(loaded, 16)
            if prev is not None:
                sp.dma_start(gamma[:], w["g"].unsqueeze(1)).then_inc(loaded, 16)
                sp.dma_start(beta_in[:], w["be"].unsqueeze(1)).then_inc(loaded, 16)

        @block.tensor
        def _(pe):
            pe.wait_ge(loaded, 16 * loads)
            if w.get("turn"):
                for i, t in enumerate(parts):
                    nc.tensor.transpose(moved_ps[i][:, 0:P], raw[:, place[t], :], c["ident"][:]).then_inc(turned, 1)
            if "b" in w:
                nc.tensor.matmul(moved_ps[3][:, 0:P], c["ones"][0:1, :], bias_row[:],
                                 start=True, stop=prev is None).then_inc(moved, 1)
            if "bl" in w:
                nc.tensor.matmul(sums_ps[:, 256:256 + P], c["ones"][0:1, :], final_row[:],
                                 start=True, stop=True).then_inc(moved, 1)
            if prev is not None:
                for s in range(2):
                    for q in range(Q):
                        ins = nc.tensor.matmul(sums_ps[:, s:s + 1], prev[s][:, q, :], c["ones"][:, 0:1],
                                               start=(q == 0), stop=(q == Q - 1))
                ins.then_inc(summed, 1)
                pe.wait_ge(wide_ready, 1)
                for t in parts:
                    if t == "Wx":
                        ins = nc.tensor.matmul(moved_ps[3][:, 0:P], beta_wide[:], raw[:, 1, :], start=False, stop=True)
                    else:
                        ins = nc.tensor.matmul(moved_ps[place[t]][:, 0:P], beta_wide[:], raw[:, place[t], :],
                                               start=True, stop=True)
                    ins.then_inc(moved, 1)

        @block.scalar
        def _(act):
            if prev is not None:
                act.wait_ge(var_ready, 1)
                nc.scalar.activation(dev[:], var[:], ACT.Sqrt, bias=c["bn_eps"][:]).then_inc(dev_ready, 1)

        @block.vector
        def _(dve):
            link = Chain(dve, step)
            if w.get("turn"):
                nc.vector.memset(w["row_Wl"], 0.0)
            dve.wait_ge(loaded, 16 * loads)
            if w.get("turn"):
                dve.wait_ge(turned, len(parts))
                for i, t in enumerate(parts):
                    nc.vector.tensor_copy(w["to_" + t], moved_ps[i][:, 0:P])
            elif prev is None:
                for t in parts:
                    nc.vector.tensor_copy(w["to_" + t], raw[:, place[t], :])
            else:
                dve.wait_ge(summed, 1)
                link(nc.vector.tensor_scalar(moments[:], sums_ps[:, 0:2], 1.0 / (B * N), None, ALU.mult))
                link(nc.vector.tensor_tensor(square[:], moments[:, 0:1], moments[:, 0:1], ALU.mult))
                link(nc.vector.tensor_tensor(var[:], moments[:, 1:2], square[:], ALU.subtract))
                nc.vector.tensor_scalar(var[:], var[:], 0.0, None, ALU.max).then_inc(var_ready, 1)
                dve.wait_ge(dev_ready, 1)
                link(nc.vector.reciprocal(alpha[:], dev[:]))
                link(nc.vector.tensor_tensor(alpha[:], alpha[:], gamma[:], ALU.mult))
                link(nc.vector.tensor_tensor(beta[:], moments[:, 0:1], alpha[:], ALU.mult))
                link(nc.vector.tensor_tensor(beta[:], beta_in[:], beta[:], ALU.subtract))
                nc.vector.tensor_scalar(beta_wide[:], c["ones"][:], beta[:], None, ALU.mult).then_inc(wide_ready, 1)
                for t in parts:
                    nc.vector.tensor_scalar(w["to_" + t], raw[:, place[t], :], alpha[:], None, ALU.mult)
                dve.wait_ge(moved, len(parts) + ("b" in w) + ("bl" in w))
                if "Wr" in w:
                    nc.vector.tensor_copy(w["row_Wr"], moved_ps[0][:, 0:P])
                nc.vector.tensor_tensor(w["row_Wl"], w["row_Wl"], moved_ps[2][:, 0:P], ALU.add)
            if "b" in w:
                dve.wait_ge(moved, 1)
                nc.vector.tensor_copy(w["row_b"], moved_ps[3][:, 0:P])
            if "bl" in w:
                nc.vector.tensor_copy(w["row_bl"], sums_ps[:, 256:256 + P])


def layer(nc, c, L, adj, turned_adj, r_in, r_out, k):
    GNN, MASK, DEEP = L == 0, L == 1, L >= 2
    ZW = 2 * P if DEEP else P
    W = Q * P
    with ExitStack() as ctx:
        def sb(name, shape, dt=F32):
            return ctx.enter_context(nc.sbuf_tensor(name + f"_L{L}", shape, dt))

        def ps(name, shape, dt=F32):
            return ctx.enter_context(nc.psum_tensor(name + f"_L{L}", shape, dt))

        sem = fresh(nc, ctx, f"_L{L}")

        HALF = NB // 2
        STAGES = 1 if MASK else 2
        stage = [sb(f"stage{i}", [P, NB, P]) for i in range(STAGES)]
        piece = [sb(f"piece{i}", [P, HALF, W]) for i in range(4)]
        r_t = [sb(f"r_t{i}", [P, W]) for i in range(2)]
        agg = [sb(f"agg{i}", [P, W]) for i in range(2)]
        z = [sb(f"z{i}", [P, Q, P]) for i in range(2)]
        r = [sb(f"r{i}", [P, Q, P]) for i in range(2)]
        waste = [sb(f"waste{i}", [P, P], BF16) for i in range(Q)]
        ss = sb("ss", [P, Q])
        root = sb("root", [P, Q])
        inv = sb("inv", [P, Q])
        if GNN:
            x_in = [sb(f"x_in{i}", [P, Q, P]) for i in range(2)]
            x2 = [sb(f"x2{i}", [P, Q, P]) for i in range(2)]
            mean = sb("mean", [P, Q])
        else:
            r_sq = sb("r_sq", [P, Q, P])
        if MASK:
            nat = [sb(f"nat{i}", [P, N]) for i in range(2 * Q)]
            word1 = sb("word1", [P, WORDS])
            word2 = sb("word2", [P, WORDS])
            words = sb("words", [P, WORDS], U16)
            words2 = sb("words2", [P, WORDS], U16)
            gone = sb("gone", [P, N], U16)
            row_sum = sb("row_sum", [P, Q])
            row_max = sb("row_max", [P, Q])
        if DEEP:
            extra = [sb(f"extra{i}", [P, Q, P]) for i in range(2)]

        turn_ps = ps("turn_ps", [P, W])
        agg_ps = [ps(f"agg_ps{i}", [P, W]) for i in range(1 if MASK else 2)]
        a_ps = ps("a_ps", [P, Q, P])
        z_ps = ps("z_ps", [P, Q, ZW])
        if MASK:
            piece_ps = [ps(f"piece_ps{i}", [P, W]) for i in range(4)]

        stage_full = [sem(f"stage_full{i}") for i in range(2)]
        piece_full = [sem(f"piece_full{i}") for i in range(4)]
        piece_stored = [sem(f"piece_stored{i}") for i in range(4)]
        nat_full = [sem(f"nat_full{i}") for i in range(2 * Q)]
        x_full = [sem(f"x_full{i}") for i in range(2)]
        r_stored = [sem(f"r_stored{i}") for i in range(2)]
        x2_stored = [sem(f"x2_stored{i}") for i in range(2)]
        half_used = sem("half_used")
        turn_ready = sem("turn_ready")
        rt_ready = sem("rt_ready")
        aggs_ready = sem("aggs_ready")
        a_ready = sem("a_ready")
        z_ready = sem("z_ready")
        mask_ready = sem("mask_ready")
        mask_step = sem("mask_step")
        piece_turned = sem("piece_turned")
        piece_moved = sem("piece_moved")
        dve_step = sem("dve_step")
        end_step = sem("end_step")
        ss_ready = sem("ss_ready")
        root_ready = sem("root_ready")
        inv_ready = sem("inv_ready")
        r_ready = sem("r_ready")
        extra_ready = sem("extra_ready")
        pool_step = sem("pool_step")
        added = sem("added")
        once = sem("once")
        block = ctx.enter_context(nc.Block())
        UNITS = 2 * G
        BODIES = B // 2
        adj_cols = adj.rearrange("b (k p) (g c) -> b g p k c", p=P, c=W)
        adj_rows = adj.rearrange("b (k p) n -> b k p n", p=P)

        def all_units(engine, unit, tail):
            for n in range(UNITS):
                unit(0, n, True)
            with engine.Fori(1, BODIES) as body:
                for n in range(UNITS):
                    unit(body, n, False)
            tail()

        def back(body, n, by):
            return (body, n - by) if n >= by else (body - 1, n - by + UNITS)

        LAST = BODIES - 1

        @block.sync
        def _(sp):
            with sp.Fori(0, BODIES) as body:
                for n in range(UNITS):
                    u = body * UNITS + n
                    b, g = body * 2 + n // G, n % G
                    if MASK:
                        for q in range(Q):
                            if q == 0:
                                sp.wait_ge(piece_turned, NB * HEAD + (u - 1) * NB)
                            i = (n % 2) * Q + q
                            sp.dma_start(nat[i][:], adj_rows[b, g * Q + q]).then_inc(nat_full[i], 16)
                    if g == 0:
                        sp.wait_ge(half_used, 2 * (HEAD + u - (STAGES - 1) * G))
                        sp.dma_start(stage[n // G % STAGES][:], r_in[b]).then_inc(stage_full[n // G % STAGES], 16)
                    if GNN:
                        sp.wait_ge(z_ready, HEAD + u - 1)
                        sp.dma_start(x_in[n % 2][:], k["x"].rearrange("b (g q p) d -> b g p q d", p=P, q=Q)[b, g]
                                     ).then_inc(x_full[n % 2], 16)
                    if not MASK:
                        for h in range(2):
                            i = 2 * (n % 2) + h
                            sp.wait_ge(half_used, 2 * HEAD + 2 * (u - 2) + h + 1)
                            src = (adj_cols[b, g, :, h * HALF:(h + 1) * HALF, :] if GNN
                                   else turned_adj[b, g, :, h * HALF:(h + 1) * HALF, :])
                            sp.dma_start(piece[i][:], src).then_inc(piece_full[i], 16)

        @block.tensor
        def _(pe):
            pe.sem_inc(half_used, 2 * HEAD)
            if MASK:
                pe.sem_inc(piece_turned, NB * HEAD)

            def post_a(body, n):
                u = body * UNITS + n
                pe.wait_ge(aggs_ready, u + 1)
                pe.wait_ge(z_ready, HEAD + u)
                for q in range(Q):
                    ins = nc.tensor.matmul(a_ps[:, q, :], agg[n % 2][:, q * P:(q + 1) * P], k["wA"][:],
                                           start=True, stop=True)
                ins.then_inc(a_ready, 1)

            def unit(body, n, first):
                    u = body * UNITS + n
                    g, s = n % G, n // G % STAGES
                    before = None if first and n == 0 else back(body, n, 1)

                    def sum_block(m):
                        i = 2 * (n % 2) + m // HALF
                        if m % HALF == 0 and not MASK:
                            pe.wait_ge(piece_full[i], (body * (UNITS // 2) + n // 2 + 1) * 16)
                        if MASK:
                            pe.wait_ge(piece_moved, HEAD + u * NB + m + 1)
                        ins = nc.tensor.matmul(agg_ps[n % len(agg_ps)][:], stage[s][:, m, :],
                                               piece[i][:, m % HALF, :], start=(m == 0), stop=(m == NB - 1))
                        if m % HALF == HALF - 1:
                            ins.then_inc(half_used, 1)

                    if MASK and before:
                        post_a(*before)
                    if g == 0:
                        pe.wait_ge(stage_full[s], (body * (2 // STAGES) + (n // G) // STAGES + 1) * 16)
                    for q in range(Q):
                        ins = nc.tensor.transpose(turn_ps[:, q * P:(q + 1) * P], stage[s][:, g * Q + q, :], c["ident"][:])
                    ins.then_inc(turn_ready, 1)
                    if MASK:
                        pe.wait_ge(mask_ready, (u + 1) * Q)
                    for m in range(NB + 2):
                        if MASK and m < NB:
                            pe.wait_ge(piece_moved, HEAD + u * NB + m - 3)
                            for q in range(Q):
                                ins = nc.tensor.transpose(piece_ps[m % 4][:, q * P:(q + 1) * P],
                                                          nat[(n % 2) * Q + q][:, m * P:(m + 1) * P], c["ident"][:])
                            ins.then_inc(piece_turned, 1)
                        if m >= 2:
                            sum_block(m - 2)
                        if m == 5 and not MASK and before:
                            post_a(*before)
                        if m == 13:
                            pe.wait_ge(rt_ready, u + 1)
                            pe.wait_ge(z_ready, HEAD + u)
                            for q in range(Q):
                                nc.tensor.matmul(z_ps[:, q, :], r_t[n % 2][:, q * P:(q + 1) * P], k["wZ"][:, 0:ZW],
                                                 start=True, stop=True)

            all_units(pe, unit, lambda: post_a(LAST, UNITS - 1))

        @block.scalar
        def _(act):
            act.sem_inc(r_ready, HEAD)
            for i in range(2):
                act.sem_inc(r_stored[i], 1)
                act.sem_inc(x2_stored[i], 1)
            if MASK:
                act.sem_inc(piece_moved, HEAD)
                for i in range(4):
                    act.sem_inc(piece_stored[i], 1)

            def post_squares(body, n):
                u, i = body * UNITS + n, n % 2
                b, g = body * 2 + n // G, n % G
                act.wait_ge(z_ready, HEAD + u + 1)
                if GNN:
                    act.dma_start(k["x2"][b, :, g * Q:(g + 1) * Q, :], x2[i][:]).then_inc(x2_stored[i], 16)
                act.wait_ge(r_ready, HEAD + u)
                for q in range(Q):
                    ins = nc.scalar.activation(waste[q][:], z[i][:, q, :], ACT.Square, accum_out=ss[:, q:q + 1])
                ins.then_inc(ss_ready, 1)
                act.wait_ge(ss_ready, u + 1)
                if GNN:
                    ins = nc.scalar.activation(root[:], ss[:], ACT.Sqrt, scale=1.0 / P, bias=c["ln_eps"][:])
                else:
                    ins = nc.scalar.activation(root[:], ss[:], ACT.Sqrt)
                ins.then_inc(root_ready, 1)

            def post_scale(body, n):
                u, i = body * UNITS + n, n % 2
                b, g = body * 2 + n // G, n % G
                act.wait_ge(inv_ready, u + 1)
                act.wait_ge(r_stored[i], (body * (UNITS // 2) + n // 2) * 16 + 1)
                if not GNN:
                    act.wait_ge(added, HEAD + u - 1)
                for q in range(Q):
                    ins = nc.scalar.activation(r[i][:, q, :], z[i][:, q, :], ACT.Relu, scale=inv[:, q:q + 1])
                ins.then_inc(r_ready, 1)
                act.wait_ge(r_ready, HEAD + u + 1)
                act.dma_start(r_out[b, :, g * Q:(g + 1) * Q, :], r[i][:]).then_inc(r_stored[i], 16)

            def unit(body, n, first):
                u = body * UNITS + n
                b, g = body * 2 + n // G, n % G
                before = None if first and n == 0 else back(body, n, 1)
                act.wait_ge(turn_ready, u + 1)
                nc.scalar.copy(r_t[n % 2][:], turn_ps[:]).then_inc(rt_ready, 1)
                if MASK:
                    for m in range(NB):
                        i = 2 * (n % 2) + m // HALF
                        if m % HALF == 0:
                            act.wait_ge(piece_stored[i], (body * (UNITS // 2) + n // 2) * 16 + 1)
                        act.wait_ge(piece_turned, NB * HEAD + u * NB + m + 1)
                        nc.scalar.copy(piece[i][:, m % HALF, :], piece_ps[m % 4][:]).then_inc(piece_moved, 1)
                        if m % HALF == HALF - 1:
                            act.wait_ge(piece_moved, HEAD + u * NB + m + 1)
                            h = m // HALF
                            act.dma_start(turned_adj[b, g, :, h * HALF:(h + 1) * HALF, :],
                                          piece[i][:]).then_inc(piece_stored[i], 16)
                        if m == 6 and before:
                            post_squares(*before)
                        if m == 12 and before:
                            post_scale(*before)
                elif before:
                    post_squares(*before)
                    post_scale(*before)
                act.wait_ge(half_used, 2 * (HEAD + u + 1))
                nc.scalar.copy(agg[n % 2][:], agg_ps[n % len(agg_ps)][:]).then_inc(aggs_ready, 1)

            def tail():
                post_squares(LAST, UNITS - 1)
                post_scale(LAST, UNITS - 1)

            all_units(act, unit, tail)
            for i in range(2):
                act.wait_ge(r_stored[i], BODIES * (UNITS // 2) * 16 + 1)
                if GNN:
                    act.wait_ge(x2_stored[i], BODIES * (UNITS // 2) * 16 + 1)
            if MASK:
                for i in range(4):
                    act.wait_ge(piece_stored[i], BODIES * (UNITS // 2) * 16 + 1)

        @block.vector
        def _(dve):
            dve.sem_inc(z_ready, HEAD)
            if GNN:
                nc.vector.reciprocal(k["rdeg"][:], k["deg"][:]).then_inc(once, 1)
                dve.wait_ge(once, 1)

            STEPS = 5 if GNN else 2

            def post_z(body, n):
                u, i = body * UNITS + n, n % 2
                b, g = body * 2 + n // G, n % G
                link = Chain(dve, dve_step, u * STEPS)
                dve.wait_ge(a_ready, u + 1)
                dve.wait_ge(r_ready, HEAD + u - 1)
                if DEEP:
                    y = k["y"][:, b, g * Q:(g + 1) * Q, :]
                    if L == 2:
                        nc.vector.tensor_scalar(y, z_ps[:, :, P:2 * P], 1.0, None, ALU.mult)
                    else:
                        nc.vector.tensor_tensor(y, y, z_ps[:, :, P:2 * P], ALU.add)
                link(nc.vector.tensor_tensor(z[i][:], a_ps[:], spread(k["rdeg"][:, b, g * Q:(g + 1) * Q], P), ALU.mult))
                link(nc.vector.tensor_tensor(z[i][:], z[i][:], z_ps[:, :, 0:P], ALU.add))
                if GNN:
                    link(nc.vector.tensor_tensor(z[i][:], z[i][:], repeat(k["row_b"][:], Q), ALU.add))
                    dve.wait_ge(x_full[i], (body * (UNITS // 2) + n // 2 + 1) * 16)
                    dve.wait_ge(x2_stored[i], (body * (UNITS // 2) + n // 2) * 16 + 1)
                    link(nc.vector.scalar_tensor_tensor(x2[i][:], z[i][:], 0.0, x_in[i][:], ALU.max, ALU.add))
                    link(nc.vector.tensor_reduce(mean[:], x2[i][:], AX, ALU.add))
                    nc.vector.tensor_scalar(mean[:], mean[:], 1.0 / P, None, ALU.mult).then_inc(end_step, 1)
                    dve.wait_ge(end_step, u + 1)
                    nc.vector.tensor_tensor(z[i][:], x2[i][:], spread(mean[:], P), ALU.subtract).then_inc(z_ready, 1)
                else:
                    if DEEP:
                        dve.wait_ge(extra_ready, u + 1)
                        nc.vector.tensor_tensor(z[i][:], z[i][:], extra[i][:], ALU.add).then_inc(z_ready, 1)
                    else:
                        nc.vector.tensor_tensor(z[i][:], z[i][:], repeat(k["row_b"][:], Q), ALU.add).then_inc(z_ready, 1)

            def post_inv(body, n):
                u = body * UNITS + n
                b, g = body * 2 + n // G, n % G
                dve.wait_ge(root_ready, u + 1)
                if not GNN:
                    nc.vector.tensor_scalar(root[:], root[:], NORM_EPS, None, ALU.max).then_inc(end_step, 1)
                    dve.wait_ge(end_step, 2 * u + 1)
                    nc.vector.reciprocal(inv[:], root[:]).then_inc(end_step, 1)
                    dve.wait_ge(end_step, 2 * u + 2)
                    nc.vector.tensor_tensor(inv[:], inv[:], c["mask"][:, b, g * Q:(g + 1) * Q], ALU.mult).then_inc(inv_ready, 1)
                else:
                    nc.vector.reciprocal(inv[:], root[:]).then_inc(inv_ready, 1)

            LAG = 2 if MASK else 1

            def unit(body, n, first):
                    u = body * UNITS + n
                    b, g = body * 2 + n // G, n % G
                    before = None if first and n < LAG else back(body, n, LAG)
                    if MASK:
                        PER = 5 * Q + 2
                        link = Chain(dve, mask_step, u * PER)
                        for q in range(Q):
                            i, m = (n % 2) * Q + q, g * Q + q

                            def own(t):
                                return k["own"][:, t, b, m:m + 1]
                            nc.vector.tensor_scalar(word1[:], c["word_index"][:], own(0), own(1), ALU.is_equal, ALU.mult)
                            link(nc.vector.tensor_scalar(word2[:], c["word_index"][:], own(2), own(3), ALU.is_equal, ALU.mult))
                            link(nc.vector.scalar_tensor_tensor(words[:], word1[:], own(4), word2[:], ALU.add, ALU.add))
                            link(nc.vector.tensor_tensor(words2[:], words[:], k["col_bits"][:, b, m, :], ALU.bitwise_or))
                            link(nc.vector.tensor_tensor(
                                gone[:].rearrange("p (k o w) -> p k o w", o=WORD, w=WB),
                                words2[:].rearrange("p (k w) -> p k w", w=WB).unsqueeze(2).broadcast_to([P, NB, WORD, WB]),
                                c["bits"][:].unsqueeze(1).broadcast_to([P, NB, WORD, WB]), ALU.bitwise_and))
                            dve.wait_ge(nat_full[i], (body * (UNITS // 2) + n // 2 + 1) * 16)
                            link(nc.vector.scalar_tensor_tensor(nat[i][:], gone[:], 0.0, nat[i][:], ALU.is_equal, ALU.mult,
                                                                accum_out=row_sum[:, q:q + 1]))
                            nc.vector.sem_inc(mask_ready, 1)
                            if q == 1 and before:
                                post_z(*before)
                        link(nc.vector.tensor_scalar(row_max[:], row_sum[:], 1.0, None, ALU.max))
                        rdeg = k["rdeg"][:, b, g * Q:(g + 1) * Q]
                        link(nc.vector.reciprocal(rdeg, row_max[:]))
                        nc.vector.tensor_tensor(k["ratio"][:, b, g * Q:(g + 1) * Q], row_sum[:], rdeg, ALU.mult)
                        assert link.n == PER
                    elif before:
                        post_z(*before)
                    if before:
                        post_inv(*before)

            def tail():
                for by in reversed(range(LAG)):
                    post_z(LAST, UNITS - 1 - by)
                    post_inv(LAST, UNITS - 1 - by)

            all_units(dve, unit, tail)

        if not GNN:
            @block.gpsimd
            def _(pool):
                pool.sem_inc(added, HEAD)
                link = Chain(pool, once)
                for s in k["sums"]:
                    link(nc.gpsimd.memset(s[:], 0.0))
                with pool.Fori(0, BODIES) as body:
                    for n in range(UNITS):
                        u = body * UNITS + n
                        i = n % 2
                        b, g = body * 2 + n // G, n % G
                        link = Chain(pool, pool_step, u * (3 if DEEP else 2))
                        if DEEP:
                            pool.wait_ge(z_ready, HEAD + u - 1)
                            link(nc.gpsimd.tensor_tensor(extra[i][:], spread(k["ratio"][:, b, g * Q:(g + 1) * Q], P),
                                                         repeat(k["row_Wr"][:], Q), ALU.mult))
                            nc.gpsimd.tensor_tensor(extra[i][:], extra[i][:], repeat(k["row_b"][:], Q),
                                                    ALU.add).then_inc(extra_ready, 1)
                        pool.wait_ge(r_ready, HEAD + u + 1)
                        link(nc.gpsimd.tensor_tensor(r_sq[:], r[i][:], r[i][:], ALU.mult))
                        nc.gpsimd.tensor_tensor(k["sums"][0][:], k["sums"][0][:], r[i][:], ALU.add)
                        link(nc.gpsimd.tensor_tensor(k["sums"][1][:], k["sums"][1][:], r_sq[:], ALU.add))
                        pool.sem_inc(added, 1)


def finish(nc, c, r_in, k, out):
    with ExitStack() as ctx:
        def sb(name, shape, dt=F32):
            return ctx.enter_context(nc.sbuf_tensor(name + "_fin", shape, dt))

        sem = fresh(nc, ctx, "_fin")

        r = [sb(f"r{i}", [P, Q, P]) for i in range(2)]
        x2 = [sb(f"x2{i}", [P, Q, P]) for i in range(2)]
        r_t = [sb(f"r_t{i}", [P, Q, P]) for i in range(2)]
        rest = [sb(f"rest{i}", [P, Q, P]) for i in range(2)]
        last = [sb(f"last{i}", [P, Q, P]) for i in range(2)]
        mask2 = sb("mask2", [P, B, NB])
        turn_ps = [ctx.enter_context(nc.psum_tensor(f"turn_ps{i}" + "_fin", [P, Q, P], F32)) for i in range(2)]
        y_ps = [ctx.enter_context(nc.psum_tensor(f"y_ps{i}" + "_fin", [P, Q, P], F32)) for i in range(2)]
        loaded = [sem(f"loaded{i}") for i in range(2)]
        stored = [sem(f"stored{i}") for i in range(2)]
        turn_ready = sem("turn_ready")
        rt_ready = sem("rt_ready")
        y_ready = sem("y_ready")
        rest_ready = sem("rest_ready")
        pool_step = sem("pool_step")
        dve_step = sem("dve_step")
        out_ready = sem("out_ready")
        mask_made = sem("mask_made")
        block = ctx.enter_context(nc.Block())
        nodes = out.rearrange("b (g q p) d -> b g p q d", p=P, q=Q)

        @block.sync
        def _(sp):
            with sp.Fori(0, B) as b:
                for g in range(G):
                    u, i = b * G + g, g % 2
                    sp.wait_ge(out_ready, HEAD + u - 1)
                    sp.dma_start(r[i][:], r_in[b, :, g * Q:(g + 1) * Q, :]).then_inc(loaded[i], 16)
                    sp.dma_start(x2[i][:], k["x2"][b, :, g * Q:(g + 1) * Q, :]).then_inc(loaded[i], 16)

        @block.tensor
        def _(pe):
            def turn(u, i, n):
                pe.wait_ge(loaded[i], n * 32)
                for q in range(Q):
                    ins = nc.tensor.transpose(turn_ps[i][:, q, :], r[i][:, q, :], c["ident"][:])
                ins.then_inc(turn_ready, 1)

            with pe.Fori(0, B) as b:
                for g in range(G):
                    u, i = b * G + g, g % 2
                    turn(u, i, b * 2 + g // 2 + 1)
                    pe.wait_ge(rt_ready, u + 1)
                    pe.wait_ge(out_ready, HEAD + u - 1)
                    for q in range(Q):
                        nc.tensor.matmul(y_ps[i][:, q, :], r_t[i][:, q, :], k["wY"][:], start=True, stop=False)
                        ins = nc.tensor.matmul(y_ps[i][:, q, :], c["ones"][0:1, :], k["row_Wl"][0:1, :],
                                               start=False, stop=True)
                    ins.then_inc(y_ready, 1)

        @block.scalar
        def _(act):
            for i in range(2):
                act.sem_inc(stored[i], 1)
            with act.Fori(0, B) as b:
                for g in range(G):
                    u, i = b * G + g, g % 2
                    act.wait_ge(turn_ready, u + 1)
                    nc.scalar.copy(r_t[i][:], turn_ps[i][:]).then_inc(rt_ready, 1)
                    act.wait_ge(out_ready, HEAD + u + 1)
                    act.dma_start(nodes[b, g], last[i][:]).then_inc(stored[i], 16)
            for i in range(2):
                act.wait_ge(stored[i], B * 2 * 16 + 1)

        @block.gpsimd
        def _(pool):
            nc.gpsimd.tensor_tensor(mask2[:], c["mask"][:], c["mask"][:], ALU.mult).then_inc(mask_made, 1)
            with pool.Fori(0, B) as b:
                for g in range(G):
                    u, i = b * G + g, g % 2
                    link = Chain(pool, pool_step, u * 2)
                    pool.wait_ge(out_ready, HEAD + u - 1)
                    link(nc.gpsimd.tensor_tensor(rest[i][:], spread(c["mask"][:, b, g * Q:(g + 1) * Q], P),
                                                 repeat(k["row_bl"][:], Q), ALU.mult))
                    pool.wait_ge(loaded[i], (b * 2 + g // 2 + 1) * 32)
                    link(nc.gpsimd.tensor_tensor(rest[i][:], rest[i][:], x2[i][:], ALU.add))
                    pool.sem_inc(rest_ready, 1)

        @block.vector
        def _(dve):
            dve.sem_inc(out_ready, HEAD)
            with dve.Fori(0, B) as b:
                for g in range(G):
                    u, i = b * G + g, g % 2
                    link = Chain(dve, dve_step, u * 2)
                    dve.wait_ge(rest_ready, u + 1)
                    dve.wait_ge(y_ready, u + 1)
                    dve.wait_ge(mask_made, 1)
                    dve.wait_ge(stored[i], (b * 2 + g // 2) * 16 + 1)
                    link(nc.vector.tensor_tensor(last[i][:], y_ps[i][:], k["y"][:, b, g * Q:(g + 1) * Q, :], ALU.add))
                    link(nc.vector.tensor_tensor(last[i][:], last[i][:], spread(mask2[:, b, g * Q:(g + 1) * Q], P),
                                                 ALU.mult))
                    nc.vector.tensor_tensor(last[i][:], last[i][:], rest[i][:], ALU.add).then_inc(out_ready, 1)


def build(nc, a, out):
    h = [nc.dram_tensor(f"r{i}", (B, P, NB, P), F32, kind="Internal").ap() for i in range(4)]
    x2 = nc.dram_tensor("x2_scratch", (B, P, NB, P), F32, kind="Internal").ap()
    turned = nc.dram_tensor("turned_adj", (B, G, P, NB, Q * P), F32, kind="Internal").ap()
    with ExitStack() as ctx:
        def sb(name, shape, dt=F32):
            return ctx.enter_context(nc.sbuf_tensor(name, shape, dt))

        c = constants(nc, ctx, a["nodemask"])
        k = {name: sb(name, [P, B, NB]) for name in ("deg", "rdeg", "ratio")}
        k["sums"] = [sb(f"sums{i}", [P, Q, P]) for i in range(2)]
        k["wA"], k["wZ"] = sb("wA", [P, P]), sb("wZ", [P, 2 * P])
        for name in ("row_Wr", "row_Wl", "row_b", "row_bl"):
            k[name] = sb(name, [P, P])
        k["x"], k["x2"] = a["x"], x2
        rows = {name: k[name][:] for name in ("row_Wr", "row_Wl", "row_b", "row_bl")}

        def sage(i, **more):
            return {"Wr": a[f"L1_gnn_Wr{i}"], "Wx": a[f"L1_gnn_Wx{i}"], "b": a[f"L1_gnn_b{i}"],
                    "to_Wr": k["wA"][:], "to_Wx": k["wZ"][:, 0:P], "to_Wl": k["wZ"][:, P:2 * P], **rows, **more}

        def normed(i):
            return {"g": a[f"L1_gnn_g{i}"], "be": a[f"L1_gnn_be{i}"], "Wl": a["L1_gnn_Wl"][(i - 1) * P:i * P, :]}

        with ExitStack() as early:
            k["col_bits"] = early.enter_context(nc.sbuf_tensor("col_bits", [P, B, NB, WORDS], U16))
            k["own"] = early.enter_context(nc.sbuf_tensor("own", [P, 5, B, NB], F32))
            norm(nc, c, a["x"], h[0])
            dilate(nc, c, a["adj"], k["col_bits"], k["deg"], k["own"])
            weights(nc, c, "_w0", {"Wx": a["L0_gnn_W"][:, 0:P], "Wr": a["L0_gnn_W"][:, P:2 * P], "b": a["L0_gnn_b"],
                            "turn": True, "to_Wr": k["wA"][:], "to_Wx": k["wZ"][:, 0:P], **rows}, None)
            layer(nc, c, 0, a["adj"], turned, h[0], h[1], k)
            weights(nc, c, "_w1", sage(1), None)
            layer(nc, c, 1, a["adj"], turned, h[1], h[2], k)
        k["y"] = sb("y", [P, B, NB, P])
        weights(nc, c, "_w2", sage(2, **normed(1)), k["sums"])
        layer(nc, c, 2, a["adj"], turned, h[2], h[3], k)
        weights(nc, c, "_w3", sage(3, **normed(2)), k["sums"])
        layer(nc, c, 3, a["adj"], turned, h[3], h[0], k)
        k["wY"] = k["wA"]
        weights(nc, c, "_w4", {**normed(3), "bl": a["L1_gnn_bl"], "to_Wl": k["wY"][:], **rows}, k["sums"])
        finish(nc, c, h[0], k, out)


NAMES = (["x", "adj", "nodemask", "L0_gnn_W", "L0_gnn_b"]
         + [f"L1_gnn_{t}{i}" for i in (1, 2, 3) for t in ("Wr", "Wx", "b", "g", "be")] + ["L1_gnn_Wl", "L1_gnn_bl"])


def kernel(**inputs):
    import numpy as _np
    import concourse.bacc as _bacc
    from concourse import mybir as _mybir
    from concourse.bass_utils import run_bass_kernel_spmd as _run

    nc = _bacc.Bacc("TRN2", target_bir_lowering=False, num_devices=1)
    arrays, args = {}, {}
    for name in NAMES:
        arr = _np.ascontiguousarray(inputs[name])
        arrays[f"in_{name}"] = arr
        args[name] = nc.dram_tensor(f"in_{name}", arr.shape, _mybir.dt.from_np(arr.dtype), kind="ExternalInput").ap()
    out = nc.dram_tensor("out", (B, N, P), F32, kind="ExternalOutput").ap()
    build(nc, args, out)
    r = _run(nc, [arrays], core_ids=[0])
    return r.results[0]["out"]
```

```python
from contextlib import ExitStack

import concourse.bass as bass
from concourse import mybir

ALU = mybir.AluOpType
ACT = mybir.ActivationFunctionType
AX = mybir.AxisListType.X
F32 = mybir.dt.float32
BF16 = mybir.dt.bfloat16
F16 = mybir.dt.float16
I32 = mybir.dt.int32
I8 = mybir.dt.int8
U16 = mybir.dt.uint16

P = 128
B = 8
N = 2048
NB = N // P
COLS = B * NB
WORD = 16
WB = P // WORD
WORDS = N // WORD
Q = 4
G = NB // Q
ROUNDS = 5
RING = 2
HOTS = 3
RANKS = 4
T_DIL = 10.0
BN_EPS = 1e-5
LN_EPS = 1e-5
NORM_EPS = 1e-12
NONE = 4096.0


class Chain:

    def __init__(self, engine, sem, base=0):
        self.engine, self.sem, self.base, self.n = engine, sem, base, 0

    def __call__(self, instruction):
        instruction.then_inc(self.sem, 1)
        self.n += 1
        self.engine.wait_ge(self.sem, self.base + self.n)


HEAD = 8


def fresh(nc, ctx, tag):
    made = []

    def clear(kind, *_):
        if kind is not None:
            return
        with nc.Block() as block:
            @block.gpsimd
            def _(pool):
                for s in made:
                    pool.sem_clear(s)

    def sem(name):
        made.append(ctx.enter_context(nc.semaphore(name + tag)))
        return made[-1]

    ctx.push(clear)
    return sem


def spread(ap, n):
    return ap.unsqueeze(2).broadcast_to([ap.shape[0], ap.shape[1], n])


def repeat(ap, n):
    return ap.unsqueeze(1).broadcast_to([ap.shape[0], n, ap.shape[1]])


def constants(nc, ctx, nodemask):
    def sb(name, shape, dt):
        return ctx.enter_context(nc.sbuf_tensor(name, shape, dt))

    c = {
        "ident": sb("ident", [P, P], F32),
        "ident_b": sb("ident_b", [P, P], BF16),
        "ones": sb("ones", [P, P], F32),
        "mask": sb("mask", [P, B, NB], F32),
        "word_index": sb("word_index", [P, WORDS], F32),
        "bits": sb("bits", [P, WORD, WB], U16),
        "ln_eps": sb("ln_eps", [P, 1], F32),
        "bn_eps": sb("bn_eps", [P, 1], F32),
    }
    with ExitStack() as inner:
        sem = fresh(nc, inner, "_c")
        mask_int = inner.enter_context(nc.sbuf_tensor("mask_int", [COLS, P], I32))
        mask_rows = inner.enter_context(nc.sbuf_tensor("mask_rows", [COLS, P], F32))
        mask_ps = inner.enter_context(nc.psum_tensor("mask_ps", [P, 512], F32))
        mask_loaded = sem("mask_loaded")
        rows_ready = sem("rows_ready")
        mask_turned = sem("mask_turned")
        filled = sem("filled")
        mask_copied = sem("mask_copied")
        block = inner.enter_context(nc.Block())

        @block.sync
        def _(sp):
            sp.dma_start(mask_int[:], nodemask.rearrange("b (j p) -> (b j) p", p=P)).then_inc(mask_loaded, 16)

        @block.gpsimd
        def _(pool):
            link = Chain(pool, filled)
            for t in ("ident", "ident_b"):
                link(nc.gpsimd.memset(c[t][:], 0.0))
                link(nc.gpsimd.affine_select(out=c[t][:], in_=c[t][:], compare_op=ALU.not_equal, fill=1.0,
                                             base=0, pattern=[[-1, P]], channel_multiplier=1))
            link(nc.gpsimd.memset(c["ones"][:], 1.0))
            link(nc.gpsimd.memset(c["ln_eps"][:], LN_EPS))
            link(nc.gpsimd.memset(c["bn_eps"][:], BN_EPS))
            for bit in range(WORD):
                link(nc.gpsimd.memset(c["bits"][:, bit, :], 1 << bit))
            link(nc.gpsimd.iota(c["word_index"][:], pattern=[[1, WORDS]], base=0, channel_multiplier=0,
                                allow_small_or_imprecise_dtypes=True))

        @block.vector
        def _(dve):
            dve.wait_ge(mask_loaded, 16)
            nc.vector.tensor_copy(mask_rows[:], mask_int[:]).then_inc(rows_ready, 1)
            dve.wait_ge(mask_turned, 1)
            nc.vector.tensor_copy(c["mask"][:].rearrange("p b j -> p (b j)"),
                                  mask_ps[:, 0:COLS]).then_inc(mask_copied, 1)
            dve.wait_ge(mask_copied, 1)

        @block.tensor
        def _(pe):
            pe.wait_ge(rows_ready, 1)
            pe.wait_ge(filled, 4)
            nc.tensor.transpose(mask_ps[:, 0:COLS], mask_rows[:], c["ident"][:]).then_inc(mask_turned, 1)
    return c


def norm(nc, c, x, h_out):
    with ExitStack() as ctx:
        def sb(name, shape, dt):
            return ctx.enter_context(nc.sbuf_tensor(name + "_norm", shape, dt))

        sem = fresh(nc, ctx, "_norm")

        xt = [sb(f"xt{i}", [P, NB, P], F32) for i in range(4)]
        h = [sb(f"h{i}", [P, NB, P], F32) for i in range(2)]
        square = [sb(f"square{i}", [P, NB, P], F32) for i in range(2)]
        mean, var, dev, rstd = ([sb(f"{name}{i}", [P, NB], F32) for i in range(2)]
                                for name in ("mean", "var", "dev", "rstd"))
        x_loaded = [sem(f"x_loaded{i}") for i in range(4)]
        h_stored = [sem(f"h_stored{i}") for i in range(2)]
        dve_step = sem("dve_step")
        centred = sem("centred")
        squared = sem("squared")
        summed = sem("summed")
        rooted = sem("rooted")
        scaled = sem("scaled")
        h_ready = sem("h_ready")
        block = ctx.enter_context(nc.Block())

        @block.sync
        def _(sp):
            with sp.Fori(0, B // 4) as four:
                for i in range(4):
                    b = four * 4 + i
                    sp.wait_ge(h_ready, HEAD + b - 3)
                    for g in range(G):
                        sp.dma_start(xt[i][:, g * Q:(g + 1) * Q, :],
                                     x.rearrange("b (g q p) d -> b g p q d", p=P, q=Q)[b, g]).then_inc(x_loaded[i], 16)

        @block.vector
        def _(dve):
            with dve.Fori(0, B // 4) as four:
                for pair in range(2):
                    b = four * 4 + pair * 2
                    link = Chain(dve, dve_step, b * 3)
                    for i in range(2):
                        x_here = xt[pair * 2 + i]
                        dve.wait_ge(x_loaded[pair * 2 + i], (four + 1) * (16 * G))
                        link(nc.vector.tensor_reduce(mean[i][:], x_here[:], AX, ALU.add))
                        link(nc.vector.tensor_scalar(mean[i][:], mean[i][:], 1.0 / P, None, ALU.mult))
                        nc.vector.tensor_tensor(x_here[:], x_here[:], spread(mean[i][:], P), ALU.subtract
                                                ).then_inc(centred, 1)
                    for i in range(2):
                        dve.wait_ge(squared, b + i + 1)
                        nc.vector.tensor_reduce(var[i][:], square[i][:], AX, ALU.add).then_inc(summed, 1)
                    for i in range(2):
                        x_here = xt[pair * 2 + i]
                        dve.wait_ge(rooted, b + i + 1)
                        link(nc.vector.reciprocal(rstd[i][:], dev[i][:]))
                        nc.vector.tensor_tensor(x_here[:], x_here[:], spread(rstd[i][:], P), ALU.mult).then_inc(scaled, 1)

        @block.scalar
        def _(act):
            act.sem_inc(h_ready, HEAD)
            for i in range(2):
                act.sem_inc(h_stored[i], 1)
            with act.Fori(0, B // 4) as four:
                for pair in range(2):
                    b = four * 4 + pair * 2
                    for i in range(2):
                        act.wait_ge(centred, b + i + 1)
                        nc.scalar.activation(square[i][:], xt[pair * 2 + i][:], ACT.Square).then_inc(squared, 1)
                    for i in range(2):
                        act.wait_ge(summed, b + i + 1)
                        nc.scalar.activation(dev[i][:], var[i][:], ACT.Sqrt, scale=1.0 / P, bias=c["ln_eps"][:]
                                             ).then_inc(rooted, 1)
                    for i in range(2):
                        act.wait_ge(scaled, b + i + 1)
                        act.wait_ge(h_stored[i], b * 8 + 1)
                        nc.scalar.activation(h[i][:], xt[pair * 2 + i][:], ACT.Relu).then_inc(h_ready, 1)
                        act.wait_ge(h_ready, HEAD + b + i + 1)
                        act.dma_start(h_out[b + i], h[i][:]).then_inc(h_stored[i], 16)
            for i in range(2):
                act.wait_ge(h_stored[i], B // 2 * 16 + 1)


def dilate(nc, c, adj, h_in, agg_out, col_bits, deg, own):
    with ExitStack() as ctx:
        def sb(name, shape, dt):
            return ctx.enter_context(nc.sbuf_tensor(name + "_dil", shape, dt))

        def ps(name, shape, dt):
            return ctx.enter_context(nc.psum_tensor(name + "_dil", shape, dt))

        sem = fresh(nc, ctx, "_dil")

        nat = [sb(f"nat{i}", [P, N], F32) for i in range(2)]
        sign = sb("sign", [P, B // 2, N], BF16)
        waste = sb("waste", [P, N], I8)
        sum_rows = [sb(f"sum_rows{i}", [P, N], F32) for i in range(RING)]
        sum_h = [sb(f"sum_h{i}", [P, B // 2, P], F32) for i in range(2)]
        agg = [sb(f"agg{i}", [P, Q * P], F32) for i in range(2)]
        gone = [sb(f"gone{i}", [P, N], U16) for i in range(2)]
        v = sb("v", [P, B, N], BF16)
        rank = [sb(f"rank{i}", [P, N], F16)[:] for i in range(RANKS - 2)] + [t[:].bitcast(F16) for t in gone]
        hot = [sb(f"hot{i}", [P, 2, N], BF16) for i in range(HOTS)]
        index = sb("index", [P, N], F16)
        weight = sb("weight", [P, WB], BF16)
        weight_every = sb("weight_every", [P, B, WB], BF16)
        weight3 = sb("weight3", [P, WORD, WB], F32)
        halved = [sb(f"halved{i}", [P, NB, P // 2], BF16) for i in range(2)]
        below = sb("below", [P, NB, NB], F32)
        upper2 = sb("upper2", [P, P], BF16)
        restart = sb("restart", [P, B, P], BF16)
        chunk = sb("chunk", [P, B, NB], F32)
        chunk_left = sb("chunk_left", [P, B, NB], F32)
        left = sb("left", [P, B], F32)
        outside = sb("outside", [P, B], F32)
        masked = sb("masked", [P, B], F32)
        num = sb("num", [P, B], I32)
        odd = sb("odd", [P, B], I32)
        t0 = sb("t0", [P, B], F32)
        t1 = sb("t1", [P, B], F32)
        half = sb("half", [P, B], F32)
        last = sb("last", [P, B], F32)
        valid = sb("valid", [P, B], F32)
        none = sb("none", [P, B], F32)
        every = sb("every", [P, B], F32)
        spot = sb("spot", [P, 32], F32)
        spot_t = sb("spot_t", [P, 32], F32)
        spot_max = sb("spot_max", [P, 1], F32)
        spots = sb("spots", [1, 4], F32)
        a2 = sb("a2", [P, B, P], BF16)
        vbs = [sb(f"vb{i}", [P, B, P], BF16) for i in range(2)]
        rk = sb("rk", [P, B, P], BF16)
        q1 = sb("q1", [P, B, P], BF16)
        q2 = sb("q2", [P, B, P], BF16)
        rm = sb("rm", [P, B, P], BF16)
        swapped = q2
        turned = sb("turned", [P, B, P], BF16)
        flag = sb("flag", [1, 1], I32)
        bias = sb("bias", [P, 2, B], F32)
        signs = sb("signs", [P, 2, B], F32)
        pos = sb("pos", [P, 2, B], F32)
        pos_i = sb("pos_i", [P, 2, B], I32)
        high = sb("high", [P, 2, B], I32)
        low = sb("low", [P, 2, B], I32)
        bit = sb("bit", [P, 2, B], I32)
        one = sb("one", [P, 2, B], I32)

        pack_ps = [ps(f"pack_ps{i}", [P, B // 2, WORDS], F32) for i in range(2)]
        agg_ps = [ps(f"agg_ps{g}", [P, Q * P], F32) for g in range(G)]

        nat_full = [sem(f"nat_full{i}") for i in range(2)]
        h_full = [sem(f"h_full{i}") for i in range(2)]
        sum_full = [sem(f"sum_full{i}") for i in range(RING)]
        sum_used = sem("sum_used")
        agg_ready = sem("agg_ready")
        agg_stored = [sem(f"agg_stored{i}") for i in range(2)]
        sign_ready = sem("sign_ready")
        act_step = sem("act_step")
        set_up = sem("set_up")
        weight_ready = sem("weight_ready")
        row_step = sem("row_step")
        joint_step = sem("joint_step")
        rank_ready = sem("rank_ready")
        signs_ready = sem("signs_ready")
        find_step = sem("find_step")
        hot_ready = sem("hot_ready")
        pack_ready = sem("pack_ready")
        bits_ready = sem("bits_ready")

        SET_UP = 11
        ROW_STEPS = 6
        JOINT_STEPS = 17
        FIND_STEPS = 3
        H = B // 2
        block = ctx.enter_context(nc.Block())
        rows = adj.rearrange("b (j p) n -> b j p n", p=P)

        @block.gpsimd
        def _(pool):
            link = Chain(pool, set_up)
            link(nc.gpsimd.iota(index[:], pattern=[[1, N]], base=0, channel_multiplier=0,
                                allow_small_or_imprecise_dtypes=True))
            link(nc.gpsimd.memset(one[:], 1))
            link(nc.gpsimd.memset(turned[:], 0.0))
            link(nc.gpsimd.memset(col_bits[:].rearrange("p b k w -> p (b k w)").bitcast(I32), 0))
            link(nc.gpsimd.memset(below[:], 1.0))
            link(nc.gpsimd.memset(spot[:], 0.0))
            link(nc.gpsimd.memset(restart[:], 1.0))
            link(nc.gpsimd.memset(restart[:, :, 0:1], 0.0))
            link(nc.gpsimd.affine_select(out=below[:], in_=below[:], compare_op=ALU.is_gt, fill=0.0,
                                         base=0, pattern=[[1, NB], [-1, NB]], channel_multiplier=0))
            link(nc.gpsimd.memset(upper2[:], 2.0))
            link(nc.gpsimd.affine_select(out=upper2[:], in_=upper2[:], compare_op=ALU.is_ge, fill=1.0,
                                         base=0, pattern=[[1, P]], channel_multiplier=-1))
            assert link.n == SET_UP

        @block.sync
        def _(sp):
            def load_pair(j, b):
                for i in range(2):
                    sp.wait_ge(act_step, HEAD + j * B + b + i - 1)
                    sp.dma_start(nat[i][:], rows[b + i, j, :, :]).then_inc(nat_full[i], 16)

            def load_sums(graph, half_of, turn):
                first = half_of * B + turn * RING
                if turn % 2 == 0:
                    sp.wait_ge(sum_used, HEAD + graph * NB + first - B)
                    sp.dma_start(sum_h[turn // 2][:], h_in[graph, :, first:first + B // 2, :]
                                 ).then_inc(h_full[turn // 2], 16)
                for i in range(RING):
                    sp.wait_ge(sum_used, HEAD + graph * NB + first + i - RING + 1)
                    sp.dma_start(sum_rows[i][:], rows[graph, first + i, :, :]).then_inc(sum_full[i], 16)

            def beside(graph, half_of, last):
                j = graph * 2 + half_of
                for turn in range(B // RING):
                    if turn < 2:
                        load_pair(j, H + turn * 2)
                    elif not last:
                        load_pair(j + 1, turn * 2 - H)
                    load_sums(graph, half_of, turn)

            for b in range(0, H, 2):
                load_pair(0, b)
            with sp.Fori(0, B - 1) as graph:
                beside(graph, 0, False)
                beside(graph, 1, False)
            beside(B - 1, 0, False)
            beside(B - 1, 1, True)

        @block.scalar
        def _(act):
            act.sem_inc(sign_ready, HEAD)
            act.sem_inc(bits_ready, HEAD)
            act.sem_inc(act_step, HEAD)
            act.sem_inc(signs_ready, HEAD)
            act.sem_inc(agg_ready, HEAD)
            for i in range(2):
                act.sem_inc(agg_stored[i], 1)

            def signs_of(j, b, first=False):
                for i in range(2):
                    u = j * B + b + i
                    act.wait_ge(nat_full[i], j * (B * 8) + b * 8 + 16)
                    if not first:
                        act.wait_ge(row_step, HEAD + (j * B + b - H) * ROW_STEPS + 4)
                    nc.scalar.activation(sign[:, b % H + i, :], nat[i][:], ACT.Sign).then_inc(sign_ready, 1)
                    act.wait_ge(sign_ready, HEAD + u + 1)
                    nc.scalar.activation(nat[i][:], sign[:, b % H + i, :], ACT.Square,
                                         accum_out=deg[:, b + i, bass.ds(j, 1)]).then_inc(act_step, 1)

            def find(j):
                with act.Fori(0, B // RANKS) as part:
                    b = part * RANKS
                    for i in range(RANKS):
                        act.wait_ge(rank_ready, j * B + b + i + 1)
                        for t in range(2):
                            act.wait_ge(signs_ready, HEAD + (j * B + b + i) * 2 + t - 1)
                            nc.scalar.activation((waste[:], rank[i])[t], rank[i], ACT.Sign,
                                                 bias=bias[:, t, bass.ds(b + i, 1)],
                                                 accum_out=signs[:, t, bass.ds(b + i, 1)]).then_inc(signs_ready, 1)

            def store_bits(j, part):
                act.wait_ge(pack_ready, j * B + (part + 1) * H)
                nc.scalar.copy(col_bits[:, part * H:(part + 1) * H, :, bass.ds(j * WB, WB)],
                               pack_ps[part][:].rearrange("p b (k w) -> p b k w", w=WB)).then_inc(bits_ready, 1)

            def store_sums(b):
                act.wait_ge(sum_used, HEAD + (b + 1) * NB)
                for g in range(G):
                    i = g % 2
                    act.wait_ge(agg_stored[i], b * 32 + g // 2 * 16 + 1)
                    nc.scalar.copy(agg[i][:], agg_ps[g][:]).then_inc(agg_ready, 1)
                    act.wait_ge(agg_ready, HEAD + b * G + g + 1)
                    act.dma_start(agg_out[b, g], agg[i][:]).then_inc(agg_stored[i], 16)

            def block_row(j, graph):
                signs_of(j + 1, 0)
                signs_of(j + 1, 2)
                find(j)
                store_bits(j, 0)
                if graph is not None:
                    store_sums(graph)
                signs_of(j + 1, H)
                store_bits(j, 1)
                signs_of(j + 1, H + 2)

            for b in range(0, B, 2):
                signs_of(0, b, b < H)
            with act.Fori(0, B - 1) as graph:
                block_row(graph * 2, None)
                block_row(graph * 2 + 1, graph)
            block_row(NB - 2, None)
            find(NB - 1)
            for part in range(2):
                store_bits(NB - 1, part)
            store_sums(B - 1)
            act.wait_ge(bits_ready, HEAD + NB * 2)
            for i in range(2):
                act.wait_ge(agg_stored[i], B * G // 2 * 16 + 1)

        @block.tensor
        def _(pe):
            pe.sem_inc(sum_used, HEAD)
            pe.wait_ge(weight_ready, 2)

            def sum_half(b, half_of, turn):
                if turn % 2 == 0:
                    pe.wait_ge(h_full[turn // 2], b * 32 + half_of * 16 + 16)
                for i in range(RING):
                    pe.wait_ge(sum_full[i], (b * (NB // RING) + half_of * (B // RING) + turn + 1) * 16)
                    for g in range(G):
                        ins = nc.tensor.matmul(agg_ps[g][:], sum_h[turn // 2][:, turn % 2 * RING + i, :],
                                               sum_rows[i][:, g * Q * P:(g + 1) * Q * P],
                                               start=(half_of == 0 and turn == 0 and i == 0),
                                               stop=(half_of == 1 and turn == B // RING - 1 and i == RING - 1))
                    ins.then_inc(sum_used, 1)

            with pe.Fori(0, B) as graph:
                for half_of in range(2):
                    j = graph * 2 + half_of
                    if half_of == 0:
                        pe.wait_ge(agg_ready, HEAD + graph * G)
                    for turn in range(B // RING):
                        sum_half(graph, half_of, turn)
                    for part in range(2):
                        pe.wait_ge(bits_ready, HEAD + j * 2 - 2 + part + 1)
                        for b in range(part * H, (part + 1) * H):
                            pe.wait_ge(hot_ready, j * B + b + 1)
                            for k in range(NB):
                                for t in range(2):
                                    nc.tensor.matmul(pack_ps[part][:, b - part * H, k * WB:(k + 1) * WB],
                                                     hot[b % HOTS][:, t, k * P:(k + 1) * P],
                                                     weight[:], start=(t == 0), stop=False)
                                ins = nc.tensor.matmul(pack_ps[part][:, b - part * H, k * WB:(k + 1) * WB],
                                                       v[:, b, k * P:(k + 1) * P],
                                                       weight_every[:, b, :], start=False, stop=True)
                            ins.then_inc(pack_ready, 1)

        @block.vector
        def _(dve):
            flat = "p b m -> p (b m)"
            dve.sem_inc(row_step, HEAD)
            link = Chain(dve, weight_ready)
            dve.wait_ge(set_up, SET_UP)
            link(nc.vector.tensor_tensor(weight3[:], c["ident"][:].rearrange("p (k w) -> p k w", w=WB),
                                         c["bits"][:], ALU.mult))
            with nc.allow_low_precision("powers of two"):
                link(nc.vector.tensor_reduce(weight[:], weight3[:].rearrange("p k w -> p w k"), AX, ALU.add))

            def full_round(link, vb):
                link(nc.vector.tensor_tensor_scan(rk[:].rearrange(flat), restart[:].rearrange(flat),
                                                  vb[:].rearrange(flat), 0.0, ALU.mult, ALU.add))
                link(nc.vector.tensor_tensor(num[:], rk[:, :, P - 1], outside[:], ALU.add))
                nc.vector.scalar_tensor_tensor(valid[:], num[:], 1.0, masked[:], ALU.is_gt, ALU.mult)
                link(nc.vector.tensor_scalar(odd[:], num[:], 1, None, ALU.bitwise_and))
                nc.vector.tensor_tensor(t0[:], num[:], left[:], ALU.subtract)
                nc.vector.scalar_tensor_tensor(every[:], num[:], T_DIL, valid[:], ALU.is_le, ALU.mult)
                nc.vector.tensor_tensor(t1[:], num[:], odd[:], ALU.add)
                link(nc.vector.tensor_scalar(none[:], valid[:], -NONE, NONE, ALU.mult, ALU.add))
                link(nc.vector.scalar_tensor_tensor(last[:], odd[:], NONE, t0[:], ALU.mult, ALU.add))
                nc.vector.scalar_tensor_tensor(half[:], t1[:], 0.5, left[:], ALU.mult, ALU.subtract)
                link(nc.vector.tensor_tensor(last[:], last[:], none[:], ALU.add))
                nc.vector.scalar_tensor_tensor(last[:], every[:], -3 * NONE, last[:], ALU.mult, ALU.add)
                link(nc.vector.tensor_tensor(half[:], half[:], none[:], ALU.add))
                nc.vector.tensor_tensor(q1[:], rk[:], spread(half[:], P), ALU.is_equal)
                link(nc.vector.tensor_tensor(q2[:], rk[:], spread(last[:], P), ALU.is_ge))
                link(nc.vector.tensor_tensor(q1[:], q1[:], q2[:], ALU.max))
                link(nc.vector.tensor_tensor(rm[:], q1[:], vb[:], ALU.mult))

            def turn_rows(link, new):
                link(nc.vector.transpose(swapped[:].rearrange(flat), rm[:].rearrange(flat)))
                for top in range(0, P, 32):
                    for under in range(top, P, 32):
                        ins = nc.vector.tensor_copy(turned[under:under + 32, :, top:top + 32],
                                                    swapped[top:top + 32, :, under:under + 32])
                link(ins)
                link(nc.vector.tensor_tensor(new[:], a2[:], turned[:], ALU.is_gt))

            def look(link, old, new):
                link(nc.vector.scalar_tensor_tensor(q1[:].rearrange(flat), old[:].rearrange(flat), 1.0,
                                                    new[:].rearrange(flat), ALU.mult, ALU.not_equal,
                                                    accum_out=spot[:, 0:1]))
                link(nc.vector.transpose(spot_t[:], spot[:]))
                link(nc.vector.tensor_reduce(spot_max[:], spot_t[:], AX, ALU.max))
                for quad in range(4):
                    ins = nc.vector.tensor_copy(spots[:, quad:quad + 1], spot_max[32 * quad:32 * quad + 1, :])
                link(ins)
                nc.vector.tensor_reduce(flag[:], spots[:], AX, ALU.max)
                dve.drain()
                return dve.value_load(flag[0:1, 0:1], min_val=0, max_val=P * B)

            def settle(depth):
                def link(ins):
                    dve.drain()
                old, new = vbs[depth % 2], vbs[(depth + 1) % 2]
                if depth < ROUNDS:
                    full_round(link, new)
                    turn_rows(link, old)
                    changed = look(link, new, old)
                    with dve.If(changed > 0):
                        settle(depth + 1)
                else:
                    with dve.Fori(0, P):
                        full_round(link, new)
                        turn_rows(link, new)

            with dve.Fori(0, NB) as j:
                for part in range(2):
                    with dve.Fori(0, H // 2) as pair:
                        b = pair * 2 + part * H
                        count = (j * B + b) * ROW_STEPS + HEAD
                        done = 0

                        def step(ins):
                            nonlocal done
                            ins.then_inc(row_step, 1)
                            done += 1
                            dve.wait_ge(row_step, count + done - 1)

                        for i in range(2):
                            if i == 0:
                                dve.wait_ge(bits_ready, HEAD - 2 + j * 2 + part + 1)
                            words = col_bits[:, b + i, j, :].rearrange("p (k w) -> p k w", w=WB).unsqueeze(2)
                            step(nc.vector.tensor_tensor(gone[i][:].rearrange("p (k o w) -> p k o w", o=WORD, w=WB),
                                                         words.broadcast_to([P, NB, WORD, WB]),
                                                         c["bits"][:].unsqueeze(1).broadcast_to([P, NB, WORD, WB]),
                                                         ALU.bitwise_and))
                        for i in range(2):
                            dve.wait_ge(sign_ready, HEAD + j * B + b + i + 1)
                            step(nc.vector.tensor_tensor(v[:, b + i, :], sign[:, pair * 2 + i, :], gone[i][:], ALU.is_gt))
                        size = P // 2
                        for i in range(2):
                            v_chunks = v[:, b + i, :].rearrange("p (k m) -> p k m", m=P)
                            step(nc.vector.tensor_tensor(halved[i][:], v_chunks[:, :, 0:size], v_chunks[:, :, size:P], ALU.add))
                        for size in (P // 4, P // 8):
                            for i in range(2):
                                step(nc.vector.tensor_tensor(halved[i][:, :, 0:size], halved[i][:, :, 0:size],
                                                             halved[i][:, :, size:2 * size], ALU.add))
                        for i in range(2):
                            step(nc.vector.tensor_reduce(chunk[:, b + i, :], halved[i][:, :, 0:size], AX, ALU.add))
                        assert done == 2 * ROW_STEPS
                dve.wait_ge(row_step, HEAD + (j + 1) * B * ROW_STEPS)

                link = Chain(dve, joint_step, j * JOINT_STEPS)
                link(nc.vector.tensor_tensor(chunk_left[:], chunk[:], repeat(below[:, j, :], B), ALU.mult))
                nc.vector.tensor_reduce(t0[:], chunk[:], AX, ALU.add)
                link(nc.vector.tensor_reduce(left[:], chunk_left[:], AX, ALU.add))
                nc.vector.tensor_tensor(outside[:], t0[:], chunk[:, :, j], ALU.subtract)
                nc.vector.tensor_scalar(masked[:], c["mask"][:, :, j], 0.0, None, ALU.not_equal)
                link(nc.vector.tensor_tensor(a2[:], v[:, :, bass.ds(j * P, P)], repeat(upper2[:], B), ALU.mult))
                link(nc.vector.tensor_scalar(vbs[0][:], v[:, :, bass.ds(j * P, P)], 1.0, None, ALU.mult))
                full_round(link, vbs[0])
                turn_rows(link, vbs[1])
                assert link.n == JOINT_STEPS
                def loose(ins):
                    dve.drain()
                changed = look(loose, vbs[0], vbs[1])
                with dve.If(changed > 0):
                    settle(0)
                nc.vector.tensor_tensor(vbs[0][:], a2[:], turned[:], ALU.is_gt)
                dve.drain()

                nc.vector.tensor_scalar(v[:, :, bass.ds(j * P, P)], vbs[0][:], 1.0, None, ALU.mult)
                nc.vector.scalar_tensor_tensor(half[:], every[:], NONE, half[:], ALU.mult, ALU.add)
                nc.vector.scalar_tensor_tensor(last[:], every[:], 4 * NONE, last[:], ALU.mult, ALU.add)
                nc.vector.tensor_tensor(weight_every[:], repeat(weight[:], B), spread(every[:], WB), ALU.mult)
                nc.vector.tensor_scalar(t0[:], left[:], -1.0, 0.5, ALU.mult, ALU.add)
                dve.drain()
                nc.vector.tensor_tensor(bias[:, 0, :], t0[:], half[:], ALU.subtract)
                nc.vector.tensor_tensor(bias[:, 1, :], t0[:], last[:], ALU.subtract)
                nc.vector.tensor_scalar(own[:, 4, :, j], every[:], float(2 ** WORD - 1), None, ALU.mult)

                def count(b):
                    for i in range(b, b + 2):
                        dve.wait_ge(signs_ready, HEAD + (j * B + i - RANKS + 1) * 2)
                        nc.vector.tensor_tensor_scan(rank[i % RANKS], v[:, i, :], v[:, i, :], 0.0,
                                                     ALU.add, ALU.max).then_inc(rank_ready, 1)

                def find(b):
                    these = slice(b, b + 2)
                    link = Chain(dve, find_step, j * (B // 2 * FIND_STEPS) + b // 2 * FIND_STEPS)
                    dve.wait_ge(signs_ready, HEAD + (j * B + b + 2) * 2)
                    nc.vector.tensor_scalar(pos[:, :, these], signs[:, :, these], -0.5, N / 2, ALU.mult, ALU.add)
                    link(nc.vector.tensor_scalar(pos_i[:, :, these], signs[:, :, these], -0.5, N / 2, ALU.mult, ALU.add))
                    nc.vector.tensor_scalar(high[:, :, these], pos_i[:, :, these], 7, 3,
                                            ALU.logical_shift_right, ALU.logical_shift_left)
                    nc.vector.tensor_scalar(low[:, :, these], pos_i[:, :, these], WB - 1, None, ALU.bitwise_and)
                    link(nc.vector.tensor_scalar(bit[:, :, these], pos_i[:, :, these], 3, WORD - 1,
                                                 ALU.logical_shift_right, ALU.bitwise_and))
                    link(nc.vector.tensor_tensor(bit[:, :, these], one[:, :, these], bit[:, :, these],
                                                 ALU.logical_shift_left))
                    for t in range(2):
                        nc.vector.tensor_tensor(own[:, 2 * t, these, j], high[:, t, these], low[:, t, these], ALU.add)
                        nc.vector.tensor_copy(own[:, 2 * t + 1, these, j], bit[:, t, these])
                    assert link.n == FIND_STEPS
                    for i in range(b, b + 2):
                        if i >= HOTS:
                            dve.wait_ge(pack_ready, j * B + i - HOTS + 1)
                        for t in range(2):
                            ins = nc.vector.tensor_scalar(hot[i % HOTS][:, t, :], index[:], pos[:, t, i:i + 1],
                                                          None, ALU.is_equal)
                        ins.then_inc(hot_ready, 1)

                count(0)
                count(2)
                find(0)
                count(4)
                find(2)
                count(6)
                find(4)
                find(6)
def first_layer(nc, c, h_in, h_out, k):
    with ExitStack() as ctx:
        def sb(name, shape, dt=F32):
            return ctx.enter_context(nc.sbuf_tensor(name + "_first", shape, dt))

        sem = fresh(nc, ctx, "_first")
        LOADS = 4

        h = [sb(f"h{i}", [P, Q, P]) for i in range(LOADS)]
        x_in = [sb(f"x_in{i}", [P, Q, P]) for i in range(LOADS)]
        agg = [sb(f"agg{i}", [P, Q, P]) for i in range(LOADS)]
        h_t = [sb(f"h_t{i}", [P, Q, P]) for i in range(2)]
        z = [sb(f"z{i}", [P, Q, P]) for i in range(2)]
        x2 = [sb(f"x2{i}", [P, Q, P]) for i in range(2)]
        centred = [sb(f"centred{i}", [P, Q, P]) for i in range(2)]
        r = [sb(f"r{i}", [P, Q, P]) for i in range(2)]
        waste = [sb(f"waste{i}", [P, P], BF16) for i in range(Q)]
        mean = [sb(f"mean{i}", [P, Q]) for i in range(2)]
        ss = [sb(f"ss{i}", [P, Q]) for i in range(2)]
        root = [sb(f"root{i}", [P, Q]) for i in range(2)]
        inv = [sb(f"inv{i}", [P, Q]) for i in range(2)]
        turn_ps, a_ps, z_ps = ([ctx.enter_context(nc.psum_tensor(f"{name}{i}_first", [P, Q, P], F32))
                                for i in range(2)] for name in ("turn_ps", "a_ps", "z_ps"))
        loaded = [sem(f"loaded{i}") for i in range(LOADS)]
        x2_stored = [sem(f"x2_stored{i}") for i in range(2)]
        r_stored = [sem(f"r_stored{i}") for i in range(2)]
        turn_ready = sem("turn_ready")
        ht_ready = sem("ht_ready")
        products = sem("products")
        emptied = sem("emptied")
        step = sem("step")
        x2_ready = sem("x2_ready")
        centred_ready = sem("centred_ready")
        ss_ready = sem("ss_ready")
        root_ready = sem("root_ready")
        inv_ready = sem("inv_ready")
        r_ready = sem("r_ready")
        block = ctx.enter_context(nc.Block())
        UNITS = 2 * G
        BODIES = B // 2
        LAST = BODIES - 1
        x_nodes = k["x"].rearrange("b (g q p) d -> b g p q d", p=P, q=Q)

        def all_units(engine, unit):
            for n in range(UNITS):
                unit(0, n, True)
            with engine.Fori(1, BODIES) as body:
                for n in range(UNITS):
                    unit(body, n, False)

        def back(body, n, by):
            return (body, n - by) if n >= by else (body - 1, n - by + UNITS)

        @block.sync
        def _(sp):
            with sp.Fori(0, BODIES) as body:
                for n in range(UNITS):
                    u, i = body * UNITS + n, n % LOADS
                    b, g = body * 2 + n // G, n % G
                    sp.wait_ge(emptied, HEAD + u - LOADS + 1)
                    sp.dma_start(h[i][:], h_in[b, :, g * Q:(g + 1) * Q, :]).then_inc(loaded[i], 16)
                    sp.dma_start(agg[i][:].rearrange("p q n -> p (q n)"), k["agg"][b, g]).then_inc(loaded[i], 16)
                    sp.wait_ge(x2_ready, HEAD + u - LOADS + 1)
                    sp.dma_start(x_in[i][:], x_nodes[b, g]).then_inc(loaded[i], 16)

        @block.tensor
        def _(pe):
            with pe.Fori(0, BODIES) as body:
                for n in range(UNITS):
                    u, i = body * UNITS + n, n % 2
                    l = n % LOADS
                    pe.wait_ge(loaded[l], (body * (UNITS // LOADS) + n // LOADS + 1) * 48)
                    for q in range(Q):
                        ins = nc.tensor.transpose(turn_ps[i][:, q, :], h[l][:, q, :], c["ident"][:])
                    ins.then_inc(turn_ready, 1)
                    pe.wait_ge(emptied, HEAD + u - 1)
                    for q in range(Q):
                        nc.tensor.matmul(a_ps[i][:, q, :], agg[l][:, q, :], k["wA"][:], start=True, stop=True)
                    pe.wait_ge(ht_ready, u + 1)
                    for q in range(Q):
                        nc.tensor.matmul(z_ps[i][:, q, :], h_t[i][:, q, :], k["wZ"][:, 0:P], start=True, stop=False)
                        ins = nc.tensor.matmul(z_ps[i][:, q, :], c["ones"][0:1, :], k["row_b"][0:1, :],
                                               start=False, stop=True)
                    ins.then_inc(products, 1)

        @block.scalar
        def _(act):
            act.sem_inc(r_ready, HEAD)
            for i in range(2):
                act.sem_inc(x2_stored[i], 1)
                act.sem_inc(r_stored[i], 1)

            def squares(body, n):
                u, i = body * UNITS + n, n % 2
                b, g = body * 2 + n // G, n % G
                act.wait_ge(x2_ready, HEAD + u + 1)
                act.dma_start(k["x2"][b, :, g * Q:(g + 1) * Q, :], x2[i][:]).then_inc(x2_stored[i], 16)
                act.wait_ge(centred_ready, u + 1)
                act.wait_ge(ss_ready, u)
                for q in range(Q):
                    ins = nc.scalar.activation(waste[q][:], centred[i][:, q, :], ACT.Square, accum_out=ss[i][:, q:q + 1])
                ins.then_inc(ss_ready, 1)
                act.wait_ge(ss_ready, u + 1)
                nc.scalar.activation(root[i][:], ss[i][:], ACT.Sqrt, scale=1.0 / P, bias=c["ln_eps"][:]
                                     ).then_inc(root_ready, 1)

            def scale(body, n):
                u, i = body * UNITS + n, n % 2
                b, g = body * 2 + n // G, n % G
                act.wait_ge(inv_ready, u + 1)
                act.wait_ge(r_stored[i], (body * (UNITS // 2) + n // 2) * 16 + 1)
                for q in range(Q):
                    ins = nc.scalar.activation(r[i][:, q, :], centred[i][:, q, :], ACT.Relu, scale=inv[i][:, q:q + 1])
                ins.then_inc(r_ready, 1)
                act.wait_ge(r_ready, HEAD + u + 1)
                act.dma_start(h_out[b, :, g * Q:(g + 1) * Q, :], r[i][:]).then_inc(r_stored[i], 16)

            def unit(body, n, first):
                u, i = body * UNITS + n, n % 2
                act.wait_ge(turn_ready, u + 1)
                nc.scalar.copy(h_t[i][:], turn_ps[i][:]).then_inc(ht_ready, 1)
                if not first or n >= 3:
                    scale(*back(body, n, 3))
                if not first or n >= 2:
                    squares(*back(body, n, 2))

            all_units(act, unit)
            scale(LAST, UNITS - 3)
            squares(LAST, UNITS - 2)
            scale(LAST, UNITS - 2)
            squares(LAST, UNITS - 1)
            scale(LAST, UNITS - 1)
            for i in range(2):
                act.wait_ge(x2_stored[i], BODIES * (UNITS // 2) * 16 + 1)
                act.wait_ge(r_stored[i], BODIES * (UNITS // 2) * 16 + 1)

        @block.vector
        def _(dve):
            dve.sem_inc(emptied, HEAD)
            dve.sem_inc(x2_ready, HEAD)
            link = Chain(dve, step)
            link(nc.vector.reciprocal(k["rdeg"][:], k["deg"][:]))

            def factors(body, n):
                u, i = body * UNITS + n, n % 2
                dve.wait_ge(root_ready, u + 1)
                nc.vector.reciprocal(inv[i][:], root[i][:]).then_inc(inv_ready, 1)

            def unit(body, n, first):
                u, i = body * UNITS + n, n % 2
                b, g = body * 2 + n // G, n % G
                link = Chain(dve, step, 1 + u * 3)
                dve.wait_ge(products, u + 1)
                link(nc.vector.tensor_tensor(z[i][:], a_ps[i][:], spread(k["rdeg"][:, b, g * Q:(g + 1) * Q], P), ALU.mult))
                nc.vector.tensor_tensor(z[i][:], z[i][:], z_ps[i][:], ALU.add).then_inc(emptied, 1)
                dve.wait_ge(emptied, HEAD + u + 1)
                dve.wait_ge(x2_stored[i], (body * (UNITS // 2) + n // 2) * 16 + 1)
                nc.vector.scalar_tensor_tensor(x2[i][:], z[i][:], 0.0, x_in[n % LOADS][:], ALU.max, ALU.add).then_inc(x2_ready, 1)
                dve.wait_ge(x2_ready, HEAD + u + 1)
                link(nc.vector.tensor_reduce(mean[i][:], x2[i][:], AX, ALU.add))
                link(nc.vector.tensor_scalar(mean[i][:], mean[i][:], 1.0 / P, None, ALU.mult))
                dve.wait_ge(r_ready, HEAD + u - 1)
                nc.vector.tensor_tensor(centred[i][:], x2[i][:], spread(mean[i][:], P), ALU.subtract
                                        ).then_inc(centred_ready, 1)
                if not first or n >= 1:
                    factors(*back(body, n, 1))

            all_units(dve, unit)
            factors(LAST, UNITS - 1)


def weights(nc, c, tag, w, prev):
    with ExitStack() as ctx:
        def sb(name, shape, dt=F32):
            return ctx.enter_context(nc.sbuf_tensor(name + tag, shape, dt))

        sem = fresh(nc, ctx, tag)

        raw = sb("raw", [P, 3, P])
        bias_row = sb("bias_row", [1, P])
        final_row = sb("final_row", [1, P])
        gamma = sb("gamma", [P, 1])
        beta_in = sb("beta_in", [P, 1])
        moments = sb("moments", [P, 2])
        square = sb("square", [P, 1])
        var = sb("var", [P, 1])
        dev = sb("dev", [P, 1])
        alpha = sb("alpha", [P, 1])
        beta = sb("beta", [P, 1])
        beta_wide = sb("beta_wide", [P, P])
        sums_ps = ctx.enter_context(nc.psum_tensor("sums_ps" + tag, [P, 512], F32))
        moved_ps = [ctx.enter_context(nc.psum_tensor(f"moved_ps{i}" + tag, [P, 512], F32)) for i in range(4)]
        loaded = sem("loaded")
        turned = sem("turned")
        summed = sem("summed")
        step = sem("step")
        var_ready = sem("var_ready")
        dev_ready = sem("dev_ready")
        wide_ready = sem("wide_ready")
        moved = sem("moved")
        block = ctx.enter_context(nc.Block())
        parts = [t for t in ("Wr", "Wx", "Wl") if t in w]
        place = {"Wr": 0, "Wx": 1, "Wl": 2}
        loads = len(parts) + ("b" in w) + ("bl" in w) + 2 * (prev is not None)

        @block.sync
        def _(sp):
            for t in parts:
                sp.dma_start(raw[:, place[t], :], w[t]).then_inc(loaded, 16)
            if "b" in w:
                sp.dma_start(bias_row[:], w["b"].unsqueeze(0)).then_inc(loaded, 16)
            if "bl" in w:
                sp.dma_start(final_row[:], w["bl"].unsqueeze(0)).then_inc(loaded, 16)
            if prev is not None:
                sp.dma_start(gamma[:], w["g"].unsqueeze(1)).then_inc(loaded, 16)
                sp.dma_start(beta_in[:], w["be"].unsqueeze(1)).then_inc(loaded, 16)

        @block.tensor
        def _(pe):
            pe.wait_ge(loaded, 16 * loads)
            if w.get("turn"):
                for i, t in enumerate(parts):
                    nc.tensor.transpose(moved_ps[i][:, 0:P], raw[:, place[t], :], c["ident"][:]).then_inc(turned, 1)
            if "b" in w:
                nc.tensor.matmul(moved_ps[3][:, 0:P], c["ones"][0:1, :], bias_row[:],
                                 start=True, stop=prev is None).then_inc(moved, 1)
            if "bl" in w:
                nc.tensor.matmul(sums_ps[:, 256:256 + P], c["ones"][0:1, :], final_row[:],
                                 start=True, stop=True).then_inc(moved, 1)
            if prev is not None:
                for s in range(2):
                    for q in range(Q):
                        ins = nc.tensor.matmul(sums_ps[:, s:s + 1], prev[s][:, q, :], c["ones"][:, 0:1],
                                               start=(q == 0), stop=(q == Q - 1))
                ins.then_inc(summed, 1)
                pe.wait_ge(wide_ready, 1)
                for t in parts:
                    if t == "Wx":
                        ins = nc.tensor.matmul(moved_ps[3][:, 0:P], beta_wide[:], raw[:, 1, :], start=False, stop=True)
                    else:
                        ins = nc.tensor.matmul(moved_ps[place[t]][:, 0:P], beta_wide[:], raw[:, place[t], :],
                                               start=True, stop=True)
                    ins.then_inc(moved, 1)

        @block.scalar
        def _(act):
            if prev is not None:
                act.wait_ge(var_ready, 1)
                nc.scalar.activation(dev[:], var[:], ACT.Sqrt, bias=c["bn_eps"][:]).then_inc(dev_ready, 1)

        @block.vector
        def _(dve):
            link = Chain(dve, step)
            if w.get("turn"):
                nc.vector.memset(w["row_Wl"], 0.0)
            dve.wait_ge(loaded, 16 * loads)
            if w.get("turn"):
                dve.wait_ge(turned, len(parts))
                for i, t in enumerate(parts):
                    nc.vector.tensor_copy(w["to_" + t], moved_ps[i][:, 0:P])
            elif prev is None:
                for t in parts:
                    nc.vector.tensor_copy(w["to_" + t], raw[:, place[t], :])
            else:
                dve.wait_ge(summed, 1)
                link(nc.vector.tensor_scalar(moments[:], sums_ps[:, 0:2], 1.0 / (B * N), None, ALU.mult))
                link(nc.vector.tensor_tensor(square[:], moments[:, 0:1], moments[:, 0:1], ALU.mult))
                link(nc.vector.tensor_tensor(var[:], moments[:, 1:2], square[:], ALU.subtract))
                nc.vector.tensor_scalar(var[:], var[:], 0.0, None, ALU.max).then_inc(var_ready, 1)
                dve.wait_ge(dev_ready, 1)
                link(nc.vector.reciprocal(alpha[:], dev[:]))
                link(nc.vector.tensor_tensor(alpha[:], alpha[:], gamma[:], ALU.mult))
                link(nc.vector.tensor_tensor(beta[:], moments[:, 0:1], alpha[:], ALU.mult))
                link(nc.vector.tensor_tensor(beta[:], beta_in[:], beta[:], ALU.subtract))
                nc.vector.tensor_scalar(beta_wide[:], c["ones"][:], beta[:], None, ALU.mult).then_inc(wide_ready, 1)
                for t in parts:
                    nc.vector.tensor_scalar(w["to_" + t], raw[:, place[t], :], alpha[:], None, ALU.mult)
                dve.wait_ge(moved, len(parts) + ("b" in w) + ("bl" in w))
                if "Wr" in w:
                    nc.vector.tensor_copy(w["row_Wr"], moved_ps[0][:, 0:P])
                nc.vector.tensor_tensor(w["row_Wl"], w["row_Wl"], moved_ps[2][:, 0:P], ALU.add)
            if "b" in w:
                dve.wait_ge(moved, 1)
                nc.vector.tensor_copy(w["row_b"], moved_ps[3][:, 0:P])
            if "bl" in w:
                nc.vector.tensor_copy(w["row_bl"], sums_ps[:, 256:256 + P])


def layer(nc, c, L, adj, turned_adj, r_in, r_out, k):
    MASK, DEEP = L == 1, L >= 2
    ZW = 2 * P if DEEP else P
    W = Q * P
    with ExitStack() as ctx:
        def sb(name, shape, dt=F32):
            return ctx.enter_context(nc.sbuf_tensor(name + f"_L{L}", shape, dt))

        def ps(name, shape, dt=F32):
            return ctx.enter_context(nc.psum_tensor(name + f"_L{L}", shape, dt))

        sem = fresh(nc, ctx, f"_L{L}")

        HALF = NB // 2
        STAGES = 1 if MASK else 2
        stage = [sb(f"stage{i}", [P, NB, P]) for i in range(STAGES)]
        piece = [sb(f"piece{i}", [P, HALF, W]) for i in range(4)]
        r_t = [sb(f"r_t{i}", [P, W]) for i in range(2)]
        agg = [sb(f"agg{i}", [P, W]) for i in range(2)]
        z = [sb(f"z{i}", [P, Q, P]) for i in range(2)]
        r = [sb(f"r{i}", [P, Q, P]) for i in range(2)]
        waste = [sb(f"waste{i}", [P, P], BF16) for i in range(Q)]
        ss = sb("ss", [P, Q])
        root = sb("root", [P, Q])
        inv = sb("inv", [P, Q])
        r_sq = sb("r_sq", [P, Q, P])
        if MASK:
            nat = [sb(f"nat{i}", [P, N]) for i in range(2 * Q)]
            word1 = sb("word1", [P, WORDS])
            word2 = sb("word2", [P, WORDS])
            words = sb("words", [P, WORDS], U16)
            words2 = sb("words2", [P, WORDS], U16)
            gone = sb("gone", [P, N], U16)
            row_sum = sb("row_sum", [P, Q])
            row_max = sb("row_max", [P, Q])
        if DEEP:
            extra = [sb(f"extra{i}", [P, Q, P]) for i in range(2)]

        turn_ps = ps("turn_ps", [P, W])
        agg_ps = [ps(f"agg_ps{i}", [P, W]) for i in range(1 if MASK else 2)]
        a_ps = ps("a_ps", [P, Q, P])
        z_ps = ps("z_ps", [P, Q, ZW])
        if MASK:
            piece_ps = [ps(f"piece_ps{i}", [P, W]) for i in range(4)]

        stage_full = [[sem(f"stage_full{i}{h}") for h in range(2)] for i in range(STAGES)]
        piece_full = [sem(f"piece_full{i}") for i in range(4)]
        piece_stored = [sem(f"piece_stored{i}") for i in range(4)]
        nat_full = [sem(f"nat_full{i}") for i in range(2 * Q)]
        r_stored = [sem(f"r_stored{i}") for i in range(2)]
        half_used = sem("half_used")
        turn_ready = sem("turn_ready")
        rt_ready = sem("rt_ready")
        aggs_ready = sem("aggs_ready")
        a_ready = sem("a_ready")
        z_ready = sem("z_ready")
        mask_ready = sem("mask_ready")
        mask_step = sem("mask_step")
        piece_turned = sem("piece_turned")
        piece_moved = sem("piece_moved")
        dve_step = sem("dve_step")
        end_step = sem("end_step")
        ss_ready = sem("ss_ready")
        root_ready = sem("root_ready")
        inv_ready = sem("inv_ready")
        r_ready = sem("r_ready")
        extra_ready = sem("extra_ready")
        pool_step = sem("pool_step")
        added = sem("added")
        once = sem("once")
        block = ctx.enter_context(nc.Block())
        UNITS = 2 * G
        BODIES = B // 2
        adj_rows = adj.rearrange("b (k p) n -> b k p n", p=P)

        def all_units(engine, unit, tail):
            for n in range(UNITS):
                unit(0, n, True)
            with engine.Fori(1, BODIES) as body:
                for n in range(UNITS):
                    unit(body, n, False)
            tail()

        def back(body, n, by):
            return (body, n - by) if n >= by else (body - 1, n - by + UNITS)

        LAST = BODIES - 1

        @block.sync
        def _(sp):
            with sp.Fori(0, BODIES) as body:
                for n in range(UNITS):
                    u = body * UNITS + n
                    b, g = body * 2 + n // G, n % G
                    if MASK:
                        for q in range(Q):
                            if q == 0:
                                sp.wait_ge(piece_turned, NB * HEAD + (u - 1) * NB)
                            i = (n % 2) * Q + q
                            sp.dma_start(nat[i][:], adj_rows[b, g * Q + q]).then_inc(nat_full[i], 16)
                    if g == 0:
                        for h in range(2):
                            sp.wait_ge(half_used, 2 * (HEAD + u - (STAGES - 1) * G) - 1 + h)
                            s, these = n // G % STAGES, slice(h * HALF, (h + 1) * HALF)
                            sp.dma_start(stage[s][:, these, :], r_in[b, :, these, :]).then_inc(stage_full[s][h], 16)
                    if DEEP:
                        for h in range(2):
                            i = 2 * (n % 2) + h
                            sp.wait_ge(half_used, 2 * HEAD + 2 * (u - 2) + h + 1)
                            sp.dma_start(piece[i][:], turned_adj[b, g, :, h * HALF:(h + 1) * HALF, :]
                                         ).then_inc(piece_full[i], 16)

        @block.tensor
        def _(pe):
            pe.sem_inc(half_used, 2 * HEAD)
            if MASK:
                pe.sem_inc(piece_turned, NB * HEAD)

            def post_a(body, n):
                u = body * UNITS + n
                pe.wait_ge(aggs_ready, u + 1)
                pe.wait_ge(z_ready, HEAD + u)
                for q in range(Q):
                    ins = nc.tensor.matmul(a_ps[:, q, :], agg[n % 2][:, q * P:(q + 1) * P], k["wA"][:],
                                           start=True, stop=True)
                ins.then_inc(a_ready, 1)

            def post_z(body, n):
                u = body * UNITS + n
                pe.wait_ge(rt_ready, u + 1)
                pe.wait_ge(z_ready, HEAD + u)
                for q in range(Q):
                    nc.tensor.matmul(z_ps[:, q, :], r_t[n % 2][:, q * P:(q + 1) * P], k["wZ"][:, 0:ZW],
                                     start=True, stop=True)

            def unit(body, n, first):
                    u = body * UNITS + n
                    g, s = n % G, n // G % STAGES
                    before = None if first and n == 0 else back(body, n, 1)

                    def sum_block(m):
                        i = 2 * (n % 2) + m // HALF
                        if g == 0 and m == HALF:
                            pe.wait_ge(stage_full[s][1], (body * (2 // STAGES) + (n // G) // STAGES + 1) * 16)
                        if m % HALF == 0 and not MASK:
                            pe.wait_ge(piece_full[i], (body * (UNITS // 2) + n // 2 + 1) * 16)
                        if MASK:
                            pe.wait_ge(piece_moved, HEAD + u * NB + m + 1)
                        ins = nc.tensor.matmul(agg_ps[n % len(agg_ps)][:], stage[s][:, m, :],
                                               piece[i][:, m % HALF, :], start=(m == 0), stop=(m == NB - 1))
                        if m % HALF == HALF - 1:
                            ins.then_inc(half_used, 1)

                    if g == 0:
                        pe.wait_ge(stage_full[s][0], (body * (2 // STAGES) + (n // G) // STAGES + 1) * 16)
                    for q in range(Q):
                        ins = nc.tensor.transpose(turn_ps[:, q * P:(q + 1) * P], stage[s][:, g * Q + q, :], c["ident"][:])
                    ins.then_inc(turn_ready, 1)
                    if MASK:
                        pe.wait_ge(mask_ready, (u + 1) * Q)
                    for m in range(NB + 2):
                        if MASK and m < NB:
                            pe.wait_ge(piece_moved, HEAD + u * NB + m - 3)
                            for q in range(Q):
                                ins = nc.tensor.transpose(piece_ps[m % 4][:, q * P:(q + 1) * P],
                                                          nat[(n % 2) * Q + q][:, m * P:(m + 1) * P], c["ident"][:])
                            ins.then_inc(piece_turned, 1)
                        if m == 2 and MASK and before:
                            pe.wait_ge(aggs_ready, u)
                        if m >= 2:
                            sum_block(m - 2)
                        if m == 6 and before:
                            if MASK:
                                post_z(*before)
                            post_a(*before)
                        if m == 13 and not MASK:
                            post_z(body, n)

            def tail():
                if MASK:
                    post_z(LAST, UNITS - 1)
                post_a(LAST, UNITS - 1)

            all_units(pe, unit, tail)

        @block.scalar
        def _(act):
            act.sem_inc(r_ready, HEAD)
            for i in range(2):
                act.sem_inc(r_stored[i], 1)
            if MASK:
                act.sem_inc(piece_moved, HEAD)
                for i in range(4):
                    act.sem_inc(piece_stored[i], 1)

            def post_squares(body, n):
                u, i = body * UNITS + n, n % 2
                b, g = body * 2 + n // G, n % G
                act.wait_ge(z_ready, HEAD + u + 1)
                act.wait_ge(r_ready, HEAD + u)
                for q in range(Q):
                    ins = nc.scalar.activation(waste[q][:], z[i][:, q, :], ACT.Square, accum_out=ss[:, q:q + 1])
                ins.then_inc(ss_ready, 1)
                act.wait_ge(ss_ready, u + 1)
                nc.scalar.activation(root[:], ss[:], ACT.Sqrt).then_inc(root_ready, 1)

            def post_scale(body, n):
                u, i = body * UNITS + n, n % 2
                b, g = body * 2 + n // G, n % G
                act.wait_ge(inv_ready, u + 1)
                act.wait_ge(r_stored[i], (body * (UNITS // 2) + n // 2) * 16 + 1)
                act.wait_ge(added, HEAD + u - 1)
                for q in range(Q):
                    ins = nc.scalar.activation(r[i][:, q, :], z[i][:, q, :], ACT.Relu, scale=inv[:, q:q + 1])
                ins.then_inc(r_ready, 1)
                act.wait_ge(r_ready, HEAD + u + 1)
                act.dma_start(r_out[b, :, g * Q:(g + 1) * Q, :], r[i][:]).then_inc(r_stored[i], 16)

            def unit(body, n, first):
                u = body * UNITS + n
                b, g = body * 2 + n // G, n % G
                before = None if first and n == 0 else back(body, n, 1)
                act.wait_ge(turn_ready, u + 1)
                nc.scalar.copy(r_t[n % 2][:], turn_ps[:]).then_inc(rt_ready, 1)
                if MASK:
                    for m in range(NB):
                        i = 2 * (n % 2) + m // HALF
                        if m % HALF == 0:
                            act.wait_ge(piece_stored[i], (body * (UNITS // 2) + n // 2) * 16 + 1)
                        act.wait_ge(piece_turned, NB * HEAD + u * NB + m + 1)
                        nc.scalar.copy(piece[i][:, m % HALF, :], piece_ps[m % 4][:]).then_inc(piece_moved, 1)
                        if m % HALF == HALF - 1:
                            act.wait_ge(piece_moved, HEAD + u * NB + m + 1)
                            h = m // HALF
                            act.dma_start(turned_adj[b, g, :, h * HALF:(h + 1) * HALF, :],
                                          piece[i][:]).then_inc(piece_stored[i], 16)
                        if m == 6 and not (first and n < 2):
                            post_scale(*back(body, n, 2))
                        if m == 14 and before:
                            post_squares(*before)
                elif before:
                    post_squares(*before)
                    post_scale(*before)
                act.wait_ge(half_used, 2 * (HEAD + u + 1))
                nc.scalar.copy(agg[n % 2][:], agg_ps[n % len(agg_ps)][:]).then_inc(aggs_ready, 1)

            def tail():
                if MASK:
                    post_scale(LAST, UNITS - 2)
                post_squares(LAST, UNITS - 1)
                post_scale(LAST, UNITS - 1)

            all_units(act, unit, tail)
            for i in range(2):
                act.wait_ge(r_stored[i], BODIES * (UNITS // 2) * 16 + 1)
            if MASK:
                for i in range(4):
                    act.wait_ge(piece_stored[i], BODIES * (UNITS // 2) * 16 + 1)

        @block.vector
        def _(dve):
            dve.sem_inc(z_ready, HEAD)
            def post_z(body, n):
                u, i = body * UNITS + n, n % 2
                b, g = body * 2 + n // G, n % G
                link = Chain(dve, dve_step, u * 2)
                dve.wait_ge(a_ready, u + 1)
                dve.wait_ge(r_ready, HEAD + u - 1)
                if DEEP:
                    y = k["y"][:, b, g * Q:(g + 1) * Q, :]
                    if L == 2:
                        nc.vector.tensor_scalar(y, z_ps[:, :, P:2 * P], 1.0, None, ALU.mult)
                    else:
                        nc.vector.tensor_tensor(y, y, z_ps[:, :, P:2 * P], ALU.add)
                link(nc.vector.tensor_tensor(z[i][:], a_ps[:], spread(k["rdeg"][:, b, g * Q:(g + 1) * Q], P), ALU.mult))
                link(nc.vector.tensor_tensor(z[i][:], z[i][:], z_ps[:, :, 0:P], ALU.add))
                if DEEP:
                    dve.wait_ge(extra_ready, u + 1)
                    nc.vector.tensor_tensor(z[i][:], z[i][:], extra[i][:], ALU.add).then_inc(z_ready, 1)
                else:
                    nc.vector.tensor_tensor(z[i][:], z[i][:], repeat(k["row_b"][:], Q), ALU.add).then_inc(z_ready, 1)

            def post_inv(body, n):
                u = body * UNITS + n
                b, g = body * 2 + n // G, n % G
                dve.wait_ge(root_ready, u + 1)
                nc.vector.tensor_scalar(root[:], root[:], NORM_EPS, None, ALU.max).then_inc(end_step, 1)
                dve.wait_ge(end_step, 2 * u + 1)
                nc.vector.reciprocal(inv[:], root[:]).then_inc(end_step, 1)
                dve.wait_ge(end_step, 2 * u + 2)
                nc.vector.tensor_tensor(inv[:], inv[:], c["mask"][:, b, g * Q:(g + 1) * Q], ALU.mult).then_inc(inv_ready, 1)

            LAG = 2 if MASK else 1
            LAG_INV = 3 if MASK else 1

            def unit(body, n, first):
                    u = body * UNITS + n
                    b, g = body * 2 + n // G, n % G
                    before = None if first and n < LAG else back(body, n, LAG)
                    rooted = None if first and n < LAG_INV else back(body, n, LAG_INV)
                    if MASK:
                        PER = 5 * Q + 2
                        link = Chain(dve, mask_step, u * PER)
                        for q in range(Q):
                            i, m = (n % 2) * Q + q, g * Q + q

                            def own(t):
                                return k["own"][:, t, b, m:m + 1]
                            nc.vector.tensor_scalar(word1[:], c["word_index"][:], own(0), own(1), ALU.is_equal, ALU.mult)
                            link(nc.vector.tensor_scalar(word2[:], c["word_index"][:], own(2), own(3), ALU.is_equal, ALU.mult))
                            link(nc.vector.scalar_tensor_tensor(words[:], word1[:], own(4), word2[:], ALU.add, ALU.add))
                            link(nc.vector.tensor_tensor(words2[:], words[:], k["col_bits"][:, b, m, :], ALU.bitwise_or))
                            link(nc.vector.tensor_tensor(
                                gone[:].rearrange("p (k o w) -> p k o w", o=WORD, w=WB),
                                words2[:].rearrange("p (k w) -> p k w", w=WB).unsqueeze(2).broadcast_to([P, NB, WORD, WB]),
                                c["bits"][:].unsqueeze(1).broadcast_to([P, NB, WORD, WB]), ALU.bitwise_and))
                            dve.wait_ge(nat_full[i], (body * (UNITS // 2) + n // 2 + 1) * 16)
                            link(nc.vector.scalar_tensor_tensor(nat[i][:], gone[:], 0.0, nat[i][:], ALU.is_equal, ALU.mult,
                                                                accum_out=row_sum[:, q:q + 1]))
                            nc.vector.sem_inc(mask_ready, 1)
                            if q == 0 and rooted:
                                post_inv(*rooted)
                            if q == 1 and before:
                                post_z(*before)
                        link(nc.vector.tensor_scalar(row_max[:], row_sum[:], 1.0, None, ALU.max))
                        rdeg = k["rdeg"][:, b, g * Q:(g + 1) * Q]
                        link(nc.vector.reciprocal(rdeg, row_max[:]))
                        nc.vector.tensor_tensor(k["ratio"][:, b, g * Q:(g + 1) * Q], row_sum[:], rdeg, ALU.mult)
                        assert link.n == PER
                    elif before:
                        post_z(*before)
                    if not MASK and before:
                        post_inv(*before)

            def tail():
                if MASK:
                    post_inv(LAST, UNITS - 3)
                for by in reversed(range(LAG)):
                    post_z(LAST, UNITS - 1 - by)
                    post_inv(LAST, UNITS - 1 - by)

            all_units(dve, unit, tail)

        @block.gpsimd
        def _(pool):
            pool.sem_inc(added, HEAD)
            link = Chain(pool, once)
            for s in k["sums"]:
                link(nc.gpsimd.memset(s[:], 0.0))
            with pool.Fori(0, BODIES) as body:
                for n in range(UNITS):
                    u = body * UNITS + n
                    i = n % 2
                    b, g = body * 2 + n // G, n % G
                    link = Chain(pool, pool_step, u * (3 if DEEP else 2))
                    if DEEP:
                        pool.wait_ge(z_ready, HEAD + u - 1)
                        link(nc.gpsimd.tensor_tensor(extra[i][:], spread(k["ratio"][:, b, g * Q:(g + 1) * Q], P),
                                                     repeat(k["row_Wr"][:], Q), ALU.mult))
                        nc.gpsimd.tensor_tensor(extra[i][:], extra[i][:], repeat(k["row_b"][:], Q),
                                                ALU.add).then_inc(extra_ready, 1)
                    pool.wait_ge(r_ready, HEAD + u + 1)
                    link(nc.gpsimd.tensor_tensor(r_sq[:], r[i][:], r[i][:], ALU.mult))
                    nc.gpsimd.tensor_tensor(k["sums"][0][:], k["sums"][0][:], r[i][:], ALU.add)
                    link(nc.gpsimd.tensor_tensor(k["sums"][1][:], k["sums"][1][:], r_sq[:], ALU.add))
                    pool.sem_inc(added, 1)


def finish(nc, c, r_in, k, out):
    with ExitStack() as ctx:
        def sb(name, shape, dt=F32):
            return ctx.enter_context(nc.sbuf_tensor(name + "_fin", shape, dt))

        sem = fresh(nc, ctx, "_fin")

        r = [sb(f"r{i}", [P, Q, P]) for i in range(G)]
        x2 = [sb(f"x2{i}", [P, Q, P]) for i in range(G)]
        r_t = [sb(f"r_t{i}", [P, Q, P]) for i in range(2)]
        rest = [sb(f"rest{i}", [P, Q, P]) for i in range(2)]
        last = [sb(f"last{i}", [P, Q, P]) for i in range(2)]
        mask2 = sb("mask2", [P, B, NB])
        turn_ps = [ctx.enter_context(nc.psum_tensor(f"turn_ps{i}" + "_fin", [P, Q, P], F32)) for i in range(2)]
        y_ps = [ctx.enter_context(nc.psum_tensor(f"y_ps{i}" + "_fin", [P, Q, P], F32)) for i in range(2)]
        loaded = [sem(f"loaded{i}") for i in range(G)]
        stored = [sem(f"stored{i}") for i in range(2)]
        turn_ready = sem("turn_ready")
        rt_ready = sem("rt_ready")
        y_ready = sem("y_ready")
        rest_ready = sem("rest_ready")
        pool_step = sem("pool_step")
        dve_step = sem("dve_step")
        out_ready = sem("out_ready")
        mask_made = sem("mask_made")
        block = ctx.enter_context(nc.Block())
        nodes = out.rearrange("b (g q p) d -> b g p q d", p=P, q=Q)

        @block.sync
        def _(sp):
            with sp.Fori(0, B) as b:
                for g in range(G):
                    sp.wait_ge(out_ready, HEAD + b * G + g - G + 1)
                    sp.dma_start(r[g][:], r_in[b, :, g * Q:(g + 1) * Q, :]).then_inc(loaded[g], 16)
                    sp.dma_start(x2[g][:], k["x2"][b, :, g * Q:(g + 1) * Q, :]).then_inc(loaded[g], 16)

        @block.tensor
        def _(pe):
            def turn(b, g):
                pe.wait_ge(loaded[g], (b + 1) * 32)
                for q in range(Q):
                    ins = nc.tensor.transpose(turn_ps[g % 2][:, q, :], r[g][:, q, :], c["ident"][:])
                ins.then_inc(turn_ready, 1)

            def products(b, g):
                u, i = b * G + g, g % 2
                pe.wait_ge(rt_ready, u + 1)
                pe.wait_ge(out_ready, HEAD + u - 1)
                for q in range(Q):
                    nc.tensor.matmul(y_ps[i][:, q, :], r_t[i][:, q, :], k["wY"][:], start=True, stop=False)
                    ins = nc.tensor.matmul(y_ps[i][:, q, :], c["ones"][0:1, :], k["row_Wl"][0:1, :],
                                           start=False, stop=True)
                ins.then_inc(y_ready, 1)

            turn(0, 0)
            for g in range(1, G):
                turn(0, g)
                products(0, g - 1)
            with pe.Fori(1, B) as b:
                for g in range(G):
                    turn(b, g)
                    products(b - (g == 0), (g - 1) % G)
            products(B - 1, G - 1)

        @block.scalar
        def _(act):
            for i in range(2):
                act.sem_inc(stored[i], 1)

            def move(b, g):
                act.wait_ge(turn_ready, b * G + g + 1)
                nc.scalar.copy(r_t[g % 2][:], turn_ps[g % 2][:]).then_inc(rt_ready, 1)

            def store(b, g):
                act.wait_ge(out_ready, HEAD + b * G + g + 1)
                act.dma_start(nodes[b, g], last[g % 2][:]).then_inc(stored[g % 2], 16)

            move(0, 0)
            for g in range(1, G):
                move(0, g)
                store(0, g - 1)
            with act.Fori(1, B) as b:
                for g in range(G):
                    move(b, g)
                    store(b - (g == 0), (g - 1) % G)
            store(B - 1, G - 1)
            for i in range(2):
                act.wait_ge(stored[i], B * 2 * 16 + 1)

        @block.gpsimd
        def _(pool):
            nc.gpsimd.tensor_tensor(mask2[:], c["mask"][:], c["mask"][:], ALU.mult).then_inc(mask_made, 1)
            with pool.Fori(0, B) as b:
                for g in range(G):
                    u, i = b * G + g, g % 2
                    link = Chain(pool, pool_step, u * 2)
                    pool.wait_ge(out_ready, HEAD + u - 1)
                    link(nc.gpsimd.tensor_tensor(rest[i][:], spread(c["mask"][:, b, g * Q:(g + 1) * Q], P),
                                                 repeat(k["row_bl"][:], Q), ALU.mult))
                    pool.wait_ge(loaded[g], (b + 1) * 32)
                    link(nc.gpsimd.tensor_tensor(rest[i][:], rest[i][:], x2[g][:], ALU.add))
                    pool.sem_inc(rest_ready, 1)

        @block.vector
        def _(dve):
            dve.sem_inc(out_ready, HEAD)
            with dve.Fori(0, B) as b:
                for g in range(G):
                    u, i = b * G + g, g % 2
                    link = Chain(dve, dve_step, u * 2)
                    dve.wait_ge(rest_ready, u + 1)
                    dve.wait_ge(y_ready, u + 1)
                    dve.wait_ge(mask_made, 1)
                    dve.wait_ge(stored[i], (b * 2 + g // 2) * 16 + 1)
                    link(nc.vector.tensor_tensor(last[i][:], y_ps[i][:], k["y"][:, b, g * Q:(g + 1) * Q, :], ALU.add))
                    link(nc.vector.tensor_tensor(last[i][:], last[i][:], spread(mask2[:, b, g * Q:(g + 1) * Q], P),
                                                 ALU.mult))
                    nc.vector.tensor_tensor(last[i][:], last[i][:], rest[i][:], ALU.add).then_inc(out_ready, 1)


def build(nc, a, out):
    h = [nc.dram_tensor(f"r{i}", (B, P, NB, P), F32, kind="Internal").ap() for i in range(4)]
    x2 = nc.dram_tensor("x2_scratch", (B, P, NB, P), F32, kind="Internal").ap()
    turned = nc.dram_tensor("turned_adj", (B, G, P, NB, Q * P), F32, kind="Internal").ap()
    with ExitStack() as ctx:
        def sb(name, shape, dt=F32):
            return ctx.enter_context(nc.sbuf_tensor(name, shape, dt))

        c = constants(nc, ctx, a["nodemask"])
        k = {name: sb(name, [P, B, NB]) for name in ("deg", "rdeg", "ratio")}
        k["sums"] = [sb(f"sums{i}", [P, Q, P]) for i in range(2)]
        k["wA"], k["wZ"] = sb("wA", [P, P]), sb("wZ", [P, 2 * P])
        for name in ("row_Wr", "row_Wl", "row_b", "row_bl"):
            k[name] = sb(name, [P, P])
        k["x"], k["x2"] = a["x"], x2
        k["agg"] = nc.dram_tensor("agg_scratch", (B, G, P, Q * P), F32, kind="Internal").ap()
        rows = {name: k[name][:] for name in ("row_Wr", "row_Wl", "row_b", "row_bl")}

        def sage(i, **more):
            return {"Wr": a[f"L1_gnn_Wr{i}"], "Wx": a[f"L1_gnn_Wx{i}"], "b": a[f"L1_gnn_b{i}"],
                    "to_Wr": k["wA"][:], "to_Wx": k["wZ"][:, 0:P], "to_Wl": k["wZ"][:, P:2 * P], **rows, **more}

        def normed(i):
            return {"g": a[f"L1_gnn_g{i}"], "be": a[f"L1_gnn_be{i}"], "Wl": a["L1_gnn_Wl"][(i - 1) * P:i * P, :]}

        with ExitStack() as early:
            k["col_bits"] = early.enter_context(nc.sbuf_tensor("col_bits", [P, B, NB, WORDS], U16))
            k["own"] = early.enter_context(nc.sbuf_tensor("own", [P, 5, B, NB], F32))
            norm(nc, c, a["x"], h[0])
            dilate(nc, c, a["adj"], h[0], k["agg"], k["col_bits"], k["deg"], k["own"])
            weights(nc, c, "_w0", {"Wx": a["L0_gnn_W"][:, 0:P], "Wr": a["L0_gnn_W"][:, P:2 * P], "b": a["L0_gnn_b"],
                            "turn": True, "to_Wr": k["wA"][:], "to_Wx": k["wZ"][:, 0:P], **rows}, None)
            first_layer(nc, c, h[0], h[1], k)
            weights(nc, c, "_w1", sage(1), None)
            layer(nc, c, 1, a["adj"], turned, h[1], h[2], k)
        k["y"] = sb("y", [P, B, NB, P])
        weights(nc, c, "_w2", sage(2, **normed(1)), k["sums"])
        layer(nc, c, 2, a["adj"], turned, h[2], h[3], k)
        weights(nc, c, "_w3", sage(3, **normed(2)), k["sums"])
        layer(nc, c, 3, a["adj"], turned, h[3], h[0], k)
        k["wY"] = k["wA"]
        weights(nc, c, "_w4", {**normed(3), "bl": a["L1_gnn_bl"], "to_Wl": k["wY"][:], **rows}, k["sums"])
        finish(nc, c, h[0], k, out)


NAMES = (["x", "adj", "nodemask", "L0_gnn_W", "L0_gnn_b"]
         + [f"L1_gnn_{t}{i}" for i in (1, 2, 3) for t in ("Wr", "Wx", "b", "g", "be")] + ["L1_gnn_Wl", "L1_gnn_bl"])


def kernel(**inputs):
    import numpy as _np
    import concourse.bacc as _bacc
    from concourse import mybir as _mybir
    from concourse.bass_utils import run_bass_kernel_spmd as _run

    nc = _bacc.Bacc("TRN2", target_bir_lowering=False, num_devices=1)
    arrays, args = {}, {}
    for name in NAMES:
        arr = _np.ascontiguousarray(inputs[name])
        arrays[f"in_{name}"] = arr
        args[name] = nc.dram_tensor(f"in_{name}", arr.shape, _mybir.dt.from_np(arr.dtype), kind="ExternalInput").ap()
    out = nc.dram_tensor("out", (B, N, P), F32, kind="ExternalOutput").ap()
    build(nc, args, out)
    r = _run(nc, [arrays], core_ids=[0])
    return r.results[0]["out"]
```
